# Optimizing a Trainium2 kernel written in Bass

```python
import numpy as np
import jax
import jax.numpy as jnp

def _softmax(x, axis=-1):
    return jax.nn.softmax(x, axis=axis)

def _gelu(x):
    return jax.nn.gelu(x, approximate=True)

def _silu(x):
    return jax.nn.silu(x)

def _sigmoid(x):
    return jax.nn.sigmoid(x)

def _layernorm(x, axis=-1, eps=1e-05):
    m = jnp.mean(x, axis=axis, keepdims=True)
    v = jnp.var(x, axis=axis, keepdims=True)
    return (x - m) / jnp.sqrt(v + eps)

def _scatter_add(tgt, idx, src, axis=0):
    return tgt.at[idx].add(src)

def _segment_sum(src, seg, n):
    return jax.ops.segment_sum(src, seg, n)
kernel_name = 'mk_adaln_attn_ffn_d4_seqx_r8_b00645'

def setup_inputs(seed: int=0):
    np.random.seed(seed)
    _w = jnp.asarray

    def _rec_inputs():
        import jax
        import jax.numpy as jnp
        _rk = jax.random.key(seed)
        x = -0.000125 + 0.9999 * jax.random.normal(jax.random.fold_in(_rk, 1), (4, 256, 256), jnp.float32)
        _lenS = 256 - jax.random.randint(jax.random.fold_in(_rk, 7), (4,), 0, max(1, 256 // 4) + 1, jnp.int32)
        _lenS2 = 256 - jax.random.randint(jax.random.fold_in(_rk, 8), (4,), 0, max(1, 256 // 4) + 1, jnp.int32)
        fside_BxSxS_0 = -1.52775e-05 + 0.999936 * jax.random.normal(jax.random.fold_in(_rk, 11), (4, 256, 256), jnp.float32)
        cond_512 = -5.03954e-05 + 1.00559 * jax.random.normal(jax.random.fold_in(_rk, 12), (4, 64), jnp.float32)
        return (x, fside_BxSxS_0, cond_512)
    x, fside_BxSxS_0, cond_512 = _rec_inputs()

    def _L0_cond_setup():
        import jax, jax.numpy as jnp
        from jax import lax
        import numpy as np
        B, T, C, TD = (8, 256, 256, 64)

        def _bi_wkv(r, k, v, w, u, time_emb):
            tf = jax.nn.sigmoid(jnp.sum(time_emb, axis=-1))[:, None, None]
            decay = jnp.exp(-jnp.exp(w.astype(jnp.float32)))[None, :] * (0.5 + 0.5 * tf[:, :, 0])
            kf = k.astype(jnp.float32)
            vf = v.astype(jnp.float32)
            ek = jnp.exp(jnp.minimum(kf, 30.0))
            ekv = ek * vf

            def step(carry, x):
                a, b = carry
                ekv_t, ek_t = x
                a = a * decay + ekv_t
                b = b * decay + ek_t
                return ((a, b), (a, b))
            ekv_t = jnp.swapaxes(ekv, 0, 1)
            ek_t = jnp.swapaxes(ek, 0, 1)
            init = (jnp.zeros_like(decay), jnp.zeros_like(decay))
            _, (nf, df) = lax.scan(step, init, (ekv_t, ek_t))
            _, (nb, db) = lax.scan(step, init, (ekv_t, ek_t), reverse=True)
            nf = jnp.swapaxes(nf, 0, 1)
            df = jnp.swapaxes(df, 0, 1)
            nb = jnp.swapaxes(nb, 0, 1)
            db = jnp.swapaxes(db, 0, 1)
            euk = jnp.exp(jnp.minimum(u.astype(jnp.float32)[None, None, :] + kf, 30.0))
            num = nf + nb - ekv + euk * vf
            den = df + db - ek + euk
            base = jax.nn.sigmoid(r.astype(jnp.float32)) * (num / jnp.maximum(den, 1e-08))
            out = base * (0.8 + 0.2 * tf)
            return out.astype(r.dtype)
        key = jax.random.key(seed)
        ks = jax.random.split(key, 6)
        return {'r': jax.random.normal(ks[0], (B, T, C), dtype=jnp.float32), 'k': jax.random.normal(ks[1], (B, T, C), dtype=jnp.float32), 'v': jax.random.normal(ks[2], (B, T, C), dtype=jnp.float32), 'w': jax.random.normal(ks[3], (C,), dtype=jnp.float32), 'u': jax.random.normal(ks[4], (C,), dtype=jnp.float32), 'time_emb': jax.random.normal(ks[5], (B, TD), dtype=jnp.float32)}
    _L0_cond_all = _L0_cond_setup()
    _L0_cond_in = {k: v for k, v in _L0_cond_all.items() if k in ('w', 'u')}
    del _L0_cond_all

    def _L0_attn_setup():
        import jax, jax.numpy as jnp
        import numpy as np
        HIDDEN = 256
        NUM_HEADS = 32
        HEAD_DIM = 64
        NUM_KV = 8
        GROUP = NUM_HEADS // NUM_KV
        SCALE = HEAD_DIM ** (-0.5)
        ROPE_BASE = 10000.0

        def apply_rope(t):
            S, D = (t.shape[-2], t.shape[-1])
            inv_freq = 1.0 / ROPE_BASE ** (jnp.arange(0, D, 2, dtype=jnp.float32) / D)
            ang = jnp.arange(S, dtype=jnp.float32)[:, None] * inv_freq[None, :]
            cos, sin = (jnp.cos(ang), jnp.sin(ang))
            x1, x2 = (t[..., :D // 2], t[..., D // 2:])
            return jnp.concatenate([x1 * cos - x2 * sin, x2 * cos + x1 * sin], axis=-1)
        key = jax.random.key(seed)
        ks = jax.random.split(key, 10)
        B, S = (2, 256)
        s_in = HIDDEN ** (-0.5)
        s_o = (NUM_HEADS * HEAD_DIM) ** (-0.5)
        return {'x': jax.random.normal(ks[0], (B, S, HIDDEN), jnp.float32), 'Wq': jax.random.normal(ks[1], (NUM_HEADS * HEAD_DIM, HIDDEN), jnp.float32) * s_in, 'bq': jnp.zeros((NUM_HEADS * HEAD_DIM,), jnp.float32), 'Wk': jax.random.normal(ks[2], (NUM_KV * HEAD_DIM, HIDDEN), jnp.float32) * s_in, 'bk': jnp.zeros((NUM_KV * HEAD_DIM,), jnp.float32), 'Wv': jax.random.normal(ks[3], (NUM_KV * HEAD_DIM, HIDDEN), jnp.float32) * s_in, 'bv': jnp.zeros((NUM_KV * HEAD_DIM,), jnp.float32), 'Wo': jax.random.normal(ks[4], (HIDDEN, NUM_HEADS * HEAD_DIM), jnp.float32) * s_o, 'bo': jnp.zeros((HIDDEN,), jnp.float32), 'key_weights': jax.random.normal(ks[5], (NUM_HEADS,), jnp.float32)}
    _L0_attn_all = _L0_attn_setup()
    _L0_attn_in = {k: v for k, v in _L0_attn_all.items() if k in ('Wq', 'bq', 'Wk', 'bk', 'Wv', 'bv', 'Wo', 'bo', 'key_weights')}
    del _L0_attn_all

    def _L0_cond2_setup():
        import jax, jax.numpy as jnp
        from jax import lax
        import numpy as np
        B, T, C, TD = (8, 256, 256, 64)

        def _bi_wkv(r, k, v, w, u, time_emb):
            tf = jax.nn.sigmoid(jnp.sum(time_emb, axis=-1))[:, None, None]
            decay = jnp.exp(-jnp.exp(w.astype(jnp.float32)))[None, :] * (0.5 + 0.5 * tf[:, :, 0])
            kf = k.astype(jnp.float32)
            vf = v.astype(jnp.float32)
            ek = jnp.exp(jnp.minimum(kf, 30.0))
            ekv = ek * vf

            def step(carry, x):
                a, b = carry
                ekv_t, ek_t = x
                a = a * decay + ekv_t
                b = b * decay + ek_t
                return ((a, b), (a, b))
            ekv_t = jnp.swapaxes(ekv, 0, 1)
            ek_t = jnp.swapaxes(ek, 0, 1)
            init = (jnp.zeros_like(decay), jnp.zeros_like(decay))
            _, (nf, df) = lax.scan(step, init, (ekv_t, ek_t))
            _, (nb, db) = lax.scan(step, init, (ekv_t, ek_t), reverse=True)
            nf = jnp.swapaxes(nf, 0, 1)
            df = jnp.swapaxes(df, 0, 1)
            nb = jnp.swapaxes(nb, 0, 1)
            db = jnp.swapaxes(db, 0, 1)
            euk = jnp.exp(jnp.minimum(u.astype(jnp.float32)[None, None, :] + kf, 30.0))
            num = nf + nb - ekv + euk * vf
            den = df + db - ek + euk
            base = jax.nn.sigmoid(r.astype(jnp.float32)) * (num / jnp.maximum(den, 1e-08))
            out = base * (0.8 + 0.2 * tf)
            return out.astype(r.dtype)
        key = jax.random.key(seed)
        ks = jax.random.split(key, 6)
        return {'r': jax.random.normal(ks[0], (B, T, C), dtype=jnp.float32), 'k': jax.random.normal(ks[1], (B, T, C), dtype=jnp.float32), 'v': jax.random.normal(ks[2], (B, T, C), dtype=jnp.float32), 'w': jax.random.normal(ks[3], (C,), dtype=jnp.float32), 'u': jax.random.normal(ks[4], (C,), dtype=jnp.float32), 'time_emb': jax.random.normal(ks[5], (B, TD), dtype=jnp.float32)}
    _L0_cond2_all = _L0_cond2_setup()
    _L0_cond2_in = {k: v for k, v in _L0_cond2_all.items() if k in ('w', 'u')}
    del _L0_cond2_all

    def _L0_ffn_setup():
        import jax, jax.numpy as jnp
        import numpy as np
        B, L, D = (2, 128, 256)
        E, K = (8, 2)
        H, HS = (176, 352)
        key = jax.random.key(seed)
        ks = jax.random.split(key, 9)
        s = 0.02
        return {'x': jax.random.normal(ks[0], (B, L, D), dtype=jnp.float32), 'gate_w': jax.random.normal(ks[1], (E, D), dtype=jnp.float32) * s, 'w_gate': jax.random.normal(ks[2], (E, D, H), dtype=jnp.float32) * s, 'w_up': jax.random.normal(ks[3], (E, D, H), dtype=jnp.float32) * s, 'w_down': jax.random.normal(ks[4], (E, H, D), dtype=jnp.float32) * s, 'shgate_w': jax.random.normal(ks[5], (D,), dtype=jnp.float32) * s, 'shw_gate': jax.random.normal(ks[6], (D, HS), dtype=jnp.float32) * s, 'shw_up': jax.random.normal(ks[7], (D, HS), dtype=jnp.float32) * s, 'shw_down': jax.random.normal(ks[8], (HS, D), dtype=jnp.float32) * s}
    _L0_ffn_all = _L0_ffn_setup()
    _L0_ffn_in = {k: v for k, v in _L0_ffn_all.items() if k in ('gate_w', 'w_gate', 'w_up', 'w_down', 'shgate_w', 'shw_gate', 'shw_up', 'shw_down')}
    del _L0_ffn_all

    def _L1_cond_setup():
        import jax, jax.numpy as jnp
        from jax import lax
        import numpy as np
        B, T, C, TD = (8, 256, 256, 64)

        def _bi_wkv(r, k, v, w, u, time_emb):
            tf = jax.nn.sigmoid(jnp.sum(time_emb, axis=-1))[:, None, None]
            decay = jnp.exp(-jnp.exp(w.astype(jnp.float32)))[None, :] * (0.5 + 0.5 * tf[:, :, 0])
            kf = k.astype(jnp.float32)
            vf = v.astype(jnp.float32)
            ek = jnp.exp(jnp.minimum(kf, 30.0))
            ekv = ek * vf

            def step(carry, x):
                a, b = carry
                ekv_t, ek_t = x
                a = a * decay + ekv_t
                b = b * decay + ek_t
                return ((a, b), (a, b))
            ekv_t = jnp.swapaxes(ekv, 0, 1)
            ek_t = jnp.swapaxes(ek, 0, 1)
            init = (jnp.zeros_like(decay), jnp.zeros_like(decay))
            _, (nf, df) = lax.scan(step, init, (ekv_t, ek_t))
            _, (nb, db) = lax.scan(step, init, (ekv_t, ek_t), reverse=True)
            nf = jnp.swapaxes(nf, 0, 1)
            df = jnp.swapaxes(df, 0, 1)
            nb = jnp.swapaxes(nb, 0, 1)
            db = jnp.swapaxes(db, 0, 1)
            euk = jnp.exp(jnp.minimum(u.astype(jnp.float32)[None, None, :] + kf, 30.0))
            num = nf + nb - ekv + euk * vf
            den = df + db - ek + euk
            base = jax.nn.sigmoid(r.astype(jnp.float32)) * (num / jnp.maximum(den, 1e-08))
            out = base * (0.8 + 0.2 * tf)
            return out.astype(r.dtype)
        key = jax.random.key(seed)
        ks = jax.random.split(key, 6)
        return {'r': jax.random.normal(ks[0], (B, T, C), dtype=jnp.float32), 'k': jax.random.normal(ks[1], (B, T, C), dtype=jnp.float32), 'v': jax.random.normal(ks[2], (B, T, C), dtype=jnp.float32), 'w': jax.random.normal(ks[3], (C,), dtype=jnp.float32), 'u': jax.random.normal(ks[4], (C,), dtype=jnp.float32), 'time_emb': jax.random.normal(ks[5], (B, TD), dtype=jnp.float32)}
    _L1_cond_all = _L1_cond_setup()
    _L1_cond_in = {k: v for k, v in _L1_cond_all.items() if k in ('w', 'u')}
    del _L1_cond_all

    def _L1_attn_setup():
        import jax, jax.numpy as jnp
        import numpy as np
        C_RGLRU = 8.0

        def _rg_lru(x, wa, ba, wx, bx, lam):
            r = jax.nn.sigmoid(jnp.einsum('bld,ed->ble', x, wa) + ba)
            i = jax.nn.sigmoid(jnp.einsum('bld,ed->ble', x, wx) + bx)
            log_a = -C_RGLRU * r * jax.nn.softplus(lam)
            a = jnp.exp(log_a)
            mult = jnp.sqrt(jnp.maximum(1.0 - jnp.exp(2.0 * log_a), 0.0))
            b = mult * (i * x)

            def combine(c1, c2):
                a1, b1 = c1
                a2, b2 = c2
                return (a1 * a2, a2 * b1 + b2)
            _, h = jax.lax.associative_scan(combine, (a, b), axis=1)
            return h
        key = jax.random.key(seed)
        ks = jax.random.split(key, 12)
        B, L, D, R = (4, 256, 256, 320)
        s_d = 1.0 / np.sqrt(D)
        s_r = 1.0 / np.sqrt(R)
        s_c = 1.0 / np.sqrt(R * 4)
        return {'x': jax.random.normal(ks[0], (B, L, D), jnp.float32), 'w1': jax.random.normal(ks[1], (R, D), jnp.float32) * s_d, 'b1': jnp.zeros((R,), jnp.float32), 'conv_w': jax.random.normal(ks[2], (R, R, 4), jnp.float32) * s_c, 'conv_b': jnp.zeros((R,), jnp.float32), 'wa': jax.random.normal(ks[3], (R, R), jnp.float32) * s_r, 'ba': jnp.zeros((R,), jnp.float32), 'wx': jax.random.normal(ks[4], (R, R), jnp.float32) * s_r, 'bx': jnp.zeros((R,), jnp.float32), 'lam': jax.random.uniform(ks[5], (R,), jnp.float32, 0.5, 2.0), 'w2': jax.random.normal(ks[6], (D, R), jnp.float32) * s_r, 'b2': jnp.zeros((D,), jnp.float32)}
    _L1_attn_all = _L1_attn_setup()
    _L1_attn_in = {k: v for k, v in _L1_attn_all.items() if k in ('w1', 'b1', 'conv_w', 'conv_b', 'wa', 'ba', 'wx', 'bx', 'lam', 'w2', 'b2')}
    del _L1_attn_all

    def _L1_cond2_setup():
        import jax, jax.numpy as jnp
        from jax import lax
        import numpy as np
        B, T, C, TD = (8, 256, 256, 64)

        def _bi_wkv(r, k, v, w, u, time_emb):
            tf = jax.nn.sigmoid(jnp.sum(time_emb, axis=-1))[:, None, None]
            decay = jnp.exp(-jnp.exp(w.astype(jnp.float32)))[None, :] * (0.5 + 0.5 * tf[:, :, 0])
            kf = k.astype(jnp.float32)
            vf = v.astype(jnp.float32)
            ek = jnp.exp(jnp.minimum(kf, 30.0))
            ekv = ek * vf

            def step(carry, x):
                a, b = carry
                ekv_t, ek_t = x
                a = a * decay + ekv_t
                b = b * decay + ek_t
                return ((a, b), (a, b))
            ekv_t = jnp.swapaxes(ekv, 0, 1)
            ek_t = jnp.swapaxes(ek, 0, 1)
            init = (jnp.zeros_like(decay), jnp.zeros_like(decay))
            _, (nf, df) = lax.scan(step, init, (ekv_t, ek_t))
            _, (nb, db) = lax.scan(step, init, (ekv_t, ek_t), reverse=True)
            nf = jnp.swapaxes(nf, 0, 1)
            df = jnp.swapaxes(df, 0, 1)
            nb = jnp.swapaxes(nb, 0, 1)
            db = jnp.swapaxes(db, 0, 1)
            euk = jnp.exp(jnp.minimum(u.astype(jnp.float32)[None, None, :] + kf, 30.0))
            num = nf + nb - ekv + euk * vf
            den = df + db - ek + euk
            base = jax.nn.sigmoid(r.astype(jnp.float32)) * (num / jnp.maximum(den, 1e-08))
            out = base * (0.8 + 0.2 * tf)
            return out.astype(r.dtype)
        key = jax.random.key(seed)
        ks = jax.random.split(key, 6)
        return {'r': jax.random.normal(ks[0], (B, T, C), dtype=jnp.float32), 'k': jax.random.normal(ks[1], (B, T, C), dtype=jnp.float32), 'v': jax.random.normal(ks[2], (B, T, C), dtype=jnp.float32), 'w': jax.random.normal(ks[3], (C,), dtype=jnp.float32), 'u': jax.random.normal(ks[4], (C,), dtype=jnp.float32), 'time_emb': jax.random.normal(ks[5], (B, TD), dtype=jnp.float32)}
    _L1_cond2_all = _L1_cond2_setup()
    _L1_cond2_in = {k: v for k, v in _L1_cond2_all.items() if k in ('w', 'u')}
    del _L1_cond2_all

    def _L1_ffn_setup():
        import jax, jax.numpy as jnp
        import numpy as np
        D_MODEL = 256
        HIDDEN = 4 * D_MODEL
        N_EXPERTS = 8
        TOP_K = 2
        CAP_FACTOR = 1.0
        key = jax.random.key(seed)
        ks = jax.random.split(key, 6)
        x = jax.random.normal(ks[0], (4, 256, D_MODEL), dtype=jnp.float32)
        wg = jax.random.normal(ks[1], (D_MODEL, N_EXPERTS), dtype=jnp.float32) * (1.0 / np.sqrt(D_MODEL))
        fc1_w = jax.random.normal(ks[2], (N_EXPERTS, D_MODEL, HIDDEN), dtype=jnp.float32) * 0.02
        fc1_b = jnp.zeros((N_EXPERTS, HIDDEN), dtype=jnp.float32)
        fc2_w = jax.random.normal(ks[3], (N_EXPERTS, HIDDEN, D_MODEL), dtype=jnp.float32) * 0.02
        fc2_b = jnp.zeros((N_EXPERTS, D_MODEL), dtype=jnp.float32)
        return {'x': x, 'wg': wg, 'fc1_w': fc1_w, 'fc1_b': fc1_b, 'fc2_w': fc2_w, 'fc2_b': fc2_b}
    _L1_ffn_all = _L1_ffn_setup()
    _L1_ffn_in = {k: v for k, v in _L1_ffn_all.items() if k in ('wg', 'fc1_w', 'fc1_b', 'fc2_w', 'fc2_b')}
    del _L1_ffn_all

    def _L2_cond_setup():
        import jax, jax.numpy as jnp
        from jax import lax
        import numpy as np
        B, T, C, TD = (8, 256, 256, 64)

        def _bi_wkv(r, k, v, w, u, time_emb):
            tf = jax.nn.sigmoid(jnp.sum(time_emb, axis=-1))[:, None, None]
            decay = jnp.exp(-jnp.exp(w.astype(jnp.float32)))[None, :] * (0.5 + 0.5 * tf[:, :, 0])
            kf = k.astype(jnp.float32)
            vf = v.astype(jnp.float32)
            ek = jnp.exp(jnp.minimum(kf, 30.0))
            ekv = ek * vf

            def step(carry, x):
                a, b = carry
                ekv_t, ek_t = x
                a = a * decay + ekv_t
                b = b * decay + ek_t
                return ((a, b), (a, b))
            ekv_t = jnp.swapaxes(ekv, 0, 1)
            ek_t = jnp.swapaxes(ek, 0, 1)
            init = (jnp.zeros_like(decay), jnp.zeros_like(decay))
            _, (nf, df) = lax.scan(step, init, (ekv_t, ek_t))
            _, (nb, db) = lax.scan(step, init, (ekv_t, ek_t), reverse=True)
            nf = jnp.swapaxes(nf, 0, 1)
            df = jnp.swapaxes(df, 0, 1)
            nb = jnp.swapaxes(nb, 0, 1)
            db = jnp.swapaxes(db, 0, 1)
            euk = jnp.exp(jnp.minimum(u.astype(jnp.float32)[None, None, :] + kf, 30.0))
            num = nf + nb - ekv + euk * vf
            den = df + db - ek + euk
            base = jax.nn.sigmoid(r.astype(jnp.float32)) * (num / jnp.maximum(den, 1e-08))
            out = base * (0.8 + 0.2 * tf)
            return out.astype(r.dtype)
        key = jax.random.key(seed)
        ks = jax.random.split(key, 6)
        return {'r': jax.random.normal(ks[0], (B, T, C), dtype=jnp.float32), 'k': jax.random.normal(ks[1], (B, T, C), dtype=jnp.float32), 'v': jax.random.normal(ks[2], (B, T, C), dtype=jnp.float32), 'w': jax.random.normal(ks[3], (C,), dtype=jnp.float32), 'u': jax.random.normal(ks[4], (C,), dtype=jnp.float32), 'time_emb': jax.random.normal(ks[5], (B, TD), dtype=jnp.float32)}
    _L2_cond_all = _L2_cond_setup()
    _L2_cond_in = {k: v for k, v in _L2_cond_all.items() if k in ('w', 'u')}
    del _L2_cond_all

    def _L2_attn_setup():
        import jax, jax.numpy as jnp
        import numpy as np
        B, S, QD = (2, 512, 256)
        H, D = (32, 64)
        INNER = H * D
        key = jax.random.key(seed)
        ks = jax.random.split(key, 6)
        scale = 1.0 / np.sqrt(QD)
        return {'hidden_states': jax.random.normal(ks[0], (B, S, QD), dtype=jnp.float32), 'Wq': jax.random.normal(ks[1], (QD, INNER), dtype=jnp.float32) * scale, 'Wk': jax.random.normal(ks[2], (QD, INNER), dtype=jnp.float32) * scale, 'Wv': jax.random.normal(ks[3], (QD, INNER), dtype=jnp.float32) * scale, 'Wo': jax.random.normal(ks[4], (INNER, QD), dtype=jnp.float32) * (1.0 / np.sqrt(INNER)), 'bo': jax.random.normal(ks[5], (QD,), dtype=jnp.float32) * 0.01}
    _L2_attn_all = _L2_attn_setup()
    _L2_attn_in = {k: v for k, v in _L2_attn_all.items() if k in ('Wq', 'Wk', 'Wv', 'Wo', 'bo')}
    del _L2_attn_all

    def _L2_cond2_setup():
        import jax, jax.numpy as jnp
        from jax import lax
        import numpy as np
        B, T, C, TD = (8, 256, 256, 64)

        def _bi_wkv(r, k, v, w, u, time_emb):
            tf = jax.nn.sigmoid(jnp.sum(time_emb, axis=-1))[:, None, None]
            decay = jnp.exp(-jnp.exp(w.astype(jnp.float32)))[None, :] * (0.5 + 0.5 * tf[:, :, 0])
            kf = k.astype(jnp.float32)
            vf = v.astype(jnp.float32)
            ek = jnp.exp(jnp.minimum(kf, 30.0))
            ekv = ek * vf

            def step(carry, x):
                a, b = carry
                ekv_t, ek_t = x
                a = a * decay + ekv_t
                b = b * decay + ek_t
                return ((a, b), (a, b))
            ekv_t = jnp.swapaxes(ekv, 0, 1)
            ek_t = jnp.swapaxes(ek, 0, 1)
            init = (jnp.zeros_like(decay), jnp.zeros_like(decay))
            _, (nf, df) = lax.scan(step, init, (ekv_t, ek_t))
            _, (nb, db) = lax.scan(step, init, (ekv_t, ek_t), reverse=True)
            nf = jnp.swapaxes(nf, 0, 1)
            df = jnp.swapaxes(df, 0, 1)
            nb = jnp.swapaxes(nb, 0, 1)
            db = jnp.swapaxes(db, 0, 1)
            euk = jnp.exp(jnp.minimum(u.astype(jnp.float32)[None, None, :] + kf, 30.0))
            num = nf + nb - ekv + euk * vf
            den = df + db - ek + euk
            base = jax.nn.sigmoid(r.astype(jnp.float32)) * (num / jnp.maximum(den, 1e-08))
            out = base * (0.8 + 0.2 * tf)
            return out.astype(r.dtype)
        key = jax.random.key(seed)
        ks = jax.random.split(key, 6)
        return {'r': jax.random.normal(ks[0], (B, T, C), dtype=jnp.float32), 'k': jax.random.normal(ks[1], (B, T, C), dtype=jnp.float32), 'v': jax.random.normal(ks[2], (B, T, C), dtype=jnp.float32), 'w': jax.random.normal(ks[3], (C,), dtype=jnp.float32), 'u': jax.random.normal(ks[4], (C,), dtype=jnp.float32), 'time_emb': jax.random.normal(ks[5], (B, TD), dtype=jnp.float32)}
    _L2_cond2_all = _L2_cond2_setup()
    _L2_cond2_in = {k: v for k, v in _L2_cond2_all.items() if k in ('w', 'u')}
    del _L2_cond2_all

    def _L2_ffn_setup():
        import jax, jax.numpy as jnp
        import numpy as np
        key = jax.random.key(seed)
        k1, k2, k3, k4 = jax.random.split(key, 4)
        B, S, D_IN, D_OUT = (4, 512, 256, 256)
        x = jax.random.normal(k1, (B, S, D_IN), dtype=jnp.float32)
        weight = jax.random.normal(k2, (D_OUT, D_IN), dtype=jnp.float32) * 0.02
        scale_weight = jax.random.uniform(k3, (D_OUT,), dtype=jnp.float32, minval=0.5, maxval=1.5)
        bias = jax.random.normal(k4, (D_OUT,), dtype=jnp.float32) * 0.02
        return {'x': x, 'weight': weight, 'scale_weight': scale_weight, 'bias': bias}
    _L2_ffn_all = _L2_ffn_setup()
    _L2_ffn_in = {k: v for k, v in _L2_ffn_all.items() if k in ('weight', 'scale_weight', 'bias')}
    del _L2_ffn_all

    def _L3_cond_setup():
        import jax, jax.numpy as jnp
        from jax import lax
        import numpy as np
        B, T, C, TD = (8, 256, 256, 64)

        def _bi_wkv(r, k, v, w, u, time_emb):
            tf = jax.nn.sigmoid(jnp.sum(time_emb, axis=-1))[:, None, None]
            decay = jnp.exp(-jnp.exp(w.astype(jnp.float32)))[None, :] * (0.5 + 0.5 * tf[:, :, 0])
            kf = k.astype(jnp.float32)
            vf = v.astype(jnp.float32)
            ek = jnp.exp(jnp.minimum(kf, 30.0))
            ekv = ek * vf

            def step(carry, x):
                a, b = carry
                ekv_t, ek_t = x
                a = a * decay + ekv_t
                b = b * decay + ek_t
                return ((a, b), (a, b))
            ekv_t = jnp.swapaxes(ekv, 0, 1)
            ek_t = jnp.swapaxes(ek, 0, 1)
            init = (jnp.zeros_like(decay), jnp.zeros_like(decay))
            _, (nf, df) = lax.scan(step, init, (ekv_t, ek_t))
            _, (nb, db) = lax.scan(step, init, (ekv_t, ek_t), reverse=True)
            nf = jnp.swapaxes(nf, 0, 1)
            df = jnp.swapaxes(df, 0, 1)
            nb = jnp.swapaxes(nb, 0, 1)
            db = jnp.swapaxes(db, 0, 1)
            euk = jnp.exp(jnp.minimum(u.astype(jnp.float32)[None, None, :] + kf, 30.0))
            num = nf + nb - ekv + euk * vf
            den = df + db - ek + euk
            base = jax.nn.sigmoid(r.astype(jnp.float32)) * (num / jnp.maximum(den, 1e-08))
            out = base * (0.8 + 0.2 * tf)
            return out.astype(r.dtype)
        key = jax.random.key(seed)
        ks = jax.random.split(key, 6)
        return {'r': jax.random.normal(ks[0], (B, T, C), dtype=jnp.float32), 'k': jax.random.normal(ks[1], (B, T, C), dtype=jnp.float32), 'v': jax.random.normal(ks[2], (B, T, C), dtype=jnp.float32), 'w': jax.random.normal(ks[3], (C,), dtype=jnp.float32), 'u': jax.random.normal(ks[4], (C,), dtype=jnp.float32), 'time_emb': jax.random.normal(ks[5], (B, TD), dtype=jnp.float32)}
    _L3_cond_all = _L3_cond_setup()
    _L3_cond_in = {k: v for k, v in _L3_cond_all.items() if k in ('w', 'u')}
    del _L3_cond_all

    def _L3_attn_setup():
        import jax, jax.numpy as jnp
        import numpy as np
        B, T, C = (8, 128, 256)
        NEG_BIG = -1e+38

        def rwkv_linear_attention(time_decay, time_first, k, v):
            w = -jnp.exp(time_decay)
            u = time_first
            num0 = jnp.zeros(k.shape[::2], dtype=jnp.float32)
            den0 = jnp.zeros_like(num0)
            max0 = jnp.full_like(num0, NEG_BIG)

            def step(carry, kv_t):
                num, den, mx = carry
                kt, vt = kv_t
                mo = jnp.maximum(mx, kt + u)
                e1 = jnp.exp(mx - mo)
                e2 = jnp.exp(kt + u - mo)
                out = (e1 * num + e2 * vt) / (e1 * den + e2)
                ms = jnp.maximum(mx + w, kt)
                e1s = jnp.exp(mx + w - ms)
                e2s = jnp.exp(kt - ms)
                return ((e1s * num + e2s * vt, e1s * den + e2s, ms), out)
            kT = jnp.swapaxes(k, 0, 1).astype(jnp.float32)
            vT = jnp.swapaxes(v, 0, 1).astype(jnp.float32)
            _, outT = jax.lax.scan(step, (num0, den0, max0), (kT, vT))
            return jnp.swapaxes(outT, 0, 1).astype(k.dtype)
        key = jax.random.key(seed)
        ks = jax.random.split(key, 10)
        s = 0.02
        return {'x': jax.random.normal(ks[0], (B, T, C), dtype=jnp.float32), 'time_decay': jax.random.normal(ks[1], (C,), dtype=jnp.float32) * 0.5, 'time_first': jax.random.normal(ks[2], (C,), dtype=jnp.float32) * 0.5, 'time_mix_k': jax.random.uniform(ks[3], (1, 1, C), dtype=jnp.float32), 'time_mix_v': jax.random.uniform(ks[4], (1, 1, C), dtype=jnp.float32), 'time_mix_r': jax.random.uniform(ks[5], (1, 1, C), dtype=jnp.float32), 'Wk': jax.random.normal(ks[6], (C, C), dtype=jnp.float32) * s, 'Wv': jax.random.normal(ks[7], (C, C), dtype=jnp.float32) * s, 'Wr': jax.random.normal(ks[8], (C, C), dtype=jnp.float32) * s, 'Wo': jax.random.normal(ks[9], (C, C), dtype=jnp.float32) * s}
    _L3_attn_all = _L3_attn_setup()
    _L3_attn_in = {k: v for k, v in _L3_attn_all.items() if k in ('time_decay', 'time_first', 'time_mix_k', 'time_mix_v', 'time_mix_r', 'Wk', 'Wv', 'Wr', 'Wo')}
    del _L3_attn_all

    def _L3_cond2_setup():
        import jax, jax.numpy as jnp
        from jax import lax
        import numpy as np
        B, T, C, TD = (8, 256, 256, 64)

        def _bi_wkv(r, k, v, w, u, time_emb):
            tf = jax.nn.sigmoid(jnp.sum(time_emb, axis=-1))[:, None, None]
            decay = jnp.exp(-jnp.exp(w.astype(jnp.float32)))[None, :] * (0.5 + 0.5 * tf[:, :, 0])
            kf = k.astype(jnp.float32)
            vf = v.astype(jnp.float32)
            ek = jnp.exp(jnp.minimum(kf, 30.0))
            ekv = ek * vf

            def step(carry, x):
                a, b = carry
                ekv_t, ek_t = x
                a = a * decay + ekv_t
                b = b * decay + ek_t
                return ((a, b), (a, b))
            ekv_t = jnp.swapaxes(ekv, 0, 1)
            ek_t = jnp.swapaxes(ek, 0, 1)
            init = (jnp.zeros_like(decay), jnp.zeros_like(decay))
            _, (nf, df) = lax.scan(step, init, (ekv_t, ek_t))
            _, (nb, db) = lax.scan(step, init, (ekv_t, ek_t), reverse=True)
            nf = jnp.swapaxes(nf, 0, 1)
            df = jnp.swapaxes(df, 0, 1)
            nb = jnp.swapaxes(nb, 0, 1)
            db = jnp.swapaxes(db, 0, 1)
            euk = jnp.exp(jnp.minimum(u.astype(jnp.float32)[None, None, :] + kf, 30.0))
            num = nf + nb - ekv + euk * vf
            den = df + db - ek + euk
            base = jax.nn.sigmoid(r.astype(jnp.float32)) * (num / jnp.maximum(den, 1e-08))
            out = base * (0.8 + 0.2 * tf)
            return out.astype(r.dtype)
        key = jax.random.key(seed)
        ks = jax.random.split(key, 6)
        return {'r': jax.random.normal(ks[0], (B, T, C), dtype=jnp.float32), 'k': jax.random.normal(ks[1], (B, T, C), dtype=jnp.float32), 'v': jax.random.normal(ks[2], (B, T, C), dtype=jnp.float32), 'w': jax.random.normal(ks[3], (C,), dtype=jnp.float32), 'u': jax.random.normal(ks[4], (C,), dtype=jnp.float32), 'time_emb': jax.random.normal(ks[5], (B, TD), dtype=jnp.float32)}
    _L3_cond2_all = _L3_cond2_setup()
    _L3_cond2_in = {k: v for k, v in _L3_cond2_all.items() if k in ('w', 'u')}
    del _L3_cond2_all

    def _L3_ffn_setup():
        import jax, jax.numpy as jnp
        import numpy as np
        B, S, H = (2, 128, 256)
        E, K = (8, 2)
        I = 176
        IS = 704
        WSCALE = 0.02
        key = jax.random.key(seed)
        ks = jax.random.split(key, 9)
        f32 = jnp.float32
        return {'hidden_states': jax.random.normal(ks[0], (B, S, H), dtype=f32), 'gate_w': jax.random.normal(ks[1], (E, H), dtype=f32) * WSCALE, 'w_gate': jax.random.normal(ks[2], (E, H, I), dtype=f32) * WSCALE, 'w_up': jax.random.normal(ks[3], (E, H, I), dtype=f32) * WSCALE, 'w_down': jax.random.normal(ks[4], (E, I, H), dtype=f32) * WSCALE, 'sw_gate': jax.random.normal(ks[5], (H, IS), dtype=f32) * WSCALE, 'sw_up': jax.random.normal(ks[6], (H, IS), dtype=f32) * WSCALE, 'sw_down': jax.random.normal(ks[7], (IS, H), dtype=f32) * WSCALE, 'shared_gate_w': jax.random.normal(ks[8], (H, 1), dtype=f32) * WSCALE}
    _L3_ffn_all = _L3_ffn_setup()
    _L3_ffn_in = {k: v for k, v in _L3_ffn_all.items() if k in ('gate_w', 'w_gate', 'w_up', 'w_down', 'sw_gate', 'sw_up', 'sw_down', 'shared_gate_w')}
    del _L3_ffn_all
    return {'x': x, 'fside_BxSxS_0': fside_BxSxS_0, 'cond_512': cond_512, 'L0_cond_w': _L0_cond_in['w'], 'L0_cond_u': _L0_cond_in['u'], 'L0_attn_Wq': _L0_attn_in['Wq'], 'L0_attn_bq': _L0_attn_in['bq'], 'L0_attn_Wk': _L0_attn_in['Wk'], 'L0_attn_bk': _L0_attn_in['bk'], 'L0_attn_Wv': _L0_attn_in['Wv'], 'L0_attn_bv': _L0_attn_in['bv'], 'L0_attn_Wo': _L0_attn_in['Wo'], 'L0_attn_bo': _L0_attn_in['bo'], 'L0_attn_key_weights': _L0_attn_in['key_weights'], 'L0_cond2_w': _L0_cond2_in['w'], 'L0_cond2_u': _L0_cond2_in['u'], 'L0_ffn_gate_w': _L0_ffn_in['gate_w'], 'L0_ffn_w_gate': _L0_ffn_in['w_gate'], 'L0_ffn_w_up': _L0_ffn_in['w_up'], 'L0_ffn_w_down': _L0_ffn_in['w_down'], 'L0_ffn_shgate_w': _L0_ffn_in['shgate_w'], 'L0_ffn_shw_gate': _L0_ffn_in['shw_gate'], 'L0_ffn_shw_up': _L0_ffn_in['shw_up'], 'L0_ffn_shw_down': _L0_ffn_in['shw_down'], 'L1_cond_w': _L1_cond_in['w'], 'L1_cond_u': _L1_cond_in['u'], 'L1_attn_w1': _L1_attn_in['w1'], 'L1_attn_b1': _L1_attn_in['b1'], 'L1_attn_conv_w': _L1_attn_in['conv_w'], 'L1_attn_conv_b': _L1_attn_in['conv_b'], 'L1_attn_wa': _L1_attn_in['wa'], 'L1_attn_ba': _L1_attn_in['ba'], 'L1_attn_wx': _L1_attn_in['wx'], 'L1_attn_bx': _L1_attn_in['bx'], 'L1_attn_lam': _L1_attn_in['lam'], 'L1_attn_w2': _L1_attn_in['w2'], 'L1_attn_b2': _L1_attn_in['b2'], 'L1_cond2_w': _L1_cond2_in['w'], 'L1_cond2_u': _L1_cond2_in['u'], 'L1_ffn_wg': _L1_ffn_in['wg'], 'L1_ffn_fc1_w': _L1_ffn_in['fc1_w'], 'L1_ffn_fc1_b': _L1_ffn_in['fc1_b'], 'L1_ffn_fc2_w': _L1_ffn_in['fc2_w'], 'L1_ffn_fc2_b': _L1_ffn_in['fc2_b'], 'L2_cond_w': _L2_cond_in['w'], 'L2_cond_u': _L2_cond_in['u'], 'L2_attn_Wq': _L2_attn_in['Wq'], 'L2_attn_Wk': _L2_attn_in['Wk'], 'L2_attn_Wv': _L2_attn_in['Wv'], 'L2_attn_Wo': _L2_attn_in['Wo'], 'L2_attn_bo': _L2_attn_in['bo'], 'L2_cond2_w': _L2_cond2_in['w'], 'L2_cond2_u': _L2_cond2_in['u'], 'L2_ffn_weight': _L2_ffn_in['weight'], 'L2_ffn_scale_weight': _L2_ffn_in['scale_weight'], 'L2_ffn_bias': _L2_ffn_in['bias'], 'L3_cond_w': _L3_cond_in['w'], 'L3_cond_u': _L3_cond_in['u'], 'L3_attn_time_decay': _L3_attn_in['time_decay'], 'L3_attn_time_first': _L3_attn_in['time_first'], 'L3_attn_time_mix_k': _L3_attn_in['time_mix_k'], 'L3_attn_time_mix_v': _L3_attn_in['time_mix_v'], 'L3_attn_time_mix_r': _L3_attn_in['time_mix_r'], 'L3_attn_Wk': _L3_attn_in['Wk'], 'L3_attn_Wv': _L3_attn_in['Wv'], 'L3_attn_Wr': _L3_attn_in['Wr'], 'L3_attn_Wo': _L3_attn_in['Wo'], 'L3_cond2_w': _L3_cond2_in['w'], 'L3_cond2_u': _L3_cond2_in['u'], 'L3_ffn_gate_w': _L3_ffn_in['gate_w'], 'L3_ffn_w_gate': _L3_ffn_in['w_gate'], 'L3_ffn_w_up': _L3_ffn_in['w_up'], 'L3_ffn_w_down': _L3_ffn_in['w_down'], 'L3_ffn_sw_gate': _L3_ffn_in['sw_gate'], 'L3_ffn_sw_up': _L3_ffn_in['sw_up'], 'L3_ffn_sw_down': _L3_ffn_in['sw_down'], 'L3_ffn_shared_gate_w': _L3_ffn_in['shared_gate_w']}

def reference(x, fside_BxSxS_0, cond_512, L0_cond_w, L0_cond_u, L0_attn_Wq, L0_attn_bq, L0_attn_Wk, L0_attn_bk, L0_attn_Wv, L0_attn_bv, L0_attn_Wo, L0_attn_bo, L0_attn_key_weights, L0_cond2_w, L0_cond2_u, L0_ffn_gate_w, L0_ffn_w_gate, L0_ffn_w_up, L0_ffn_w_down, L0_ffn_shgate_w, L0_ffn_shw_gate, L0_ffn_shw_up, L0_ffn_shw_down, L1_cond_w, L1_cond_u, L1_attn_w1, L1_attn_b1, L1_attn_conv_w, L1_attn_conv_b, L1_attn_wa, L1_attn_ba, L1_attn_wx, L1_attn_bx, L1_attn_lam, L1_attn_w2, L1_attn_b2, L1_cond2_w, L1_cond2_u, L1_ffn_wg, L1_ffn_fc1_w, L1_ffn_fc1_b, L1_ffn_fc2_w, L1_ffn_fc2_b, L2_cond_w, L2_cond_u, L2_attn_Wq, L2_attn_Wk, L2_attn_Wv, L2_attn_Wo, L2_attn_bo, L2_cond2_w, L2_cond2_u, L2_ffn_weight, L2_ffn_scale_weight, L2_ffn_bias, L3_cond_w, L3_cond_u, L3_attn_time_decay, L3_attn_time_first, L3_attn_time_mix_k, L3_attn_time_mix_v, L3_attn_time_mix_r, L3_attn_Wk, L3_attn_Wv, L3_attn_Wr, L3_attn_Wo, L3_cond2_w, L3_cond2_u, L3_ffn_gate_w, L3_ffn_w_gate, L3_ffn_w_up, L3_ffn_w_down, L3_ffn_sw_gate, L3_ffn_sw_up, L3_ffn_sw_down, L3_ffn_shared_gate_w):
    import jax
    import jax.numpy as jnp

    def _L0_cond_ref(r, k, v, w, u, time_emb):
        import jax, jax.numpy as jnp
        from jax import lax
        import numpy as np
        B, T, C, TD = (8, 256, 256, 64)

        def _bi_wkv(r, k, v, w, u, time_emb):
            tf = jax.nn.sigmoid(jnp.sum(time_emb, axis=-1))[:, None, None]
            decay = jnp.exp(-jnp.exp(w.astype(jnp.float32)))[None, :] * (0.5 + 0.5 * tf[:, :, 0])
            kf = k.astype(jnp.float32)
            vf = v.astype(jnp.float32)
            ek = jnp.exp(jnp.minimum(kf, 30.0))
            ekv = ek * vf

            def step(carry, x):
                a, b = carry
                ekv_t, ek_t = x
                a = a * decay + ekv_t
                b = b * decay + ek_t
                return ((a, b), (a, b))
            ekv_t = jnp.swapaxes(ekv, 0, 1)
            ek_t = jnp.swapaxes(ek, 0, 1)
            init = (jnp.zeros_like(decay), jnp.zeros_like(decay))
            _, (nf, df) = lax.scan(step, init, (ekv_t, ek_t))
            _, (nb, db) = lax.scan(step, init, (ekv_t, ek_t), reverse=True)
            nf = jnp.swapaxes(nf, 0, 1)
            df = jnp.swapaxes(df, 0, 1)
            nb = jnp.swapaxes(nb, 0, 1)
            db = jnp.swapaxes(db, 0, 1)
            euk = jnp.exp(jnp.minimum(u.astype(jnp.float32)[None, None, :] + kf, 30.0))
            num = nf + nb - ekv + euk * vf
            den = df + db - ek + euk
            base = jax.nn.sigmoid(r.astype(jnp.float32)) * (num / jnp.maximum(den, 1e-08))
            out = base * (0.8 + 0.2 * tf)
            return out.astype(r.dtype)
        return _bi_wkv(r, k, v, w, u, time_emb)

    def _L0_attn_ref(x, Wq, bq, Wk, bk, Wv, bv, Wo, bo, key_weights):
        import jax, jax.numpy as jnp
        import numpy as np
        HIDDEN = 256
        NUM_HEADS = 32
        HEAD_DIM = 64
        NUM_KV = 8
        GROUP = NUM_HEADS // NUM_KV
        SCALE = HEAD_DIM ** (-0.5)
        ROPE_BASE = 10000.0

        def apply_rope(t):
            S, D = (t.shape[-2], t.shape[-1])
            inv_freq = 1.0 / ROPE_BASE ** (jnp.arange(0, D, 2, dtype=jnp.float32) / D)
            ang = jnp.arange(S, dtype=jnp.float32)[:, None] * inv_freq[None, :]
            cos, sin = (jnp.cos(ang), jnp.sin(ang))
            x1, x2 = (t[..., :D // 2], t[..., D // 2:])
            return jnp.concatenate([x1 * cos - x2 * sin, x2 * cos + x1 * sin], axis=-1)
        B, S, _ = x.shape
        q = (x @ Wq.T + bq).reshape(B, S, NUM_HEADS, HEAD_DIM).transpose(0, 2, 1, 3)
        k = (x @ Wk.T + bk).reshape(B, S, NUM_KV, HEAD_DIM).transpose(0, 2, 1, 3)
        v = (x @ Wv.T + bv).reshape(B, S, NUM_KV, HEAD_DIM).transpose(0, 2, 1, 3)
        q = apply_rope(q)
        k = apply_rope(k)
        qg = q.reshape(B, NUM_KV, GROUP, S, HEAD_DIM)
        scores = jnp.einsum('bkgsd,bktd->bkgst', qg, k) * SCALE
        scores = scores * key_weights.reshape(1, NUM_KV, GROUP, 1, 1)
        causal = jnp.tril(jnp.ones((S, S), bool))
        scores = jnp.where(causal, scores, -jnp.inf)
        a = jax.nn.softmax(scores, axis=-1)
        o = jnp.einsum('bkgst,bktd->bkgsd', a, v)
        o = o.reshape(B, NUM_HEADS, S, HEAD_DIM).transpose(0, 2, 1, 3).reshape(B, S, NUM_HEADS * HEAD_DIM)
        return o @ Wo.T + bo

    def _L0_cond2_ref(r, k, v, w, u, time_emb):
        import jax, jax.numpy as jnp
        from jax import lax
        import numpy as np
        B, T, C, TD = (8, 256, 256, 64)

        def _bi_wkv(r, k, v, w, u, time_emb):
            tf = jax.nn.sigmoid(jnp.sum(time_emb, axis=-1))[:, None, None]
            decay = jnp.exp(-jnp.exp(w.astype(jnp.float32)))[None, :] * (0.5 + 0.5 * tf[:, :, 0])
            kf = k.astype(jnp.float32)
            vf = v.astype(jnp.float32)
            ek = jnp.exp(jnp.minimum(kf, 30.0))
            ekv = ek * vf

            def step(carry, x):
                a, b = carry
                ekv_t, ek_t = x
                a = a * decay + ekv_t
                b = b * decay + ek_t
                return ((a, b), (a, b))
            ekv_t = jnp.swapaxes(ekv, 0, 1)
            ek_t = jnp.swapaxes(ek, 0, 1)
            init = (jnp.zeros_like(decay), jnp.zeros_like(decay))
            _, (nf, df) = lax.scan(step, init, (ekv_t, ek_t))
            _, (nb, db) = lax.scan(step, init, (ekv_t, ek_t), reverse=True)
            nf = jnp.swapaxes(nf, 0, 1)
            df = jnp.swapaxes(df, 0, 1)
            nb = jnp.swapaxes(nb, 0, 1)
            db = jnp.swapaxes(db, 0, 1)
            euk = jnp.exp(jnp.minimum(u.astype(jnp.float32)[None, None, :] + kf, 30.0))
            num = nf + nb - ekv + euk * vf
            den = df + db - ek + euk
            base = jax.nn.sigmoid(r.astype(jnp.float32)) * (num / jnp.maximum(den, 1e-08))
            out = base * (0.8 + 0.2 * tf)
            return out.astype(r.dtype)
        return _bi_wkv(r, k, v, w, u, time_emb)

    def _L0_ffn_ref(x, gate_w, w_gate, w_up, w_down, shgate_w, shw_gate, shw_up, shw_down):
        import jax, jax.numpy as jnp
        import numpy as np
        B, L, D = (2, 128, 256)
        E, K = (8, 2)
        H, HS = (176, 352)
        b, l, d = x.shape
        xf = x.reshape(-1, d)
        logits = jnp.einsum('td,ed->te', xf.astype(jnp.float32), gate_w)
        probs = jax.nn.softmax(logits.astype(jnp.float32), axis=-1)
        weights, indices = jax.lax.top_k(probs, K)
        weights = (weights / weights.sum(-1, keepdims=True)).astype(x.dtype)
        onehot = jax.nn.one_hot(indices, E, dtype=x.dtype)
        combine = jnp.einsum('tk,tke->te', weights, onehot)
        g = jnp.einsum('td,edh->teh', xf, w_gate)
        u = jnp.einsum('td,edh->teh', xf, w_up)
        h = jax.nn.silu(g) * u
        out = jnp.einsum('teh,ehd,te->td', h.astype(jnp.float32), w_down.astype(jnp.float32), combine.astype(jnp.float32))
        sgate = jax.nn.sigmoid(xf @ shgate_w)[:, None]
        sh = jax.nn.silu(xf @ shw_gate) * (xf @ shw_up) @ shw_down
        out = out + (sgate * sh).astype(jnp.float32)
        return out.astype(x.dtype).reshape(b, l, d)

    def _L1_cond_ref(r, k, v, w, u, time_emb):
        import jax, jax.numpy as jnp
        from jax import lax
        import numpy as np
        B, T, C, TD = (8, 256, 256, 64)

        def _bi_wkv(r, k, v, w, u, time_emb):
            tf = jax.nn.sigmoid(jnp.sum(time_emb, axis=-1))[:, None, None]
            decay = jnp.exp(-jnp.exp(w.astype(jnp.float32)))[None, :] * (0.5 + 0.5 * tf[:, :, 0])
            kf = k.astype(jnp.float32)
            vf = v.astype(jnp.float32)
            ek = jnp.exp(jnp.minimum(kf, 30.0))
            ekv = ek * vf

            def step(carry, x):
                a, b = carry
                ekv_t, ek_t = x
                a = a * decay + ekv_t
                b = b * decay + ek_t
                return ((a, b), (a, b))
            ekv_t = jnp.swapaxes(ekv, 0, 1)
            ek_t = jnp.swapaxes(ek, 0, 1)
            init = (jnp.zeros_like(decay), jnp.zeros_like(decay))
            _, (nf, df) = lax.scan(step, init, (ekv_t, ek_t))
            _, (nb, db) = lax.scan(step, init, (ekv_t, ek_t), reverse=True)
            nf = jnp.swapaxes(nf, 0, 1)
            df = jnp.swapaxes(df, 0, 1)
            nb = jnp.swapaxes(nb, 0, 1)
            db = jnp.swapaxes(db, 0, 1)
            euk = jnp.exp(jnp.minimum(u.astype(jnp.float32)[None, None, :] + kf, 30.0))
            num = nf + nb - ekv + euk * vf
            den = df + db - ek + euk
            base = jax.nn.sigmoid(r.astype(jnp.float32)) * (num / jnp.maximum(den, 1e-08))
            out = base * (0.8 + 0.2 * tf)
            return out.astype(r.dtype)
        return _bi_wkv(r, k, v, w, u, time_emb)

    def _L1_attn_ref(x, w1, b1, conv_w, conv_b, wa, ba, wx, bx, lam, w2, b2):
        import jax, jax.numpy as jnp
        import numpy as np
        C_RGLRU = 8.0

        def _rg_lru(x, wa, ba, wx, bx, lam):
            r = jax.nn.sigmoid(jnp.einsum('bld,ed->ble', x, wa) + ba)
            i = jax.nn.sigmoid(jnp.einsum('bld,ed->ble', x, wx) + bx)
            log_a = -C_RGLRU * r * jax.nn.softplus(lam)
            a = jnp.exp(log_a)
            mult = jnp.sqrt(jnp.maximum(1.0 - jnp.exp(2.0 * log_a), 0.0))
            b = mult * (i * x)

            def combine(c1, c2):
                a1, b1 = c1
                a2, b2 = c2
                return (a1 * a2, a2 * b1 + b2)
            _, h = jax.lax.associative_scan(combine, (a, b), axis=1)
            return h
        h = jax.nn.silu(jnp.einsum('bld,rd->blr', x, w1) + b1)
        hc = h.transpose(0, 2, 1)
        hc = jax.lax.conv_general_dilated(hc, conv_w, window_strides=(1,), padding=[(3, 3)], rhs_dilation=(2,), dimension_numbers=('NCH', 'OIH', 'NCH'))
        hc = hc + conv_b[None, :, None]
        h = hc.transpose(0, 2, 1)
        h = _rg_lru(h, wa, ba, wx, bx, lam)
        return jnp.einsum('blr,dr->bld', h, w2) + b2

    def _L1_cond2_ref(r, k, v, w, u, time_emb):
        import jax, jax.numpy as jnp
        from jax import lax
        import numpy as np
        B, T, C, TD = (8, 256, 256, 64)

        def _bi_wkv(r, k, v, w, u, time_emb):
            tf = jax.nn.sigmoid(jnp.sum(time_emb, axis=-1))[:, None, None]
            decay = jnp.exp(-jnp.exp(w.astype(jnp.float32)))[None, :] * (0.5 + 0.5 * tf[:, :, 0])
            kf = k.astype(jnp.float32)
            vf = v.astype(jnp.float32)
            ek = jnp.exp(jnp.minimum(kf, 30.0))
            ekv = ek * vf

            def step(carry, x):
                a, b = carry
                ekv_t, ek_t = x
                a = a * decay + ekv_t
                b = b * decay + ek_t
                return ((a, b), (a, b))
            ekv_t = jnp.swapaxes(ekv, 0, 1)
            ek_t = jnp.swapaxes(ek, 0, 1)
            init = (jnp.zeros_like(decay), jnp.zeros_like(decay))
            _, (nf, df) = lax.scan(step, init, (ekv_t, ek_t))
            _, (nb, db) = lax.scan(step, init, (ekv_t, ek_t), reverse=True)
            nf = jnp.swapaxes(nf, 0, 1)
            df = jnp.swapaxes(df, 0, 1)
            nb = jnp.swapaxes(nb, 0, 1)
            db = jnp.swapaxes(db, 0, 1)
            euk = jnp.exp(jnp.minimum(u.astype(jnp.float32)[None, None, :] + kf, 30.0))
            num = nf + nb - ekv + euk * vf
            den = df + db - ek + euk
            base = jax.nn.sigmoid(r.astype(jnp.float32)) * (num / jnp.maximum(den, 1e-08))
            out = base * (0.8 + 0.2 * tf)
            return out.astype(r.dtype)
        return _bi_wkv(r, k, v, w, u, time_emb)

    def _L1_ffn_ref(x, wg, fc1_w, fc1_b, fc2_w, fc2_b):
        import jax, jax.numpy as jnp
        import numpy as np
        D_MODEL = 256
        HIDDEN = 4 * D_MODEL
        N_EXPERTS = 8
        TOP_K = 2
        CAP_FACTOR = 1.0
        B, L, D = x.shape
        S = B * L
        E = wg.shape[1]
        K = TOP_K
        C = int(K * S * CAP_FACTOR) // E
        xt = x.reshape(S, D)
        scores = jax.nn.softmax(xt.astype(jnp.float32) @ wg.astype(jnp.float32), axis=-1)
        gate_vals, idx = jax.lax.top_k(scores, K)
        gate_vals = gate_vals / jnp.clip(jnp.sum(gate_vals, axis=-1, keepdims=True), 1e-09)
        counts = jnp.zeros((E,), jnp.int32)
        disp = jnp.zeros((E, C, D), x.dtype)
        pos_safe_l, valid_l = ([], [])
        for s in range(K):
            mask = jax.nn.one_hot(idx[:, s], E, dtype=jnp.int32)
            loc = jnp.cumsum(mask, axis=0) - 1 + counts[None, :]
            pos = jnp.sum(loc * mask, axis=-1)
            counts = counts + jnp.sum(mask, axis=0)
            valid = pos < C
            pos_safe = jnp.where(valid, pos, 0)
            disp = disp.at[idx[:, s], pos_safe].add(xt * valid[:, None].astype(x.dtype))
            pos_safe_l.append(pos_safe)
            valid_l.append(valid)
        h = jax.nn.gelu(jnp.einsum('ecd,edh->ech', disp, fc1_w) + fc1_b[:, None, :], approximate=False)
        eo = jnp.einsum('ech,ehd->ecd', h, fc2_w) + fc2_b[:, None, :]
        y = jnp.zeros((S, D), x.dtype)
        for s in range(K):
            g = (gate_vals[:, s] * valid_l[s].astype(gate_vals.dtype)).astype(x.dtype)
            y = y + g[:, None] * eo[idx[:, s], pos_safe_l[s]]
        return y.reshape(B, L, D)

    def _L2_cond_ref(r, k, v, w, u, time_emb):
        import jax, jax.numpy as jnp
        from jax import lax
        import numpy as np
        B, T, C, TD = (8, 256, 256, 64)

        def _bi_wkv(r, k, v, w, u, time_emb):
            tf = jax.nn.sigmoid(jnp.sum(time_emb, axis=-1))[:, None, None]
            decay = jnp.exp(-jnp.exp(w.astype(jnp.float32)))[None, :] * (0.5 + 0.5 * tf[:, :, 0])
            kf = k.astype(jnp.float32)
            vf = v.astype(jnp.float32)
            ek = jnp.exp(jnp.minimum(kf, 30.0))
            ekv = ek * vf

            def step(carry, x):
                a, b = carry
                ekv_t, ek_t = x
                a = a * decay + ekv_t
                b = b * decay + ek_t
                return ((a, b), (a, b))
            ekv_t = jnp.swapaxes(ekv, 0, 1)
            ek_t = jnp.swapaxes(ek, 0, 1)
            init = (jnp.zeros_like(decay), jnp.zeros_like(decay))
            _, (nf, df) = lax.scan(step, init, (ekv_t, ek_t))
            _, (nb, db) = lax.scan(step, init, (ekv_t, ek_t), reverse=True)
            nf = jnp.swapaxes(nf, 0, 1)
            df = jnp.swapaxes(df, 0, 1)
            nb = jnp.swapaxes(nb, 0, 1)
            db = jnp.swapaxes(db, 0, 1)
            euk = jnp.exp(jnp.minimum(u.astype(jnp.float32)[None, None, :] + kf, 30.0))
            num = nf + nb - ekv + euk * vf
            den = df + db - ek + euk
            base = jax.nn.sigmoid(r.astype(jnp.float32)) * (num / jnp.maximum(den, 1e-08))
            out = base * (0.8 + 0.2 * tf)
            return out.astype(r.dtype)
        return _bi_wkv(r, k, v, w, u, time_emb)

    def _L2_attn_ref(hidden_states, Wq, Wk, Wv, Wo, bo):
        import jax, jax.numpy as jnp
        import numpy as np
        B, S, QD = (2, 512, 256)
        H, D = (32, 64)
        INNER = H * D
        b, s, _ = hidden_states.shape

        def proj(W):
            return (hidden_states @ W).reshape(b, s, H, D).transpose(0, 2, 1, 3)
        q = jax.nn.relu(proj(Wq))
        k = jax.nn.relu(proj(Wk))
        v = proj(Wv)
        kv = jnp.einsum('bhsd,bhse->bhde', k, v)
        qkv = jnp.einsum('bhsd,bhde->bhse', q, kv)
        key_sum = k.sum(axis=2)
        normalizer = jnp.einsum('bhsd,bhd->bhs', q, key_sum)
        normalizer = jnp.clip(normalizer, 1e-06, None)[..., None]
        out = qkv / normalizer
        out = out.transpose(0, 2, 1, 3).reshape(b, s, INNER)
        return out @ Wo + bo

    def _L2_cond2_ref(r, k, v, w, u, time_emb):
        import jax, jax.numpy as jnp
        from jax import lax
        import numpy as np
        B, T, C, TD = (8, 256, 256, 64)

        def _bi_wkv(r, k, v, w, u, time_emb):
            tf = jax.nn.sigmoid(jnp.sum(time_emb, axis=-1))[:, None, None]
            decay = jnp.exp(-jnp.exp(w.astype(jnp.float32)))[None, :] * (0.5 + 0.5 * tf[:, :, 0])
            kf = k.astype(jnp.float32)
            vf = v.astype(jnp.float32)
            ek = jnp.exp(jnp.minimum(kf, 30.0))
            ekv = ek * vf

            def step(carry, x):
                a, b = carry
                ekv_t, ek_t = x
                a = a * decay + ekv_t
                b = b * decay + ek_t
                return ((a, b), (a, b))
            ekv_t = jnp.swapaxes(ekv, 0, 1)
            ek_t = jnp.swapaxes(ek, 0, 1)
            init = (jnp.zeros_like(decay), jnp.zeros_like(decay))
            _, (nf, df) = lax.scan(step, init, (ekv_t, ek_t))
            _, (nb, db) = lax.scan(step, init, (ekv_t, ek_t), reverse=True)
            nf = jnp.swapaxes(nf, 0, 1)
            df = jnp.swapaxes(df, 0, 1)
            nb = jnp.swapaxes(nb, 0, 1)
            db = jnp.swapaxes(db, 0, 1)
            euk = jnp.exp(jnp.minimum(u.astype(jnp.float32)[None, None, :] + kf, 30.0))
            num = nf + nb - ekv + euk * vf
            den = df + db - ek + euk
            base = jax.nn.sigmoid(r.astype(jnp.float32)) * (num / jnp.maximum(den, 1e-08))
            out = base * (0.8 + 0.2 * tf)
            return out.astype(r.dtype)
        return _bi_wkv(r, k, v, w, u, time_emb)

    def _L2_ffn_ref(x, weight, scale_weight, bias):
        import jax, jax.numpy as jnp
        import numpy as np
        w = weight * scale_weight[:, None]
        out = jnp.einsum('bsi,oi->bso', x, w) + bias
        return out

    def _L3_cond_ref(r, k, v, w, u, time_emb):
        import jax, jax.numpy as jnp
        from jax import lax
        import numpy as np
        B, T, C, TD = (8, 256, 256, 64)

        def _bi_wkv(r, k, v, w, u, time_emb):
            tf = jax.nn.sigmoid(jnp.sum(time_emb, axis=-1))[:, None, None]
            decay = jnp.exp(-jnp.exp(w.astype(jnp.float32)))[None, :] * (0.5 + 0.5 * tf[:, :, 0])
            kf = k.astype(jnp.float32)
            vf = v.astype(jnp.float32)
            ek = jnp.exp(jnp.minimum(kf, 30.0))
            ekv = ek * vf

            def step(carry, x):
                a, b = carry
                ekv_t, ek_t = x
                a = a * decay + ekv_t
                b = b * decay + ek_t
                return ((a, b), (a, b))
            ekv_t = jnp.swapaxes(ekv, 0, 1)
            ek_t = jnp.swapaxes(ek, 0, 1)
            init = (jnp.zeros_like(decay), jnp.zeros_like(decay))
            _, (nf, df) = lax.scan(step, init, (ekv_t, ek_t))
            _, (nb, db) = lax.scan(step, init, (ekv_t, ek_t), reverse=True)
            nf = jnp.swapaxes(nf, 0, 1)
            df = jnp.swapaxes(df, 0, 1)
            nb = jnp.swapaxes(nb, 0, 1)
            db = jnp.swapaxes(db, 0, 1)
            euk = jnp.exp(jnp.minimum(u.astype(jnp.float32)[None, None, :] + kf, 30.0))
            num = nf + nb - ekv + euk * vf
            den = df + db - ek + euk
            base = jax.nn.sigmoid(r.astype(jnp.float32)) * (num / jnp.maximum(den, 1e-08))
            out = base * (0.8 + 0.2 * tf)
            return out.astype(r.dtype)
        return _bi_wkv(r, k, v, w, u, time_emb)

    def _L3_attn_ref(x, time_decay, time_first, time_mix_k, time_mix_v, time_mix_r, Wk, Wv, Wr, Wo):
        import jax, jax.numpy as jnp
        import numpy as np
        B, T, C = (8, 128, 256)
        NEG_BIG = -1e+38

        def rwkv_linear_attention(time_decay, time_first, k, v):
            w = -jnp.exp(time_decay)
            u = time_first
            num0 = jnp.zeros(k.shape[::2], dtype=jnp.float32)
            den0 = jnp.zeros_like(num0)
            max0 = jnp.full_like(num0, NEG_BIG)

            def step(carry, kv_t):
                num, den, mx = carry
                kt, vt = kv_t
                mo = jnp.maximum(mx, kt + u)
                e1 = jnp.exp(mx - mo)
                e2 = jnp.exp(kt + u - mo)
                out = (e1 * num + e2 * vt) / (e1 * den + e2)
                ms = jnp.maximum(mx + w, kt)
                e1s = jnp.exp(mx + w - ms)
                e2s = jnp.exp(kt - ms)
                return ((e1s * num + e2s * vt, e1s * den + e2s, ms), out)
            kT = jnp.swapaxes(k, 0, 1).astype(jnp.float32)
            vT = jnp.swapaxes(v, 0, 1).astype(jnp.float32)
            _, outT = jax.lax.scan(step, (num0, den0, max0), (kT, vT))
            return jnp.swapaxes(outT, 0, 1).astype(k.dtype)
        shifted = jnp.pad(x, ((0, 0), (1, 0), (0, 0)))[:, :-1]
        xk = x * time_mix_k + shifted * (1 - time_mix_k)
        xv = x * time_mix_v + shifted * (1 - time_mix_v)
        xr = x * time_mix_r + shifted * (1 - time_mix_r)
        k = jnp.einsum('btc,dc->btd', xk, Wk)
        v = jnp.einsum('btc,dc->btd', xv, Wv)
        r = jnp.einsum('btc,dc->btd', xr, Wr)
        sr = jax.nn.sigmoid(r)
        rwkv = sr * rwkv_linear_attention(time_decay, time_first, k, v)
        return jnp.einsum('btd,cd->btc', rwkv, Wo)

    def _L3_cond2_ref(r, k, v, w, u, time_emb):
        import jax, jax.numpy as jnp
        from jax import lax
        import numpy as np
        B, T, C, TD = (8, 256, 256, 64)

        def _bi_wkv(r, k, v, w, u, time_emb):
            tf = jax.nn.sigmoid(jnp.sum(time_emb, axis=-1))[:, None, None]
            decay = jnp.exp(-jnp.exp(w.astype(jnp.float32)))[None, :] * (0.5 + 0.5 * tf[:, :, 0])
            kf = k.astype(jnp.float32)
            vf = v.astype(jnp.float32)
            ek = jnp.exp(jnp.minimum(kf, 30.0))
            ekv = ek * vf

            def step(carry, x):
                a, b = carry
                ekv_t, ek_t = x
                a = a * decay + ekv_t
                b = b * decay + ek_t
                return ((a, b), (a, b))
            ekv_t = jnp.swapaxes(ekv, 0, 1)
            ek_t = jnp.swapaxes(ek, 0, 1)
            init = (jnp.zeros_like(decay), jnp.zeros_like(decay))
            _, (nf, df) = lax.scan(step, init, (ekv_t, ek_t))
            _, (nb, db) = lax.scan(step, init, (ekv_t, ek_t), reverse=True)
            nf = jnp.swapaxes(nf, 0, 1)
            df = jnp.swapaxes(df, 0, 1)
            nb = jnp.swapaxes(nb, 0, 1)
            db = jnp.swapaxes(db, 0, 1)
            euk = jnp.exp(jnp.minimum(u.astype(jnp.float32)[None, None, :] + kf, 30.0))
            num = nf + nb - ekv + euk * vf
            den = df + db - ek + euk
            base = jax.nn.sigmoid(r.astype(jnp.float32)) * (num / jnp.maximum(den, 1e-08))
            out = base * (0.8 + 0.2 * tf)
            return out.astype(r.dtype)
        return _bi_wkv(r, k, v, w, u, time_emb)

    def _L3_ffn_ref(hidden_states, gate_w, w_gate, w_up, w_down, sw_gate, sw_up, sw_down, shared_gate_w):
        import jax, jax.numpy as jnp
        import numpy as np
        B, S, H = (2, 128, 256)
        E, K = (8, 2)
        I = 176
        IS = 704
        WSCALE = 0.02
        x = hidden_states
        logits = jnp.einsum('bsh,eh->bse', x, gate_w)
        probs = jax.nn.softmax(logits, axis=-1)
        top_w, top_i = jax.lax.top_k(probs, K)
        top_w = top_w / jnp.sum(top_w, axis=-1, keepdims=True)
        onehot = jax.nn.one_hot(top_i, E, dtype=x.dtype)
        combine = jnp.einsum('bsk,bske->bse', top_w, onehot)
        g = jnp.einsum('bsh,ehi->besi', x, w_gate)
        u = jnp.einsum('bsh,ehi->besi', x, w_up)
        h = jax.nn.silu(g) * u
        expert_out = jnp.einsum('besi,eih->besh', h, w_down)
        moe_out = jnp.einsum('besh,bse->bsh', expert_out, combine)
        sh = jax.nn.silu(x @ sw_gate) * (x @ sw_up)
        shared_out = sh @ sw_down
        shared_gate = jax.nn.sigmoid(x @ shared_gate_w)
        return moe_out + shared_out * shared_gate
    x = x + _L0_attn_ref(_L0_cond_ref(x, fside_BxSxS_0, fside_BxSxS_0, L0_cond_w, L0_cond_u, cond_512), L0_attn_Wq, L0_attn_bq, L0_attn_Wk, L0_attn_bk, L0_attn_Wv, L0_attn_bv, L0_attn_Wo, L0_attn_bo, L0_attn_key_weights)
    x = x + _L0_ffn_ref(_L0_cond2_ref(x, fside_BxSxS_0, fside_BxSxS_0, L0_cond2_w, L0_cond2_u, cond_512), L0_ffn_gate_w, L0_ffn_w_gate, L0_ffn_w_up, L0_ffn_w_down, L0_ffn_shgate_w, L0_ffn_shw_gate, L0_ffn_shw_up, L0_ffn_shw_down)
    x = x + _L1_attn_ref(_L1_cond_ref(x, fside_BxSxS_0, fside_BxSxS_0, L1_cond_w, L1_cond_u, cond_512), L1_attn_w1, L1_attn_b1, L1_attn_conv_w, L1_attn_conv_b, L1_attn_wa, L1_attn_ba, L1_attn_wx, L1_attn_bx, L1_attn_lam, L1_attn_w2, L1_attn_b2)
    x = x + _L1_ffn_ref(_L1_cond2_ref(x, fside_BxSxS_0, fside_BxSxS_0, L1_cond2_w, L1_cond2_u, cond_512), L1_ffn_wg, L1_ffn_fc1_w, L1_ffn_fc1_b, L1_ffn_fc2_w, L1_ffn_fc2_b)
    x = x + _L2_attn_ref(_L2_cond_ref(x, fside_BxSxS_0, fside_BxSxS_0, L2_cond_w, L2_cond_u, cond_512), L2_attn_Wq, L2_attn_Wk, L2_attn_Wv, L2_attn_Wo, L2_attn_bo)
    x = x + _L2_ffn_ref(_L2_cond2_ref(x, fside_BxSxS_0, fside_BxSxS_0, L2_cond2_w, L2_cond2_u, cond_512), L2_ffn_weight, L2_ffn_scale_weight, L2_ffn_bias)
    x = x + _L3_attn_ref(_L3_cond_ref(x, fside_BxSxS_0, fside_BxSxS_0, L3_cond_w, L3_cond_u, cond_512), L3_attn_time_decay, L3_attn_time_first, L3_attn_time_mix_k, L3_attn_time_mix_v, L3_attn_time_mix_r, L3_attn_Wk, L3_attn_Wv, L3_attn_Wr, L3_attn_Wo)
    x = x + _L3_ffn_ref(_L3_cond2_ref(x, fside_BxSxS_0, fside_BxSxS_0, L3_cond2_w, L3_cond2_u, cond_512), L3_ffn_gate_w, L3_ffn_w_gate, L3_ffn_w_up, L3_ffn_w_down, L3_ffn_sw_gate, L3_ffn_sw_up, L3_ffn_sw_down, L3_ffn_shared_gate_w)
    return x

_drawn_inputs = setup_inputs


def setup_inputs(seed=0):
    import zlib

    import numpy as np

    out = dict(_drawn_inputs(seed))
    spreads = {'L0_attn_bq': (0.0, 0.8),
     'L0_attn_bk': (0.0, 0.8),
     'L0_attn_bv': (0.0, 0.1),
     'L0_attn_bo': (0.0, 0.1),
     'L1_attn_b1': (0.0, 0.1),
     'L1_attn_conv_b': (0.0, 0.1),
     'L1_attn_ba': (0.0, 0.8),
     'L1_attn_bx': (0.0, 0.8),
     'L1_attn_b2': (0.0, 0.1),
     'L1_ffn_fc1_b': (0.0, 0.418),
     'L1_ffn_fc2_b': (0.0, 0.1)}
    factors = {'L0_attn_Wq': 4.889,
     'L0_attn_Wk': 4.864,
     'L0_attn_key_weights': 5.079,
     'L0_cond2_w': 8.0,
     'L0_cond2_u': 8.0,
     'L0_ffn_gate_w': 8.0,
     'L0_ffn_w_gate': 8.0,
     'L0_ffn_w_up': 8.0,
     'L0_ffn_w_down': 8.0,
     'L0_ffn_shgate_w': 8.0,
     'L0_ffn_shw_gate': 8.0,
     'L0_ffn_shw_up': 8.0,
     'L0_ffn_shw_down': 8.0,
     'L1_cond_u': 3.736,
     'L1_attn_wa': 8.0,
     'L1_attn_wx': 3.229,
     'L1_attn_lam': 8.0,
     'L2_attn_Wq': 7.564,
     'L2_attn_Wk': 6.281,
     'L2_attn_bo': 6.084,
     'L2_cond2_u': 3.369,
     'L2_ffn_bias': 3.481,
     'L3_cond_w': 8.0,
     'L3_cond_u': 8.0,
     'L3_attn_time_decay': 8.0,
     'L3_attn_time_first': 8.0,
     'L3_attn_time_mix_k': 8.0,
     'L3_attn_time_mix_v': 8.0,
     'L3_attn_time_mix_r': 8.0,
     'L3_attn_Wk': 8.0,
     'L3_attn_Wv': 3.076,
     'L3_attn_Wr': 8.0,
     'L3_attn_Wo': 3.119,
     'L3_cond2_w': 8.0,
     'L3_cond2_u': 8.0,
     'L3_ffn_gate_w': 8.0,
     'L3_ffn_w_gate': 8.0,
     'L3_ffn_w_up': 8.0,
     'L3_ffn_w_down': 8.0,
     'L3_ffn_sw_gate': 8.0,
     'L3_ffn_sw_up': 8.0,
     'L3_ffn_sw_down': 8.0,
     'L3_ffn_shared_gate_w': 8.0}
    for name, (base, spread) in spreads.items():
        noise = np.random.default_rng([zlib.crc32(name.encode()), seed]).standard_normal(out[name].shape)
        drawn = base * np.exp(spread * noise) if base else spread * noise
        out[name] = jnp.asarray(drawn.astype(out[name].dtype))
    for name, factor in factors.items():
        out[name] = (out[name] * factor).astype(out[name].dtype)
    return out
```

```python
from contextlib import ExitStack

import numpy as np

import concourse.bass as bass
from concourse import mybir

P = 128
NB, T, C = 4, 256, 256
NT = NB * T
CH = C // P
HALF = NT // 2
NL = 8
NP = CH * NB

HD = 64
L0_PAIRS, L0_GROUP = 4, 4
NE, EH = 8, 176
L0_SH, L3_SH = 352, 704
R1, TAPS = 320, 4
FF, CAP = 1024, 256
SLOTS = NE * CAP
L2_PAIRS = 16

F32 = mybir.dt.float32
U32 = mybir.dt.uint32
ALU = mybir.AluOpType
ACT = mybir.ActivationFunctionType
AX_X = mybir.AxisListType.X
ds = bass.ds
NEG = -1.0e30


def vec_columns():
    sizes = [("w", 2 * NL), ("u", NP * NL), ("bq", 16), ("kw", 16), ("bk", 4), ("bv", 4), ("bo0", 2),
             ("b1", 3), ("convb", 3), ("ba", 3), ("bx", 3), ("lam", 3), ("b2", 2), ("fc1b", NE * FF // P),
             ("bo2", 2), ("fscale", 2), ("fbias", 2), ("decay", 2), ("first", 2), ("mk", 2), ("mv", 2),
             ("mr", 2)]
    at, out = 0, {}
    for name, n in sizes:
        out[name] = (at, n)
        at += n
    return out, at


VEC, NVEC = vec_columns()


class Steps:

    def __init__(self, eng, sem):
        self.eng, self.sem, self.base, self.n = eng, sem, 0, 0

    def mark(self, ins):
        self.n += 1
        return ins.then_inc(self.sem, 1)

    def wait(self):
        self.eng.wait_ge(self.sem, self.base + self.n)

    def link(self, ins):
        self.mark(ins)
        self.wait()

    def enter(self, i, per):
        self.kept = self.base + self.n
        self.base, self.n, self.per = self.kept + i * per, 0, per

    def leave(self, count):
        assert self.n == self.per, (self.n, self.per)
        self.base, self.n = self.kept + count * self.per, 0


def build_program(nc, io):
    outer = ExitStack()

    def sem(name):
        return outer.enter_context(nc.semaphore(name))

    def keep(name, shape, dt=F32):
        return outer.enter_context(nc.sbuf_tensor(name, shape, dt))

    xT = keep("xT", [P, CH, NT])
    xin = keep("xin", [P, CH, NT])
    fside = keep("fside", [P, CH, NT])
    ek = keep("ek", [P, CH, NT])
    ekv = keep("ekv", [P, CH, NT])
    ek_back = keep("ek_back", [P, CH, NT])
    ekv_back = keep("ekv_back", [P, CH, NT])
    vecs = keep("vecs", [P, NVEC])
    ident = keep("ident", [P, P])
    decay = keep("decay", [P, NL * CH * NB])
    gain = keep("gain", [P, NB])
    mod = keep("mod", [P, 2, CH, NT])
    uk = keep("uk", [P, 2, T])
    scans = keep("scans", [P, 2, 2, 2, T])
    terms = keep("terms", [P, 2, 2, T])
    sums = keep("sums", [P, 2, 2, T])

    dve_steps_sem, act_steps_sem, pool_steps_sem = sem("dve_steps"), sem("act_steps"), sem("pool_steps")
    uk_ready = sem("uk_ready")
    euk_ready = sem("euk_ready")
    scans_ready = sem("scans_ready")
    sums_ready = sem("sums_ready")
    sig_ready = sem("sig_ready")
    xin_ready = sem("xin_ready")
    sub_ready = sem("sub_ready")
    exp_ready = sem("exp_ready")
    steps = {"dve": Steps(nc.vector, dve_steps_sem), "act": Steps(nc.scalar, act_steps_sem),
             "pool": Steps(nc.gpsimd, pool_steps_sem)}
    dstep, astep, pstep = steps["dve"], steps["act"], steps["pool"]

    def need(eng, semaphore, count):
        if not isinstance(count, int) or count > 0:
            eng.wait_ge(semaphore, count)

    def vec(name, i=0):
        return vecs[:, ds(VEC[name][0] + i, 1)]

    def part(x, i):
        return x[:, :, :].rearrange("p c t -> p (c t)")[:, ds(i * T, T)]

    def piece_scans(dve, l, i, k):
        dve.tensor_scalar(uk[:, k, :], part(fside, i), vec("u", NP * l + i), 30.0, ALU.add, ALU.min).then_inc(uk_ready, 1)
        dec = decay[:, ds(NP * l + i, 1)]
        for kind, src, back in ((0, ekv, ekv_back), (1, ek, ek_back)):
            dve.tensor_tensor_scan(scans[:, k, kind, 0, :], dec.to_broadcast([P, T]), part(src, i), 0.0, ALU.mult, ALU.add)
            ins = dve.tensor_tensor_scan(scans[:, k, kind, 1, 0:T - 1][:, ::-1], part(back, i)[:, 0:T - 1],
                                         dec.to_broadcast([P, T - 1]), 0.0, ALU.add, ALU.mult)
        ins.then_inc(scans_ready, 1)

    def piece_act(act, l, i, k):
        act.wait_ge(uk_ready, NP * l + i + 1)
        act.activation(terms[:, k, 1, :], uk[:, k, :], ACT.Exp).then_inc(euk_ready, 1)

    def piece_pool(pool, l, i, k):
        pool.wait_ge(euk_ready, NP * l + i + 1)
        pstep.mark(pool.tensor_tensor(terms[:, k, 0, :], terms[:, k, 1, :], part(fside, i), ALU.mult))
        pool.wait_ge(scans_ready, NP * l + i + 1)
        pstep.link(pool.tensor_tensor(sums[:, k, :, :], scans[:, k, :, 0, :], scans[:, k, :, 1, :], ALU.add))
        pool.tensor_tensor(sums[:, k, :, :], sums[:, k, :, :], terms[:, k, :, :], ALU.add).then_inc(sums_ready, 1)

    PIECE_POOL_STEPS = 2

    def piece_finish(dve, l, i, k):
        dve.wait_ge(sums_ready, NP * l + i + 1)
        den = sums[:, k, 1, :]
        dstep.link(dve.tensor_scalar(den, den, 1e-8, None, ALU.max))
        dstep.link(dve.reciprocal(den, den))
        dstep.mark(dve.tensor_tensor(part(mod[:, l % 2], i), sums[:, k, 0, :], den, ALU.mult))

    PIECE_DVE_STEPS = 3

    def block_dve(dve, l):
        for i in range(NP):
            piece_scans(dve, l, i, i % 2)
            if i:
                piece_finish(dve, l, i - 1, (i - 1) % 2)
        piece_finish(dve, l, NP - 1, (NP - 1) % 2)

    def block_act(act, l):
        for i in range(NP):
            piece_act(act, l, i, i % 2)

    def block_pool(pool, l):
        for i in range(NP):
            piece_pool(pool, l, i, i % 2)

    def condition_act(act, sig):
        act.activation(sig[:, :, :], xT[:, :, :], ACT.Sigmoid).then_inc(sig_ready, 1)

    def condition_dve(dve, l, sig):
        dve.wait_ge(sig_ready, l + 1)
        dstep.wait()
        for b in range(NB):
            c = slice(b * T, (b + 1) * T)
            ins = dve.scalar_tensor_tensor(out=xin[:, :, c], in0=sig[:, :, c], scalar=gain[:, b:b + 1],
                                           in1=mod[:, l % 2, :, c], op0=ALU.mult, op1=ALU.mult)
        ins.then_inc(xin_ready, 1)

    disp_dram = nc.dram_tensor("disp_scratch", (SLOTS, C), F32, kind="Internal").ap()
    eo_dram = nc.dram_tensor("expert_out_scratch", (SLOTS, C), F32, kind="Internal").ap()

    def stage_first():
        with ExitStack() as st:
            crep = st.enter_context(nc.sbuf_tensor("crep", [P, NB, 64], F32))
            small = st.enter_context(nc.sbuf_tensor("small", [P, 8 * NB], F32))
            wexp = st.enter_context(nc.sbuf_tensor("wexp", [P, 2, 2 * NL], F32))
            fmin = st.enter_context(nc.sbuf_tensor("fmin", [P, CH, NT], F32))
            s_vec, s_x, s_f, s_c, s_id = sem("ld_vecs"), sem("ld_x"), sem("ld_f"), sem("ld_cond"), sem("ld_ident")
            s_tfsum, s_tf, s_fmin, s_ek, s_wexp = (sem(n) for n in ("tf_sum", "tf", "f_min", "ek_rdy", "w_exp"))
            s_zero, s_back, s_blank, s_blanked = sem("zeroed"), sem("reversed"), sem("blank"), sem("slots_blanked")
            block = st.enter_context(nc.Block())

            @block.sync
            def _(sp):
                sp.dma_start(fside[:, :, :], io["fT"]).then_inc(s_f, 16)
                sp.dma_start(vecs[:, :], io["vecs"]).then_inc(s_vec, 16)
                sp.dma_start(crep[:, :, :], io["cond"]).then_inc(s_c, 16)
                sp.dma_start(xT[:, :, :], io["xT"]).then_inc(s_x, 16)
                sp.dma_start(ident[:, :], io["ident"]).then_inc(s_id, 16)
                sp.wait_ge(s_blank, 1)
                for i in range(2):
                    sp.dma_start(disp_dram.rearrange("(i p a) d -> i p (a d)", i=2, p=P)[i],
                                 xin[:, :, :].rearrange("p c t -> p (c t)")).then_inc(s_blanked, 16)
                sp.wait_ge(s_blanked, 32)
                sp.wait_ge(s_x, 16)
                sp.wait_ge(s_id, 16)

            @block.gpsimd
            def _(pool):
                pstep.link(pool.memset(scans[:, :, :, :, :], 0.0))
                pool.memset(xin[:, :, :], 0.0).then_inc(s_blank, 1)
                pool.wait_ge(s_ek, 1)
                pool.wait_ge(s_f, 16)
                pool.tensor_tensor(ekv[:, :, :], ek[:, :, :], fside[:, :, :], ALU.mult).then_inc(s_zero, 1)
                block_pool(pool, 0)

            @block.scalar
            def _(act):
                act.wait_ge(s_vec, 16)
                astep.link(act.activation(wexp[:, 0, :], vecs[:, 0:2 * NL], ACT.Exp))
                act.activation(wexp[:, 1, :], wexp[:, 0, :], ACT.Exp, scale=-1.0).then_inc(s_wexp, 1)
                act.wait_ge(s_fmin, 1)
                act.activation(ek[:, :, :], fmin[:, :, :], ACT.Exp).then_inc(s_ek, 1)
                back = lambda x: x[:, :, :].rearrange("p c (b t) -> p (c b) t", b=NB)[:, :, ::-1]
                ahead = lambda x: x[:, :, :].rearrange("p c (b t) -> p (c b) t", b=NB)
                act.activation(ahead(ek_back), back(fmin), ACT.Exp)
                act.wait_ge(s_tfsum, 1)
                act.activation(small[:, NB:2 * NB], small[:, 0:NB], ACT.Sigmoid).then_inc(s_tf, 1)
                act.wait_ge(s_zero, 1)
                act.activation(ahead(ekv_back), back(ekv), ACT.Identity).then_inc(s_back, 1)
                block_act(act, 0)

            @block.vector
            def _(dve):
                dve.wait_ge(s_f, 16)
                dve.tensor_scalar(fmin[:, :, :], fside[:, :, :], 30.0, None, ALU.min).then_inc(s_fmin, 1)
                dve.wait_ge(s_c, 16)
                dve.tensor_reduce(small[:, 0:NB], crep[:, :, :], AX_X, ALU.add).then_inc(s_tfsum, 1)
                dve.wait_ge(s_tf, 1)
                tf = small[:, NB:2 * NB]
                dve.tensor_scalar(gain[:, :], tf, 0.2, 0.8, ALU.mult, ALU.add)
                dstep.link(dve.tensor_scalar(small[:, 2 * NB:3 * NB], tf, 0.5, 0.5, ALU.mult, ALU.add))
                dve.wait_ge(s_wexp, 1)
                for b in range(NB):
                    ins = dve.tensor_scalar(decay[:, :].rearrange("p (c b) -> p c b", b=NB)[:, :, b], wexp[:, 1, :],
                                            small[:, 2 * NB + b:2 * NB + b + 1], None, ALU.mult)
                dstep.link(ins)
                dve.wait_ge(s_back, 1)
                block_dve(dve, 0)

    stage_first()

    def stage_l0_attn(l):
        NU = L0_GROUP * NB
        NPROJ = 4 + 2 * L0_GROUP
        with ExitStack() as st:
            def sb(name, shape, dt=F32):
                return st.enter_context(nc.sbuf_tensor(name, shape, dt))

            sig = sb("sigA", [P, CH, NT])
            wkvq = sb("wkvq", [P, 512 + 1024])
            wk = wkvq[:, 0:256].rearrange("p (k f) -> p k f", k=CH)
            wv = wkvq[:, 256:512].rearrange("p (k f) -> p k f", k=CH)
            wq = wkvq[:, 512:1536].rearrange("p (m k f) -> p m k f", m=L0_GROUP, k=CH)
            wo = sb("wo", [P, L0_GROUP, C])
            rope = sb("rope", [P, 2, T])
            mask = sb("mask", [P, P])
            kraw, kswap = sb("kraw", [P, NT]), sb("kswap", [P, NT])
            qraw, qswap = sb("qraw", [P, NT]), sb("qswap", [P, NT])
            t1, t2 = sb("t1", [P, NT]), sb("t2", [P, NT])
            kz = sb("kz", [P, NB, 2, T])
            vtok = sb("vtok", [P, 2 * NB, P])
            qr = sb("qr", [P, 2, NT])
            probs = sb("probs", [P, 2, 768])
            stats = sb("stats", [P, 2, 16])
            probT = sb("probT", [P, 2, 2, 384])
            oT = sb("oT", [P, L0_GROUP, NT])
            cols = sb("cols", [P, 10])
            ps_s = st.enter_context(nc.psum_tensor("ps_s", [P, 2, 1024], F32))
            ps_t = st.enter_context(nc.psum_tensor("ps_t", [P, 2, 512], F32))
            ps_p = st.enter_context(nc.psum_tensor("ps_p", [P, HALF], F32))
            ps_o = st.enter_context(nc.psum_tensor("ps_o", [P, HALF], F32))
            names = ("w_kvq w_wo ld_rope proj_done proj_evac s_ready max_ready exp_done "
                     "recip_ready norm_done pt_ready pt_dve pt_act o_ready o_evac wo_done wo_added rope_done "
                     "t1_ready swap_k swap_q cols_ready zeroed").split()
            s = {n: sem("A_" + n) for n in names}
            block = st.enter_context(nc.Block())

            def proj_bank(g):
                return ps_o if g < 6 and g % 2 else ps_p

            tail = lambda x, n: x[:, :].rearrange("p (b t) -> p b t", b=n)
            cosb = rope[:, 0:1, :].to_broadcast([P, NB, T])
            sinb = rope[:, 1:2, :].to_broadcast([P, NB, T])

            def scores(u):
                return (ps_s[:, u % 2, 0:512].rearrange("p (r t) -> p r t", r=2),
                        ps_s[:, u % 2, 512:768].rearrange("p (r t) -> p r t", r=2))

            def prob(u):
                return (probs[:, u % 2, 0:512].rearrange("p (r t) -> p r t", r=2),
                        probs[:, u % 2, 512:768].rearrange("p (r t) -> p r t", r=2))

            @block.sync
            def _(sp):
                sp.dma_start(rope[:, :, :], io["rope"]).then_inc(s["ld_rope"], 16)
                sp.dma_start(mask[:, :], io["mask"]).then_inc(s["ld_rope"], 16)
                with sp.Fori(0, L0_PAIRS) as c:
                    sp.wait_ge(s["proj_done"], NPROJ * c + 1)
                    sp.dma_start(wkvq[:, :], io["w_l0a"][c][:, 0:1536]).then_inc(s["w_kvq"], 16)
                    sp.wait_ge(s["wo_done"], 4 * c + 1)
                    sp.dma_start(wo[:, :, :].rearrange("p m n -> p (m n)"),
                                 io["w_l0a"][c][:, 1536:2560]).then_inc(s["w_wo"], 16)
                    for j in range(1 + L0_GROUP):
                        raw, swap, done = (kraw, kswap, "swap_k") if j == 0 else (qraw, qswap, "swap_q")
                        g = 2 if j == 0 else 4 + 2 * j
                        sp.wait_ge(s["proj_evac"], NPROJ * c + g)
                        for q in range(4):
                            sp.dma_start(swap[32 * q:32 * q + 32, :], raw[32 * (q ^ 1):32 * (q ^ 1) + 32, :]) \
                                .then_inc(s[done], 16)

            @block.gpsimd
            def _(pool):
                pool.memset(kz[:, :, :, :], 0.0).then_inc(s["zeroed"], 1)
                with pool.Fori(0, L0_PAIRS) as c:
                    pstep.enter(c, 2 * PIECE_POOL_STEPS + NU)

                    def rope_cos(j):
                        raw, g = (kraw, 2) if j == 0 else (qraw, 4 + 2 * j)
                        pool.wait_ge(s["proj_evac"], NPROJ * c + g)
                        pool.wait_ge(s["rope_done"], 5 * c + j + 1)
                        pool.tensor_tensor(tail(t1, NB), tail(raw, NB), cosb, ALU.mult).then_inc(s["t1_ready"], 1)

                    pool.wait_ge(s["ld_rope"], 32)
                    rope_cos(0)
                    rope_cos(1)
                    for u in range(NU):
                        pool.wait_ge(s["recip_ready"], NU * c + u + 1)
                        p1, p0 = prob(u)
                        rs = stats[:, u % 2, 12:16]
                        pstep.mark(pool.tensor_tensor(p1, p1, rs[:, 0:2].unsqueeze(2).to_broadcast([P, 2, T]), ALU.mult))
                        pool.tensor_tensor(p0, p0, rs[:, 2:4].unsqueeze(2).to_broadcast([P, 2, P]),
                                           ALU.mult).then_inc(s["norm_done"], 1)
                        if u in (5, 9):
                            piece_pool(pool, l + 1, 2 * c + u // 9, u // 9)
                        if u % NB == 2 and u < NU - NB:
                            rope_cos(2 + u // NB)
                pstep.leave(L0_PAIRS)

            @block.scalar
            def _(act):
                act.sem_inc(s["exp_done"], 2)
                act.sem_inc(s["pt_act"], 1)
                act.sem_inc(s["o_evac"], 2)
                condition_act(act, sig)
                with act.Fori(0, L0_PAIRS) as c:
                    def evac(g, out, **k):
                        act.wait_ge(s["proj_done"], NPROJ * c + g + 2)
                        act.activation(out, proj_bank(g)[:, :], ACT.Identity, **k).then_inc(s["proj_evac"], 1)

                    def evac_q(m, h):
                        if h == 0:
                            act.wait_ge(s["rope_done"], 5 * c + (1 if m == 0 else m + 2))
                            if m:
                                act.wait_ge(s["swap_q"], 64 * (4 * c + m))
                        evac(4 + 2 * m + h, qraw[:, h * HALF:(h + 1) * HALF], scale=cols[:, 2 + m:3 + m],
                             bias=cols[:, 6 + m:7 + m])

                    def exps(u):
                        act.wait_ge(s["max_ready"], NU * c + u + 1)
                        act.wait_ge(s["pt_ready"], NU * c + u + 1)
                        for i in range(4):
                            src, dst = scores(u)[i // 2], prob(u)[i // 2]
                            ins = act.activation(dst[:, i % 2, :], src[:, i % 2, :], ACT.Exp,
                                                 bias=stats[:, u % 2, 4 + i:5 + i],
                                                 accum_out=stats[:, u % 2, 8 + i:9 + i])
                        ins.then_inc(s["exp_done"], 1)

                    def pt_evac(u):
                        act.wait_ge(s["pt_ready"], NU * c + u + 3)
                        act.wait_ge(s["o_ready"], NU * c + u + 1)
                        act.activation(probT[:, u % 2, 1, :], ps_t[:, 1, 0:384], ACT.Identity) \
                            .then_inc(s["pt_act"], 1)

                    def o_evac(u):
                        act.wait_ge(s["o_ready"], NU * c + u + 3)
                        if u == 0:
                            act.wait_ge(s["wo_done"], 4 * c + 1)
                        act.activation(oT[:, u // NB, ds(u % NB * T, T)], ps_o[:, 0:T], ACT.Identity,
                                       bias=cols[:, 1:2]).then_inc(s["o_evac"], 1)

                    act.wait_ge(s["cols_ready"], c + 1)
                    act.wait_ge(s["rope_done"], 5 * c + 1)
                    for h in range(2):
                        evac(h, kraw[:, h * HALF:(h + 1) * HALF], bias=cols[:, 0:1])
                    act.wait_ge(s["o_ready"], NU * c + 2)
                    for h in range(2):
                        evac(2 + h, vtok[:, NB * h:NB * h + NB, :].rearrange("p a f -> p (a f)"))
                    for h in range(2):
                        evac_q(0, h)
                    for k in range(2):
                        piece_act(act, l + 1, 2 * c + k, k)
                    for u in range(NU):
                        exps(u)
                        if u % NB < 2 and u < NU - NB:
                            evac_q(u // NB + 1, u % NB)
                        if u >= 1:
                            pt_evac(u - 1)
                        if u >= 2:
                            o_evac(u - 2)
                    pt_evac(NU - 1)
                    o_evac(NU - 2)
                    o_evac(NU - 1)

            @block.vector
            def _(dve):
                dve.sem_inc(s["rope_done"], 1)
                dve.sem_inc(s["pt_dve"], 1)
                dve.sem_inc(s["wo_added"], 1)
                condition_dve(dve, l, sig)
                for ch in range(CH):
                    dstep.link(dve.tensor_scalar(xT[:, ch, :], xT[:, ch, :], vec("bo0", ch), None, ALU.add))
                dve.wait_ge(s["ld_rope"], 32)
                dve.wait_ge(s["zeroed"], 1)
                per = 2 * PIECE_DVE_STEPS + 2 + L0_GROUP + 2 * NU
                with dve.Fori(0, L0_PAIRS) as c:
                    dstep.enter(c, per)

                    def rope_sum(j):
                        swap, done, n = (kswap, "swap_k", c + 1) if j == 0 else (qswap, "swap_q", 4 * c + j)
                        dve.wait_ge(s["rope_done"], 5 * c + j + 1)
                        dve.wait_ge(s[done], 64 * n)
                        dstep.link(dve.tensor_tensor(tail(t2, NB), tail(swap, NB), sinb, ALU.mult))
                        dve.wait_ge(s["t1_ready"], 5 * c + j + 1)
                        if j == 0:
                            dve.wait_ge(s["s_ready"], NU * c + 5)
                            for r in range(2):
                                h = slice(64 * r, 64 * r + 64)
                                ins = dve.tensor_tensor(kz[h, :, r, :], t1[h, :].rearrange("p (b t) -> p b t", b=NB),
                                                        t2[h, :].rearrange("p (b t) -> p b t", b=NB), ALU.add)
                        else:
                            dve.wait_ge(s["s_ready"], NU * c + NB * (j - 1) + 1)
                            ins = dve.tensor_tensor(qr[:, (j - 1) % 2, :], t1[:, :], t2[:, :], ALU.add)
                        ins.then_inc(s["rope_done"], 1)

                    def max_rows(u):
                        dve.wait_ge(s["s_ready"], NU * c + u + 6)
                        s1, s0 = scores(u)
                        mb = mask[:, :].unsqueeze(1).to_broadcast([P, 2, P])
                        dve.tensor_tensor(s1[:, :, P:T], s1[:, :, P:T], mb, ALU.add)
                        dstep.link(dve.tensor_tensor(s0, s0, mb, ALU.add))
                        dve.tensor_reduce(stats[:, u % 2, 0:2], s1, AX_X, ALU.max)
                        dstep.link(dve.tensor_reduce(stats[:, u % 2, 2:4], s0, AX_X, ALU.max))
                        dve.tensor_scalar(stats[:, u % 2, 4:8], stats[:, u % 2, 0:4], -1.0, None,
                                          ALU.mult).then_inc(s["max_ready"], 1)

                    def recip(u):
                        dve.wait_ge(s["exp_done"], NU * c + u + 3)
                        dve.reciprocal(stats[:, u % 2, 12:16], stats[:, u % 2, 8:12]).then_inc(s["recip_ready"], 1)

                    def pt_evac(u):
                        dve.wait_ge(s["pt_ready"], NU * c + u + 3)
                        dve.wait_ge(s["o_ready"], NU * c + u + 1)
                        dve.tensor_copy(probT[:, u % 2, 0, :], ps_t[:, 0, 0:384]).then_inc(s["pt_dve"], 1)

                    dve.wait_ge(s["o_evac"], NU * c + 2)
                    dve.tensor_scalar(cols[:, 0:2], vecs[:, VEC["bk"][0]:VEC["bk"][0] + 8]
                                      .rearrange("p (a c) -> p a c", a=2)[:, :, ds(c, 1)].rearrange("p a c -> p (a c)"),
                                      1.0, None, ALU.mult)
                    four = lambda n: vecs[:, ds(4 * c + VEC[n][0], 4)]
                    dstep.link(dve.tensor_scalar(cols[:, 2:6], four("kw"), HD ** -0.5, None, ALU.mult))
                    dve.tensor_tensor(cols[:, 6:10], cols[:, 2:6], four("bq"), ALU.mult).then_inc(s["cols_ready"], 1)
                    for k in range(2):
                        piece_scans(dve, l + 1, 2 * c + k, k)
                    rope_sum(0)
                    rope_sum(1)
                    for u in range(NU):
                        max_rows(u)
                        if u >= 1:
                            recip(u - 1)
                            pt_evac(u - 1)
                        if u % NB == 3 and u < NU - NB:
                            rope_sum(2 + u // NB)
                        if u in (11, 13):
                            piece_finish(dve, l + 1, 2 * c + u // 13, u // 13)
                    recip(NU - 1)
                    pt_evac(NU - 1)
                    for j in range(4):
                        dve.wait_ge(s["wo_done"], 4 * c + j + 2)
                        half, ch = j % 2, j // 2
                        x = xT[:, ch, half * HALF:(half + 1) * HALF]
                        dve.tensor_tensor(x, x, ps_p[:, :], ALU.add).then_inc(s["wo_added"], 1)
                dstep.leave(L0_PAIRS)

            @block.tensor
            def _(pe):
                pe.sem_inc(s["proj_done"], 1)
                pe.sem_inc(s["s_ready"], 5)
                pe.sem_inc(s["pt_ready"], 2)
                pe.sem_inc(s["o_ready"], 2)
                pe.sem_inc(s["wo_done"], 1)
                pe.wait_ge(xin_ready, l + 1)
                with pe.Fori(0, L0_PAIRS) as c:
                    def bank_free(g):
                        if g == 0:
                            pe.wait_ge(s["wo_added"], 4 * c + 1)
                        elif g == 1:
                            pe.wait_ge(s["o_evac"], NU * c + 2)
                        else:
                            pe.wait_ge(s["proj_evac"], NPROJ * c + (g - 1 if g <= 6 else g))

                    def project(g, w, h):
                        bank_free(g)
                        for k in range(CH):
                            ins = pe.matmul(proj_bank(g)[:, :], w[:, k, :], xin[:, k, h * HALF:(h + 1) * HALF],
                                            start=(k == 0), stop=(k == CH - 1))
                        ins.then_inc(s["proj_done"], 1)

                    def score(u):
                        m, b = divmod(u, NB)
                        if b == 0:
                            pe.wait_ge(s["rope_done"], 5 * c + m + 3)
                        pe.wait_ge(s["exp_done"], NU * c + u + 1)
                        for tile, view in zip((1, 0), scores(u)):
                            n = T if tile else P
                            ins = pe.matmul(view, qr[:, m % 2, b * T + tile * P:b * T + tile * P + P],
                                            kz[:, b, :, 0:n], start=True, stop=True)
                        ins.then_inc(s["s_ready"], 1)

                    def turn(u):
                        pe.wait_ge(s["norm_done"], NU * c + u + 1)
                        pe.wait_ge(s["pt_dve"], NU * c + u + 1)
                        pe.wait_ge(s["pt_act"], NU * c + u + 1)
                        p1, p0 = prob(u)
                        for r in range(2):
                            pe.transpose(ps_t[:, r, 0:128], p0[:, r, :], ident[:, :])
                            pe.transpose(ps_t[:, r, 128:256], p1[:, r, 0:128], ident[:, :])
                            ins = pe.transpose(ps_t[:, r, 256:384], p1[:, r, 128:256], ident[:, :])
                        ins.then_inc(s["pt_ready"], 1)

                    def weigh(u):
                        b = u % NB
                        pe.wait_ge(s["pt_dve"], NU * c + u + 2)
                        pe.wait_ge(s["pt_act"], NU * c + u + 2)
                        pe.wait_ge(s["o_evac"], NU * c + u + 2)
                        for key in range(2):
                            for r in range(2):
                                o = ps_o[64 * r:64 * r + 64, key * P:T]
                                ins = pe.matmul(o, vtok[:, 2 * b + key, 64 * r:64 * r + 64],
                                                probT[:, u % 2, r, 0:256] if key == 0 else probT[:, u % 2, r, 256:384],
                                                start=(key == 0), stop=(key == 1), skip_group_check=True)
                        ins.then_inc(s["o_ready"], 1)

                    pe.wait_ge(s["w_kvq"], 16 * c + 16)
                    for h in range(2):
                        project(h, wk, h)
                    for h in range(2):
                        bank_free(2 + h)
                        for t in range(NB):
                            for k in range(CH):
                                ins = pe.matmul(proj_bank(2 + h)[:, t * P:(t + 1) * P],
                                                xin[:, k, h * HALF + t * P:h * HALF + t * P + P], wv[:, k, :],
                                                start=(k == 0), stop=(k == CH - 1))
                        ins.then_inc(s["proj_done"], 1)
                    for h in range(2):
                        project(4 + h, wq[:, 0], h)
                    for u in range(NU):
                        score(u)
                        if u % NB < 2 and u < NU - NB:
                            m, h = u // NB + 1, u % NB
                            project(4 + 2 * m + h, wq[:, m], h)
                        if u >= 1:
                            turn(u - 1)
                        if u >= 2:
                            weigh(u - 2)
                    turn(NU - 1)
                    weigh(NU - 2)
                    weigh(NU - 1)
                    pe.wait_ge(s["w_wo"], 16 * c + 16)
                    pe.wait_ge(s["o_evac"], NU * c + NU + 2)
                    pe.wait_ge(s["proj_evac"], NPROJ * c + NPROJ)
                    for j in range(4):
                        half, ch = j % 2, j // 2
                        if j:
                            pe.wait_ge(s["wo_added"], 4 * c + j + 1)
                        for m in range(L0_GROUP):
                            ins = pe.matmul(ps_p[:, :], wo[:, m, ch * P:(ch + 1) * P], oT[:, m, half * HALF:(half + 1) * HALF],
                                            start=(m == 0), stop=(m == L0_GROUP - 1))
                        ins.then_inc(s["wo_done"], 1)


    def route_act(act, lt, n):
        act.wait_ge(sub_ready, n)
        act.activation(lt[:, 1, :, :], lt[:, 1, :, :], ACT.Exp).then_inc(exp_ready, 1)

    def route_dve(dve, lt, one, rank, n):
        bc = lambda v: v.unsqueeze(2).to_broadcast([P, 8, NE])
        dstep.link(dve.tensor_reduce(one[:, 2, :], lt[:, 0, :, :], AX_X, ALU.max))
        dve.tensor_tensor(lt[:, 1, :, :], lt[:, 0, :, :], bc(one[:, 2, :]), ALU.subtract).then_inc(sub_ready, 1)
        dve.wait_ge(exp_ready, n)
        dstep.link(dve.tensor_reduce(one[:, 3, :], lt[:, 1, :, :], AX_X, ALU.add))
        dstep.link(dve.reciprocal(one[:, 3, :], one[:, 3, :]))
        dstep.link(dve.tensor_tensor(lt[:, 1, :, :], lt[:, 1, :, :], bc(one[:, 3, :]), ALU.mult))
        for k in range(2):
            p, hot = lt[:, 1, :, :], lt[:, 2 + k, :, :]
            dstep.link(dve.tensor_reduce(one[:, k, :], p, AX_X, ALU.max))
            dstep.link(dve.tensor_tensor(hot, p, bc(one[:, k, :]), ALU.is_equal))
            dstep.link(dve.tensor_tensor(hot, hot, rank, ALU.mult))
            dstep.link(dve.tensor_reduce(one[:, 2, :], hot, AX_X, ALU.max))
            dstep.link(dve.tensor_tensor(hot, hot, bc(one[:, 2, :]), ALU.is_equal))
            if k == 0:
                dstep.link(dve.scalar_tensor_tensor(out=p, in0=hot, scalar=-2.0, in1=p, op0=ALU.mult, op1=ALU.add))

    NROW = 4
    moe_sems = {n: sem("moe_" + n) for n in
                ("ld_gate router_done shared_ready comb_ready combT_ps "
                 "combT_ready comb_stored gu_done silu_done prod_ready hid_ready down_done w0 w1 "
                 "y_act").split() + [f"rows{g}" for g in range(NROW)]}
    moe_left = {n: 0 for n in moe_sems}

    def stage_moe(l, name):
        NF = NE * EH + (L0_SH if name == "L0" else L3_SH)
        NCH = -(-NF // P)
        with ExitStack() as st:
            def sb(n, shape, dt=F32):
                return st.enter_context(nc.sbuf_tensor(name + n, shape, dt))

            sig = sb("sig", [P, CH, NT])
            wgate = sb("wgate", [P, CH, NE + 1])
            w = sb("w", [P, 2, 768])
            rank = sb("rank", [P, 8, NE])
            lt = sb("lt", [P, 4, 8, NE])
            one = sb("one", [P, 6, 8])
            comb = sb("comb", [P, 8, NE + 1])
            combT = sb("combT", [NE + 1, NT])
            rowsb = sb("rows", [P, NCH, NT])
            act_g = sb("actg", [P, 2, HALF])
            prod = sb("prod", [P, 2, HALF])
            hid = sb("hid", [P, 2, 2, HALF])
            comb_dram = nc.dram_tensor(name + "_comb_scratch", (NE + 1, NT), F32, kind="Internal").ap()
            ps_y = st.enter_context(nc.psum_tensor(name + "ps_y", [P, CH, 2, HALF], F32))
            ps_g = st.enter_context(nc.psum_tensor(name + "ps_g", [P, 2, HALF], F32))
            ps_u = st.enter_context(nc.psum_tensor(name + "ps_u", [P, 2, HALF], F32))
            block = st.enter_context(nc.Block())

            s = moe_sems

            def at(n, count):
                return s[n], moe_left[n] + count

            def row_group(ch):
                return min(ch * NROW // NCH, NROW - 1)

            row_parts = []
            for ch in range(NCH):
                f = ch * P
                while f < (ch + 1) * P:
                    e = min(f // EH, NE)
                    end = (ch + 1) * P if e == NE else min((e + 1) * EH, (ch + 1) * P)
                    row_parts.append((ch, f - ch * P, end - ch * P, e))
                    f = end

            def pairs(eng, body):
                with eng.Fori(0, NCH // 2) as p:
                    body(2 * p, 0)
                    body(2 * p + 1, 1)
                if NCH % 2:
                    body(NCH - 1, 0)

            @block.sync
            def _(sp):
                sp.dma_start(wgate[:, :, :], io[name + "_gate"]).then_inc(s["ld_gate"], 16)
                sp.dma_start(rank[:, :, :], io["rank"]).then_inc(s["ld_gate"], 16)

                def load(ch, k):
                    sp.wait_ge(*at("down_done", ch + 1))
                    sp.dma_start(w[:, k, :], io[name + "_w"][ch]).then_inc(s[f"w{k}"], 16)

                pairs(sp, load)

            @block.gpsimd
            def _(pool):
                block_pool(pool, l + 1) if l + 1 < NL else None

                def gate(ch, k, first=False):
                    for h in range(2):
                        pool.wait_ge(*at("prod_ready", 2 * ch + h + 3))
                        pool.wait_ge(*at("down_done", ch + 1))
                        pool.tensor_tensor(hid[:, k, h, :], prod[:, h, :], rowsb[:, ds(ch, 1), h * HALF:(h + 1) * HALF]
                                           .rearrange("p a t -> p (a t)"), ALU.mult).then_inc(s["hid_ready"], 1)

                pool.sem_inc(s["hid_ready"], 2)
                for g in range(NROW):
                    pool.wait_ge(*at(f"rows{g}", 16 * sum(row_group(r[0]) == g for r in row_parts)))
                pairs(pool, gate)

            @block.scalar
            def _(act):
                condition_act(act, sig)
                route_act(act, lt, l // 6 * 2 + 1)
                act.wait_ge(*at("router_done", 1))
                act.activation(comb[:, :, NE:NE + 1], ps_g[:, 0, 0:8 * (NE + 1)].rearrange("p (t e) -> p t e", t=8)[:, :, NE:NE + 1],
                               ACT.Sigmoid).then_inc(s["shared_ready"], 1)
                act.wait_ge(*at("combT_ps", 1))
                for i in range(2):
                    ins = act.activation(combT[:, i * HALF:(i + 1) * HALF], ps_u[0:NE + 1, i, :], ACT.Identity)
                ins.then_inc(s["combT_ready"], 1)
                act.wait_ge(*at("combT_ready", 1))
                act.dma_start(comb_dram, combT[:, :]).then_inc(s["comb_stored"], 16)
                act.wait_ge(*at("comb_stored", 16))
                for ch, a, b, e in row_parts:
                    act.dma_start(rowsb[a:b, ch, :], comb_dram[e:e + 1, :].to_broadcast([b - a, NT])) \
                        .then_inc(s[f"rows{row_group(ch)}"], 16)
                if l + 1 < NL:
                    block_act(act, l + 1)

                def silu(ch, k):
                    for h in range(2):
                        act.wait_ge(*at("gu_done", 2 * ch + h + 1))
                        act.wait_ge(*at("prod_ready", 2 * ch + h + 1))
                        act.activation(act_g[:, h, :], ps_g[:, h, :], ACT.Silu).then_inc(s["silu_done"], 1)

                pairs(act, silu)
                act.wait_ge(*at("down_done", NCH + 2))
                act.activation(xT[:, 0, :], ps_y[:, 0, :, :].rearrange("p a t -> p (a t)"), ACT.Identity) \
                    .then_inc(s["y_act"], 1)
                act.wait_ge(*at("y_act", 1))

            @block.vector
            def _(dve):
                dve.sem_inc(s["prod_ready"], 2)
                condition_dve(dve, l, sig)
                dve.wait_ge(*at("router_done", 1))
                dve.wait_ge(*at("ld_gate", 32))
                logits = ps_g[:, 0, 0:8 * (NE + 1)].rearrange("p (t e) -> p t e", t=8)
                dstep.link(dve.tensor_copy(lt[:, 0, :, :], logits[:, :, 0:NE]))
                route_dve(dve, lt, one, rank[:, :, :], l // 6 * 2 + 1)
                bc = lambda v: v.unsqueeze(2).to_broadcast([P, 8, NE])
                dstep.link(dve.tensor_tensor(one[:, 2, :], one[:, 0, :], one[:, 1, :], ALU.add))
                dstep.link(dve.reciprocal(one[:, 2, :], one[:, 2, :]))
                for k in range(2):
                    dstep.link(dve.tensor_tensor(one[:, 4 + k, :], one[:, k, :], one[:, 2, :], ALU.mult))
                    dstep.link(dve.tensor_tensor(lt[:, 2 + k, :, :], lt[:, 2 + k, :, :], bc(one[:, 4 + k, :]), ALU.mult))
                dve.tensor_tensor(comb[:, :, 0:NE], lt[:, 2, :, :], lt[:, 3, :, :], ALU.add).then_inc(s["comb_ready"], 1)
                if l + 1 < NL:
                    block_dve(dve, l + 1)

                def multiply(ch, k):
                    for h in range(2):
                        dve.wait_ge(*at("silu_done", 2 * ch + h + 1))
                        dve.wait_ge(*at("hid_ready", 2 * ch + h + 1))
                        dve.tensor_tensor(prod[:, h, :], act_g[:, h, :], ps_u[:, h, :], ALU.mult) \
                            .then_inc(s["prod_ready"], 1)

                pairs(dve, multiply)
                dve.wait_ge(*at("down_done", NCH + 2))
                dstep.link(dve.tensor_copy(xT[:, 1, :], ps_y[:, 1, :, :].rearrange("p a t -> p (a t)")))

            @block.tensor
            def _(pe):
                pe.sem_inc(s["down_done"], 2)
                pe.wait_ge(*at("ld_gate", 32))
                pe.wait_ge(xin_ready, l + 1)
                for t in range(8):
                    for k in range(CH):
                        ins = pe.matmul(ps_g[:, 0, t * (NE + 1):(t + 1) * (NE + 1)], xin[:, k, t * P:(t + 1) * P],
                                        wgate[:, k, :], start=(k == 0), stop=(k == CH - 1))
                ins.then_inc(s["router_done"], 1)
                for ch in range(CH):
                    for h in range(2):
                        pe.matmul(ps_y[:, ch, h, :], ident[:, :], xT[:, ch, h * HALF:(h + 1) * HALF],
                                  start=True, stop=False)
                pe.wait_ge(*at("comb_ready", 1))
                pe.wait_ge(*at("shared_ready", 1))
                for t in range(8):
                    ins = pe.transpose(ps_u[0:NE + 1, t // 4, t % 4 * P:t % 4 * P + P], comb[:, t, :], ident[:, :])
                ins.then_inc(s["combT_ps"], 1)
                pe.wait_ge(*at("combT_ready", 1))

                def gate_up(ch, k, n):
                    pe.wait_ge(*at(f"w{k}", 16 * n + 16))
                    for h in range(2):
                        pe.wait_ge(*at("prod_ready", 2 * ch + h + 1))
                        for ps, o in ((ps_g, 0), (ps_u, 256)):
                            for i in range(CH):
                                ins = pe.matmul(ps[:, h, :], w[:, k, o + i * P:o + (i + 1) * P],
                                                xin[:, i, h * HALF:(h + 1) * HALF], start=(i == 0), stop=(i == CH - 1))
                        ins.then_inc(s["gu_done"], 1)

                def down(ch, k, last=False):
                    for h in range(2):
                        pe.wait_ge(*at("hid_ready", 2 * ch + h + 3))
                        for m in range(CH):
                            ins = pe.matmul(ps_y[:, m, h, :], w[:, k, 512 + m * P:512 + (m + 1) * P], hid[:, k, h, :],
                                            start=False, stop=last)
                    ins.then_inc(s["down_done"], 1)

                gate_up(0, 0, 0)
                with pe.Fori(0, (NCH - 1) // 2) as p:
                    gate_up(2 * p + 1, 1, p)
                    down(2 * p, 0)
                    gate_up(2 * p + 2, 0, p + 1)
                    down(2 * p + 1, 1)
                if NCH % 2 == 0:
                    gate_up(NCH - 1, 1, NCH // 2 - 1)
                    down(NCH - 2, 0)
                    down(NCH - 1, 1, True)
                else:
                    down(NCH - 1, 0, True)

            once = ("router_done shared_ready comb_ready combT_ps "
                    "combT_ready y_act").split()
            left = {n: 1 for n in once}
            left.update(ld_gate=32, comb_stored=16, gu_done=2 * NCH, silu_done=2 * NCH, prod_ready=2 * NCH + 2,
                        hid_ready=2 * NCH + 2, down_done=NCH + 2, w0=16 * ((NCH + 1) // 2), w1=16 * (NCH // 2))
            for g in range(NROW):
                left[f"rows{g}"] = 16 * sum(row_group(r[0]) == g for r in row_parts)
            for n in moe_left:
                moe_left[n] += left[n]


    def stage_l1_attn(l):
        TP = T + 6
        RC = 3
        rows = (P, P, R1 - 2 * P)
        with ExitStack() as st:
            def sb(n, shape, dt=F32):
                return st.enter_context(nc.sbuf_tensor("R_" + n, shape, dt))

            sig = sb("sig", [P, CH, NT])
            w1 = sb("w1", [P, CH, RC * P])
            wconv = sb("wconv", [P, 10, R1])
            wgate = sb("wgate", [P, 2, RC, R1])
            w2 = sb("w2", [P, RC, C])
            hid = sb("hid", [P, CH, NB, TP])
            hid2 = sb("hid2", [P, NB, TP])
            conv = sb("conv", [P, RC, NT])
            rec = sb("rec", [P, RC, NT])
            inp = sb("inp", [P, RC, NT])
            mul = sb("mul", [P, RC, NT])
            lam = sb("lam", [P, 6, RC])
            ps = st.enter_context(nc.psum_tensor("R_ps", [P, 8, HALF], F32))
            names = ("ld_w1 ld_conv ld_gate ld_w2 zeroed done evac lam_ln "
                     "lam_ready a2_ready one_minus root_ready ix_ready scan_ready out_read").split()
            s = {n: sem("R_" + n) for n in names}
            block = st.enter_context(nc.Block())
            G_CONV, G_GATE, G_OUT = 6, 12, 24
            h512 = lambda h: slice(h * HALF, (h + 1) * HALF)

            @block.sync
            def _(sp):
                sp.dma_start(w1[:, :, :], io["l1_w1"]).then_inc(s["ld_w1"], 16)
                sp.dma_start(wconv[:, :, :], io["l1_conv"]).then_inc(s["ld_conv"], 16)
                sp.dma_start(wgate[:, :, :, :], io["l1_gate"]).then_inc(s["ld_gate"], 16)
                sp.dma_start(w2[:, :, :], io["l1_w2"]).then_inc(s["ld_w2"], 16)

            @block.gpsimd
            def _(pool):
                pool.memset(hid[:, :, :, :], 0.0)
                pstep.link(pool.memset(hid2[:, :, :], 0.0))
                pstep.link(pool.memset(conv[64:P, 2, :], 0.0))
                pool.memset(inp[64:P, 2, :], 0.0).then_inc(s["zeroed"], 1)
                for h in range(2):
                    pool.wait_ge(s["evac"], G_GATE + 6 * (h + 1))
                    for f in range(RC):
                        n = rows[f]
                        ins = pool.tensor_tensor(inp[0:n, f, h512(h)], inp[0:n, f, h512(h)], conv[0:n, f, h512(h)], ALU.mult)
                        if f == RC - 2:
                            pstep.link(ins)
                    ins.then_inc(s["ix_ready"], 1)
                    pool.wait_ge(s["ix_ready"], h + 1)
                block_pool(pool, l + 1)

            @block.scalar
            def _(act):
                condition_act(act, sig)
                astep.link(act.activation(lam[:, 0, :], vecs[:, VEC["lam"][0]:VEC["lam"][0] + RC], ACT.Abs))
                astep.link(act.activation(lam[:, 1, :], lam[:, 0, :], ACT.Exp, scale=-1.0))
                act.activation(lam[:, 2, :], lam[:, 1, :], ACT.Ln, bias=1.0).then_inc(s["lam_ln"], 1)
                act.wait_ge(s["zeroed"], 1)
                pair = lambda x: x.rearrange("p (b t) -> p b t", b=2)
                for h in range(2):
                    for f in range(RC):
                        g = 3 * h + f
                        act.wait_ge(s["done"], g + 1)
                        if f < 2:
                            ins = act.activation(hid[:, f, 2 * h:2 * h + 2, 3:3 + T], pair(ps[:, g, :]), ACT.Silu, bias=vec("b1", f))
                        else:
                            act.activation(hid2[0:64, 2 * h:2 * h + 2, 3:3 + T], pair(ps[0:64, g, :]), ACT.Silu,
                                           bias=vec("b1", f)[0:64, :])
                            ins = act.activation(hid2[64:P, 2 * h:2 * h + 2, 1:1 + T], pair(ps[64:P, g, :]), ACT.Silu,
                                                 bias=vec("b1", f)[64:P, :])
                        ins.then_inc(s["evac"], 1)
                for h in range(2):
                    for f in range(RC):
                        g, n = G_CONV + 3 * h + f, rows[f]
                        act.wait_ge(s["done"], g + 1)
                        act.activation(conv[0:n, f, h512(h)], ps[0:n, g % 8, :], ACT.Identity,
                                       bias=vec("convb", f)[0:n, :]).then_inc(s["evac"], 1)
                for h in range(2):
                    for f in range(RC):
                        for j, (dst, b) in enumerate(((rec, "ba"), (inp, "bx"))):
                            g, n = G_GATE + 6 * h + 2 * f + j, rows[f]
                            act.wait_ge(s["done"], g + 1)
                            act.activation(dst[0:n, f, h512(h)], ps[0:n, g % 8, :], ACT.Sigmoid,
                                           bias=vec(b, f)[0:n, :]).then_inc(s["evac"], 1)
                act.wait_ge(s["lam_ready"], 1)
                act.wait_ge(s["evac"], G_OUT)
                for h in range(2):
                    for f in range(RC):
                        n = rows[f]
                        astep.mark(act.activation(mul[0:n, f, h512(h)], rec[0:n, f, h512(h)], ACT.Exp, scale=lam[0:n, 5, f:f + 1]))
                    astep.wait()
                    for f in range(RC):
                        n = rows[f]
                        ins = act.activation(rec[0:n, f, h512(h)], rec[0:n, f, h512(h)], ACT.Exp, scale=lam[0:n, 4, f:f + 1])
                    ins.then_inc(s["a2_ready"], 1)
                for h in range(2):
                    act.wait_ge(s["one_minus"], h + 1)
                    for f in range(RC):
                        n = rows[f]
                        ins = act.activation(mul[0:n, f, h512(h)], mul[0:n, f, h512(h)], ACT.Sqrt, bias=1.0)
                    ins.then_inc(s["root_ready"], 1)
                block_act(act, l + 1)

            @block.vector
            def _(dve):
                lv = vecs[:, VEC["lam"][0]:VEC["lam"][0] + RC]
                condition_dve(dve, l, sig)
                dstep.link(dve.tensor_scalar(lam[:, 3, :], lv, 0.0, None, ALU.max))
                dve.wait_ge(s["lam_ln"], 1)
                dstep.link(dve.tensor_tensor(lam[:, 3, :], lam[:, 3, :], lam[:, 2, :], ALU.add))
                dstep.mark(dve.tensor_scalar(lam[:, 4, :], lam[:, 3, :], -8.0, None, ALU.mult))
                dve.tensor_scalar(lam[:, 5, :], lam[:, 3, :], -16.0, None, ALU.mult).then_inc(s["lam_ready"], 1)
                for h in range(2):
                    dve.wait_ge(s["a2_ready"], h + 1)
                    for f in range(RC):
                        n = rows[f]
                        ins = dve.tensor_scalar(mul[0:n, f, h512(h)], mul[0:n, f, h512(h)], 1.0, -1.0, ALU.min, ALU.mult)
                    ins.then_inc(s["one_minus"], 1)
                for h in range(2):
                    dve.wait_ge(s["root_ready"], h + 1)
                    dve.wait_ge(s["ix_ready"], h + 1)
                    for f in range(RC):
                        n = rows[f]
                        dstep.link(dve.tensor_tensor(mul[0:n, f, h512(h)], mul[0:n, f, h512(h)], inp[0:n, f, h512(h)], ALU.mult))
                    for f in range(RC):
                        n = rows[f]
                        for b in (2 * h, 2 * h + 1):
                            c = slice(b * T, (b + 1) * T)
                            ins = dve.tensor_tensor_scan(inp[0:n, f, c], rec[0:n, f, c], mul[0:n, f, c], 0.0, ALU.mult, ALU.add)
                    ins.then_inc(s["scan_ready"], 1)
                for h in range(2):
                    for m in range(CH):
                        dve.wait_ge(s["done"], G_OUT + 2 * h + m + 1)
                        x = xT[:, m, h512(h)]
                        dstep.link(dve.scalar_tensor_tensor(out=x, in0=ps[:, (G_OUT + 2 * h + m) % 8, :], scalar=vec("b2", m),
                                                            in1=x, op0=ALU.add, op1=ALU.add))
                block_dve(dve, l + 1)

            @block.tensor
            def _(pe):
                group = [0]

                def product(pairs, n):
                    g = group[0]
                    group[0] += 1
                    if g >= 8:
                        pe.wait_ge(s["evac"], g - 7)
                    for i, (w, x) in enumerate(pairs):
                        ins = pe.matmul(ps[0:n, g % 8, :], w, x, start=(i == 0), stop=(i == len(pairs) - 1))
                    ins.then_inc(s["done"], 1)

                pe.wait_ge(s["ld_w1"], 16)
                pe.wait_ge(xin_ready, l + 1)
                for h in range(2):
                    for f in range(RC):
                        product([(w1[:, k, f * P:(f + 1) * P], xin[:, k, h512(h)]) for k in range(CH)], P)
                pe.wait_ge(s["ld_conv"], 16)
                for h in range(2):
                    pe.wait_ge(s["evac"], 3 * (h + 1))
                    b = slice(2 * h, 2 * h + 2)
                    for f in range(RC):
                        c = slice(f * P, f * P + rows[f])
                        product([(wconv[:, 2 * k + i, c], hid[:, i, b, 2 * k:2 * k + T]) for k in range(TAPS) for i in range(CH)]
                                + [(wconv[:, 8 + q, c], hid2[:, b, 4 * q:4 * q + T]) for q in range(2)], rows[f])
                pe.wait_ge(s["ld_gate"], 16)
                for h in range(2):
                    pe.wait_ge(s["evac"], G_CONV + 3 * (h + 1))
                    for f in range(RC):
                        c = slice(f * P, f * P + rows[f])
                        for j in range(2):
                            product([(wgate[:, j, k, c], conv[:, k, h512(h)]) for k in range(RC)], rows[f])
                pe.wait_ge(s["ld_w2"], 16)
                for h in range(2):
                    pe.wait_ge(s["scan_ready"], h + 1)
                    for m in range(CH):
                        product([(w2[:, k, m * P:(m + 1) * P], inp[:, k, h512(h)]) for k in range(RC)], P)


    def stage_l1_ffn(l):
        HC = FF // P
        with ExitStack() as st:
            def sb(n, shape, dt=F32):
                return st.enter_context(nc.sbuf_tensor("E_" + n, shape, dt))

            tok = sb("tok", [P, 8, C])
            sig = tok[:, :, :].rearrange("p a b -> p (a b)").rearrange("p (c t) -> p c t", c=CH)
            wgate = sb("wgate", [P, CH, NE])
            rank = sb("rank", [P, 8, NE])
            base = sb("base", [NE, 4])
            lt = sb("lt", [P, 4, 8, NE])
            one = sb("one", [P, 4, 8])
            gates = sb("gates", [P, 16])
            slotf = sb("slotf", [P, 3, 16])
            sloti = sb("sloti", [P, 2, 16], U32)
            fc1 = sb("fc1", [P, 2, CH, FF])
            fc2 = sb("fc2", [P, 2, HC, C])
            fc2b = sb("fc2b", [P, NE, C])
            rows = sb("rows", [P, 16, C])
            dT = sb("dT", [P, CH, SLOTS])
            hid = sb("hid", [P, 2, HC, CAP])
            fc1b = sb("fc1b", [P, 2, HC])
            eo = sb("eo", [P, 2, 2, C])
            flat = rows[:, :, :].rearrange("p a b -> p (a b)")
            picks, count = flat[0:NE, 0:SLOTS], flat[0:NE, SLOTS:2 * SLOTS]
            fits, pos = dT[0:NE, 0, :], dT[0:NE, 1, :]
            ps = st.enter_context(nc.psum_tensor("E_ps", [P, 8, HALF], F32))
            names = ("ld_gate ld_fc2b fc1_0 fc1_1 fc2_0 fc2_1 router_done "
                     "x_turned tok_ready hot_ready hot_turned picks_ready slots_ready slots_ps sidx_ready scattered "
                     "rows_loaded rows_turned dT_act dT_dve fc1_done gelu_done fc2_done eo_ready eo_st0 eo_st1 "
                     "gathered bias_ready y_ready y_turned").split()
            s = {n: sem("E_" + n) for n in names}
            block = st.enter_context(nc.Block())

            def experts(eng, body):
                with eng.Fori(0, NE // 2) as j:
                    body(2 * j, 0, j)
                    body(2 * j + 1, 1, j)

            @block.sync
            def _(sp):
                sp.dma_start(wgate[:, :, :], io["l1_wg"]).then_inc(s["ld_gate"], 16)
                sp.dma_start(rank[:, :, :], io["rank"]).then_inc(s["ld_gate"], 16)
                sp.dma_start(base[:, :], io["base"]).then_inc(s["ld_gate"], 16)
                sp.dma_start(fc2b[:, :, :].rearrange("p e d -> p (e d)"), io["l1_fc2b"].to_broadcast([P, NE * C])) \
                    .then_inc(s["ld_fc2b"], 16)

                def load(e, k):
                    sp.wait_ge(s["fc1_done"], HC // 2 * (e + 1))
                    sp.dma_start(fc1[:, k, :, :].rearrange("p a f -> p (a f)"), io["l1_fc1"][e]).then_inc(s[f"fc1_{k}"], 16)
                    sp.wait_ge(s["fc2_done"], e + 1)
                    sp.dma_start(fc2[:, k, :, :].rearrange("p a f -> p (a f)"), io["l1_fc2"][e]).then_inc(s[f"fc2_{k}"], 16)

                def store(e, k):
                    sp.wait_ge(s["eo_ready"], e + 3)
                    sp.dma_start(eo_dram[ds(e * CAP, CAP), :].rearrange("(a p) d -> p a d", p=P), eo[:, k, :, :]) \
                        .then_inc(s[f"eo_st{k}"], 16)

                for k in range(2):
                    sp.sem_inc(s[f"eo_st{k}"], 16)
                load(0, 0)
                load(1, 1)
                with sp.Fori(1, NE // 2) as j:
                    for k in range(2):
                        load(2 * j + k, k)
                        store(2 * j + k - 2, k)
                for k in range(2):
                    store(NE - 2 + k, k)

            @block.gpsimd
            def _(pool):
                pool.wait_ge(s["tok_ready"], 1)
                pool.wait_ge(s["sidx_ready"], 1)
                for i in range(16):
                    pool.indirect_dma_start(out=disp_dram, out_offset=bass.IndirectOffsetOnAxis(ap=sloti[:, 1, i:i + 1], axis=0),
                                            in_=tok[:, i % 8, :], in_offset=None, bounds_check=SLOTS - 1,
                                            oob_is_err=False).then_inc(s["scattered"], 16)
                block_pool(pool, l + 1)
                for k in range(2):
                    pool.wait_ge(s[f"eo_st{k}"], 16 * (NE // 2 + 1))
                for i in range(16):
                    pool.indirect_dma_start(out=rows[:, i, :], out_offset=None, in_=eo_dram,
                                            in_offset=bass.IndirectOffsetOnAxis(ap=sloti[:, 0, i:i + 1], axis=0),
                                            bounds_check=SLOTS - 1, oob_is_err=False).then_inc(s["gathered"], 16)
                pool.wait_ge(s["gathered"], 16 * 16)

            @block.scalar
            def _(act):
                act.sem_inc(s["gelu_done"], HC // 2)
                condition_act(act, sig)
                route_act(act, lt, 2)
                act.wait_ge(s["x_turned"], 1)
                for j in range(4):
                    ins = act.activation(tok[:, 2 * j:2 * j + 2, :].rearrange("p a b -> p (a b)"), ps[:, 4 + j, :], ACT.Identity)
                ins.then_inc(s["tok_ready"], 1)
                act.wait_ge(s["hot_turned"], 1)
                for j in range(4):
                    ins = act.activation(picks[:, j * HALF:(j + 1) * HALF], ps[0:NE, 4 + j, :], ACT.Identity)
                ins.then_inc(s["picks_ready"], 1)
                act.wait_ge(s["scattered"], 16 * 16)
                act.dma_start(rows[:, :, :], disp_dram.rearrange("(a p) d -> p a d", p=P)).then_inc(s["rows_loaded"], 16)
                act.wait_ge(s["rows_turned"], 1)
                for j in range(4):
                    ins = act.activation(dT[:, 0, j * HALF:(j + 1) * HALF], ps[:, j, :], ACT.Identity)
                ins.then_inc(s["dT_act"], 1)
                block_act(act, l + 1)

                def gelu(e, k, j):
                    act.wait_ge(s["bias_ready"], e + 1)
                    act.wait_ge(s["fc2_done"], e + 1)
                    for h in range(HC // 2):
                        act.wait_ge(s["fc1_done"], HC // 2 * e + h + 1 + HC)
                        for i in range(2):
                            ins = act.activation(hid[:, k, 2 * h + i, :], ps[:, h, i * CAP:(i + 1) * CAP], ACT.Gelu,
                                                 bias=fc1b[:, k, 2 * h + i:2 * h + i + 1])
                        ins.then_inc(s["gelu_done"], 1)

                experts(act, gelu)

            @block.vector
            def _(dve):
                dve.sem_inc(s["eo_ready"], 2)
                condition_dve(dve, l, sig)
                dve.wait_ge(s["router_done"], 1)
                dve.wait_ge(s["ld_gate"], 48)
                dstep.link(dve.tensor_copy(lt[:, 0, :, :], ps[:, 0, 0:8 * NE].rearrange("p (t e) -> p t e", t=8)))
                route_dve(dve, lt, one, rank[:, :, :], 2)
                dve.nop().then_inc(s["hot_ready"], 1)
                dstep.link(dve.tensor_tensor(one[:, 2, :], one[:, 0, :], one[:, 1, :], ALU.add))
                dstep.link(dve.tensor_scalar(one[:, 2, :], one[:, 2, :], 1e-9, None, ALU.max))
                dstep.link(dve.reciprocal(one[:, 2, :], one[:, 2, :]))
                for k in range(2):
                    dstep.mark(dve.tensor_tensor(gates[:, 8 * k:8 * k + 8], one[:, k, :], one[:, 2, :], ALU.mult))
                dve.wait_ge(s["picks_ready"], 1)
                dstep.link(dve.tensor_tensor_scan(count, base[:, 1:2].to_broadcast([NE, SLOTS]), picks, 0.0, ALU.mult, ALU.add))
                dstep.link(dve.tensor_scalar(fits, count, float(CAP), None, ALU.is_le))
                dstep.link(dve.scalar_tensor_tensor(out=pos, in0=count, scalar=-1.0, in1=fits, op0=ALU.add, op1=ALU.mult))
                dstep.link(dve.scalar_tensor_tensor(out=count, in0=pos, scalar=base[:, 0:1], in1=picks, op0=ALU.add, op1=ALU.mult))
                dve.tensor_tensor(fits, fits, picks, ALU.mult).then_inc(s["slots_ready"], 1)
                dve.wait_ge(s["slots_ps"], 1)
                dstep.link(dve.tensor_copy(slotf[:, 0:2, :].rearrange("p a b -> p (a b)"), ps[:, 0, 0:32]))
                dstep.link(dve.tensor_tensor(gates[:, :], gates[:, :], slotf[:, 1, :], ALU.mult))
                dstep.link(dve.tensor_scalar(slotf[:, 2, :], slotf[:, 1, :], -2.0 * SLOTS, 2.0 * SLOTS, ALU.mult, ALU.add))
                dstep.link(dve.tensor_tensor(slotf[:, 2, :], slotf[:, 2, :], slotf[:, 0, :], ALU.add))
                dve.tensor_copy(sloti[:, 0, :], slotf[:, 0, :])
                dve.tensor_copy(sloti[:, 1, :], slotf[:, 2, :]).then_inc(s["sidx_ready"], 1)
                dve.wait_ge(s["rows_turned"], 1)
                for j in range(4):
                    ins = dve.tensor_copy(dT[:, 1, j * HALF:(j + 1) * HALF], ps[:, 4 + j, :])
                ins.then_inc(s["dT_dve"], 1)
                block_dve(dve, l + 1)
                dve.wait_ge(s["ld_fc2b"], 16)

                def biases(e, k):
                    dve.tensor_scalar(fc1b[:, k, :], vecs[:, ds(HC * e + VEC["fc1b"][0], HC)], 1.0, None, ALU.mult) \
                        .then_inc(s["bias_ready"], 1)

                def store_rows(e, k, j):
                    dve.wait_ge(s["fc2_done"], e + 3)
                    dve.wait_ge(s[f"eo_st{k}"], 16 * j + 16)
                    dve.tensor_tensor(eo[:, k, :, :], ps[:, 4 + k, :].rearrange("p (a d) -> p a d", a=2),
                                      fc2b[:, ds(e, 1), :].to_broadcast([P, 2, C]), ALU.add).then_inc(s["eo_ready"], 1)

                for k in range(2):
                    biases(k, k)
                with dve.Fori(0, NE // 2 - 1) as j:
                    for k in range(2):
                        store_rows(2 * j + k, k, j)
                        biases(2 * j + k + 2, k)
                for k in range(2):
                    store_rows(NE - 2 + k, k, NE // 2 - 1)
                dve.wait_ge(s["gathered"], 16 * 16)
                for k in range(2):
                    for t in range(8):
                        if k == 0:
                            ins = dve.tensor_scalar(tok[:, t, :], rows[:, t, :], gates[:, t:t + 1], None, ALU.mult)
                        else:
                            ins = dve.scalar_tensor_tensor(out=tok[:, t, :], in0=rows[:, 8 + t, :], scalar=gates[:, 8 + t:9 + t],
                                                           in1=tok[:, t, :], op0=ALU.mult, op1=ALU.add)
                    if k == 0:
                        dstep.link(ins)
                ins.then_inc(s["y_ready"], 1)
                dve.wait_ge(s["y_turned"], 1)
                for ch in range(CH):
                    for h in range(2):
                        x = xT[:, ch, h * HALF:(h + 1) * HALF]
                        dstep.link(dve.tensor_tensor(x, x, ps[:, 2 * ch + h, :], ALU.add))

            @block.tensor
            def _(pe):
                pe.sem_inc(s["fc1_done"], HC)
                pe.sem_inc(s["fc2_done"], 2)
                pe.wait_ge(s["ld_gate"], 48)
                pe.wait_ge(xin_ready, l + 1)
                for t in range(8):
                    for k in range(CH):
                        ins = pe.matmul(ps[:, 0, t * NE:(t + 1) * NE], xin[:, k, t * P:(t + 1) * P], wgate[:, k, :],
                                        start=(k == 0), stop=(k == CH - 1))
                ins.then_inc(s["router_done"], 1)
                for t in range(8):
                    for k in range(CH):
                        ins = pe.transpose(ps[:, 4 + t // 2, t % 2 * C + k * P:t % 2 * C + (k + 1) * P],
                                           xin[:, k, t * P:(t + 1) * P], ident[:, :])
                ins.then_inc(s["x_turned"], 1)
                pe.wait_ge(s["hot_ready"], 1)
                pe.wait_ge(s["tok_ready"], 1)
                for i in range(16):
                    ins = pe.transpose(ps[0:NE, 4 + i // 4, i % 4 * P:(i % 4 + 1) * P], lt[:, 2 + i // 8, i % 8, :], ident[:, :])
                ins.then_inc(s["hot_turned"], 1)
                pe.wait_ge(s["slots_ready"], 1)
                for a, src in enumerate((count, fits)):
                    for i in range(16):
                        ins = pe.matmul(ps[:, 0, 16 * a + i:16 * a + i + 1], src[:, i * P:(i + 1) * P], base[:, 1:2],
                                        start=True, stop=True)
                ins.then_inc(s["slots_ps"], 1)
                pe.wait_ge(s["rows_loaded"], 16)
                for a in range(16):
                    for k in range(CH):
                        ins = pe.transpose(ps[:, 4 * k + a // 4, a % 4 * P:(a % 4 + 1) * P], rows[:, a, k * P:(k + 1) * P], ident[:, :])
                ins.then_inc(s["rows_turned"], 1)
                pe.wait_ge(s["dT_act"], 1)
                pe.wait_ge(s["dT_dve"], 1)

                def up(e, k, n):
                    pe.wait_ge(s[f"fc1_{k}"], 16 * n + 16)
                    for h in range(HC // 2):
                        pe.wait_ge(s["gelu_done"], HC // 2 * e + h + 1)
                        for i in range(2):
                            f = (2 * h + i) * P
                            for c in range(CH):
                                ins = pe.matmul(ps[:, h, i * CAP:(i + 1) * CAP], fc1[:, k, c, f:f + P],
                                                dT[:, c, ds(e * CAP, CAP)], start=(c == 0), stop=(c == CH - 1))
                        ins.then_inc(s["fc1_done"], 1)

                def down(e, k, n):
                    pe.wait_ge(s[f"fc2_{k}"], 16 * n + 16)
                    pe.wait_ge(s["gelu_done"], HC // 2 * (e + 2))
                    pe.wait_ge(s["eo_ready"], e + 1)
                    for a in range(2):
                        for h in range(HC):
                            ins = pe.matmul(ps[:, 4 + k, a * C:(a + 1) * C], hid[:, k, h, a * P:(a + 1) * P], fc2[:, k, h, :],
                                            start=(h == 0), stop=(h == HC - 1))
                    ins.then_inc(s["fc2_done"], 1)

                up(0, 0, 0)
                with pe.Fori(0, NE // 2 - 1) as j:
                    up(2 * j + 1, 1, j)
                    down(2 * j, 0, j)
                    up(2 * j + 2, 0, j + 1)
                    down(2 * j + 1, 1, j)
                up(NE - 1, 1, NE // 2 - 1)
                down(NE - 2, 0, NE // 2 - 1)
                down(NE - 1, 1, NE // 2 - 1)
                pe.wait_ge(s["y_ready"], 1)
                for t in range(8):
                    for k in range(CH):
                        ins = pe.transpose(ps[:, 2 * k + t // 4, t % 4 * P:(t % 4 + 1) * P], tok[:, t, k * P:(k + 1) * P], ident[:, :])
                ins.then_inc(s["y_turned"], 1)


    def stage_l2_attn(l):
        PAIRS, PER, HS = L2_PAIRS, 4, HD + 1
        ITER = PAIRS // 2
        STEPS = PER * ITER
        with ExitStack() as st:
            def sb(n, shape, dt=F32):
                return st.enter_context(nc.sbuf_tensor("K_" + n, shape, dt))

            sig = sb("sig", [P, CH, NT])
            wqkv = sb("wqkv", [P, 2, CH, 3 * P])
            wo = sb("wo", [P, 2, C])
            qT = sb("qT", [P, 2, HALF])
            ks = sb("ks", [P, 2, 4, P])
            vs = sb("vs", [P, 2, 4, 2, HS])
            kv = sb("kv", [P, 2, 2, 2 * HS])
            quot = sb("quot", [P, 4, P])
            norm = sb("norm", [P, 2, 4])
            oT = sb("oT", [P, 2, HALF])
            ps_q = st.enter_context(nc.psum_tensor("K_ps_q", [P, HALF], F32))
            ps_kvp = st.enter_context(nc.psum_tensor("K_ps_kvp", [P, 2, 2, 2 * P], F32))
            ps_kv = st.enter_context(nc.psum_tensor("K_ps_kv", [P, HALF], F32))
            ps_o = st.enter_context(nc.psum_tensor("K_ps_o", [P, 2, HALF], F32))
            ps_t = st.enter_context(nc.psum_tensor("K_ps_t", [P, HALF], F32))
            ps_y = st.enter_context(nc.psum_tensor("K_ps_y", [P, HALF], F32))
            names = ("wqkv0 wqkv1 wo0 wo1 zeroed q_done q_evac kvp_done kvp_evac kv_done kv_evac o_done quot_ready "
                     "t_done t_evac y_done y_added").split()
            s = {n: sem("K_" + n) for n in names}
            block = st.enter_context(nc.Block())

            def loop(eng, step, per=0, count=None):
                for j in range(PER):
                    step(j, j, 0)
                if count:
                    assert count.n - loop.start == per, (count.n - loop.start, per)
                with eng.Fori(1, ITER) as i:
                    if count:
                        count.enter(i - 1, per)
                    for j in range(PER):
                        step(PER * i + j, j, i)
                if count:
                    count.leave(ITER - 1)

            @block.sync
            def _(sp):
                def load(p, k):
                    need(sp, s["kvp_done"], 4 * (p - 1))
                    sp.dma_start(wqkv[:, k, :, :].rearrange("p a b -> p (a b)"), io["l2_wqkv"][p]).then_inc(s[f"wqkv{k}"], 16)
                    need(sp, s["y_done"], 4 * (p - 1))
                    sp.dma_start(wo[:, k, :], io["l2_wo"][p]).then_inc(s[f"wo{k}"], 16)

                for k in range(2):
                    load(k, k)
                with sp.Fori(1, ITER) as i:
                    for k in range(2):
                        load(2 * i + k, k)

            @block.gpsimd
            def _(pool):
                pstep.mark(pool.memset(kv[:, :, :, :], 0.0))
                pool.memset(vs[:, :, :, :, HD:HS], 1.0).then_inc(s["zeroed"], 1)
                with pool.Fori(0, NP) as i:
                    pstep.enter(i, PIECE_POOL_STEPS)
                    piece_pool(pool, l + 1, i, 0)
                pstep.leave(NP)

            @block.scalar
            def _(act):
                condition_act(act, sig)
                act.wait_ge(s["zeroed"], 1)

                def step(n, j, i):
                    act.wait_ge(s["q_done"], n + 1)
                    need(act, s["o_done"], n - 1)
                    act.activation(qT[:, j % 2, :], ps_q[:, :], ACT.Relu).then_inc(s["q_evac"], 1)
                    need(act, s["kv_done"], n - 1)
                    for h in range(2):
                        act.wait_ge(s["kvp_done"], 2 * n + h + 1)
                        act.activation(ks[:, j % 2, 2 * h:2 * h + 2, :], ps_kvp[:, h, :, 0:P], ACT.Relu)
                        act.activation(vs[:, j % 2, 2 * h:2 * h + 2, :, 0:HD],
                                       ps_kvp[:, h, :, P:2 * P].rearrange("p a (r d) -> p a r d", r=2),
                                       ACT.Identity).then_inc(s["kvp_evac"], 1)
                    if j == 0:
                        piece_act(act, l + 1, i, 0)
                    if not isinstance(n, int) or n:
                        turned(n - 1, (j + 1) % 2)

                def turned(n, k):
                    act.wait_ge(s["t_done"], n + 1)
                    need(act, s["y_done"], 2 * (n - 1))
                    act.activation(oT[:, k, :], ps_t[:, :], ACT.Identity).then_inc(s["t_evac"], 1)

                loop(act, step)
                turned(STEPS - 1, 1)

            @block.vector
            def _(dve):
                condition_dve(dve, l, sig)
                for ch in range(CH):
                    dstep.link(dve.tensor_scalar(xT[:, ch, :], xT[:, ch, :], vec("bo2", ch), None, ALU.add))
                dve.wait_ge(s["zeroed"], 1)

                def add(n, j):
                    for ch in range(CH):
                        dve.wait_ge(s["y_done"], 2 * n + ch + 1)
                        x = xT[:, ch, j % 2 * HALF:(j % 2 + 1) * HALF]
                        dve.tensor_tensor(x, x, ps_y[:, :], ALU.add).then_inc(s["y_added"], 1)

                def step(n, j, i):
                    if j == 0:
                        piece_scans(dve, l + 1, i, 0)
                    dve.wait_ge(s["kv_done"], n + 1)
                    need(dve, s["o_done"], n - 1)
                    for r in range(2):
                        h = slice(HD * r, HD * r + HD)
                        ins = dve.tensor_copy(kv[h, j % 2, :, HS * r:HS * r + HS],
                                              ps_kv[h, 0:4 * HS].rearrange("p (b e) -> p b e", b=2)[:, :, HS * r:HS * r + HS])
                    ins.then_inc(s["kv_evac"], 1)
                    if j == 2:
                        piece_finish(dve, l + 1, i, 0)
                    dve.wait_ge(s["o_done"], n + 1)
                    o = ps_o[:, :, 0:4 * HS].rearrange("p a (q e) -> p a q e", e=HS)
                    dstep.link(dve.tensor_scalar(norm[:, :, :], o[:, :, :, HD], 1e-6, None, ALU.max))
                    dstep.link(dve.reciprocal(norm[:, :, :], norm[:, :, :]))
                    need(dve, s["t_done"], n)
                    dve.tensor_tensor(quot[:, :, :].rearrange("p (a b) (r e) -> p a (b r) e", a=2, r=2), o[:, :, :, 0:HD],
                                      norm[:, :, :].unsqueeze(3).to_broadcast([P, 2, 4, HD]),
                                      ALU.mult).then_inc(s["quot_ready"], 1)
                    if not isinstance(n, int) or n:
                        add(n - 1, j + 1)

                loop.start = dstep.n
                loop(dve, step, PIECE_DVE_STEPS + 2 * PER, dstep)
                add(STEPS - 1, 1)

            @block.tensor
            def _(pe):
                pe.wait_ge(xin_ready, l + 1)

                def queries(n, j):
                    need(pe, s["q_evac"], n)
                    for k in range(CH):
                        ins = pe.matmul(ps_q[:, :], wqkv[:, j // 2, k, 0:P], xin[:, k, j % 2 * HALF:(j % 2 + 1) * HALF],
                                        start=(k == 0), stop=(k == CH - 1))
                    ins.then_inc(s["q_done"], 1)

                def keys_values(n, j, h):
                    need(pe, s["kvp_evac"], 2 * n - 1 + h)
                    for a in range(2):
                        t = j % 2 * HALF + (2 * h + a) * P
                        for k in range(CH):
                            ins = pe.matmul(ps_kvp[:, h, a, :], xin[:, k, t:t + P], wqkv[:, j // 2, k, P:3 * P],
                                            start=(k == 0), stop=(k == CH - 1))
                    ins.then_inc(s["kvp_done"], 1)

                def key_value(n, j):
                    pe.wait_ge(s["kvp_evac"], 2 * n + 2)
                    need(pe, s["kv_evac"], n)
                    for b in range(2):
                        for t in range(2):
                            ins = pe.matmul(ps_kv[:, 2 * HS * b:2 * HS * (b + 1)], ks[:, j % 2, 2 * b + t, :],
                                            vs[:, j % 2, 2 * b + t, :, :].rearrange("p r e -> p (r e)"),
                                            start=(t == 0), stop=(t == 1))
                    ins.then_inc(s["kv_done"], 1)

                def weighted(n, j):
                    pe.wait_ge(s["kv_evac"], n + 1)
                    pe.wait_ge(s["q_evac"], n + 1)
                    need(pe, s["quot_ready"], n)
                    for t in range(4):
                        ins = pe.matmul(ps_o[:, t // 2, 2 * HS * (t % 2):2 * HS * (t % 2 + 1)], qT[:, j % 2, t * P:(t + 1) * P],
                                        kv[:, j % 2, t // 2, :], start=True, stop=True)
                    ins.then_inc(s["o_done"], 1)

                def turn(n):
                    pe.wait_ge(s["quot_ready"], n + 1)
                    need(pe, s["t_evac"], n)
                    for t in range(4):
                        ins = pe.transpose(ps_t[:, t * P:(t + 1) * P], quot[:, t, :], ident[:, :])
                    ins.then_inc(s["t_done"], 1)

                def output(n, j, ch):
                    need(pe, s["y_added"], 2 * n + ch)
                    pe.matmul(ps_y[:, :], wo[:, j // 2, ch * P:(ch + 1) * P], oT[:, j % 2, :],
                              start=True, stop=True).then_inc(s["y_done"], 1)

                def step(n, j, i):
                    first = isinstance(n, int)
                    if j % 2 == 0:
                        pe.wait_ge(s[f"wqkv{j // 2}"], 16 * i + 16)
                    queries(n, j)
                    if not (first and n < 1):
                        weighted(n - 1, (j + 3) % 4)
                    keys_values(n, j, 0)
                    if not (first and n < 2):
                        k = (j + 2) % 4
                        if k % 2 == 0:
                            pe.wait_ge(s[f"wo{k // 2}"], 16 * (i if j >= 2 else i - 1) + 16)
                        pe.wait_ge(s["t_evac"], n - 1)
                        output(n - 2, k, 0)
                    keys_values(n, j, 1)
                    if not (first and n < 1):
                        turn(n - 1)
                    if not (first and n < 2):
                        output(n - 2, (j + 2) % 4, 1)
                    key_value(n, j)

                loop(pe, step)
                weighted(STEPS - 1, 3)
                pe.wait_ge(s["wo1"], 16 * ITER)
                pe.wait_ge(s["t_evac"], STEPS - 1)
                for ch in range(CH):
                    output(STEPS - 2, 2, ch)
                turn(STEPS - 1)
                pe.wait_ge(s["t_evac"], STEPS)
                for ch in range(CH):
                    output(STEPS - 1, 3, ch)

    def stage_l2_ffn(l):
        with ExitStack() as st:
            sig = st.enter_context(nc.sbuf_tensor("F_sig", [P, CH, NT], F32))
            w = st.enter_context(nc.sbuf_tensor("F_w", [P, CH, C], F32))
            scaled = st.enter_context(nc.sbuf_tensor("F_scaled", [P, 4, HALF], F32))
            ps = st.enter_context(nc.psum_tensor("F_ps", [P, 4, HALF], F32))
            s = {n: sem("F_" + n) for n in ("ld_w", "done", "scaled")}
            block = st.enter_context(nc.Block())
            half = lambda h: slice(h * HALF, (h + 1) * HALF)

            @block.sync
            def _(sp):
                sp.dma_start(w[:, :, :], io["l2_w"]).then_inc(s["ld_w"], 16)

            @block.gpsimd
            def _(pool):
                block_pool(pool, l + 1)

            @block.scalar
            def _(act):
                condition_act(act, sig)
                for g in range(4):
                    act.wait_ge(s["done"], g + 1)
                    act.activation(scaled[:, g, :], ps[:, g, :], ACT.Identity, scale=vec("fscale", g % 2),
                                   bias=vec("fbias", g % 2)).then_inc(s["scaled"], 1)
                block_act(act, l + 1)

            @block.vector
            def _(dve):
                condition_dve(dve, l, sig)
                for g in range(4):
                    dve.wait_ge(s["scaled"], g + 1)
                    x = xT[:, g % 2, half(g // 2)]
                    dstep.mark(dve.tensor_tensor(x, x, scaled[:, g, :], ALU.add))
                block_dve(dve, l + 1)

            @block.tensor
            def _(pe):
                pe.wait_ge(s["ld_w"], 16)
                pe.wait_ge(xin_ready, l + 1)
                for g in range(4):
                    m = g % 2
                    for k in range(CH):
                        ins = pe.matmul(ps[:, g, :], w[:, k, m * P:(m + 1) * P], xin[:, k, half(g // 2)],
                                        start=(k == 0), stop=(k == CH - 1))
                    ins.then_inc(s["done"], 1)

    def stage_l3_attn(l):
        LOW = -1.0e38
        with ExitStack() as st:
            def sb(n, shape, dt=F32):
                return st.enter_context(nc.sbuf_tensor("V_" + n, shape, dt))

            sig = sb("sig", [P, CH, NT])
            w = sb("w", [P, 4, CH, C])
            mixed = sb("mixed", [P, 3, CH, NT])
            rest = sb("rest", [P, 8])
            k, v, r = sb("k", [P, CH, NT]), sb("v", [P, CH, NT]), sb("r", [P, CH, NT])
            top = sb("top", [P, CH, NB, T + 1])
            num = sb("num", [P, CH, NB, T + 1])
            den = sb("den", [P, CH, NB, T + 1])
            grow = sb("grow", [P, CH, NT])
            ps = st.enter_context(nc.psum_tensor("V_ps", [P, 8, HALF], F32))
            names = "ld_w w_exp scaled mixed done evac diff_ready exp_ready prod_ready rwkv_ready".split()
            s = {n: sem("V_" + n) for n in names}
            block = st.enter_context(nc.Block())
            half = lambda h: slice(h * HALF, (h + 1) * HALF)
            wave = lambda x: x.rearrange("p (b t) -> p b t", b=NB)
            keep1, keep2 = mixed[:, 0], mixed[:, 1]
            out1, out2 = mixed[:, 2], sig

            @block.sync
            def _(sp):
                sp.dma_start(w[:, :, :, :], io["l3_w"]).then_inc(s["ld_w"], 16)

            @block.gpsimd
            def _(pool):
                for ch in range(CH):
                    pool.wait_ge(s["exp_ready"], 2 * ch + 1)
                    pool.tensor_tensor(grow[:, ch, :], keep2[:, ch, :], v[:, ch, :], ALU.mult).then_inc(s["prod_ready"], 1)
                    pool.wait_ge(s["exp_ready"], 2 * ch + 2)
                    pool.tensor_tensor(k[:, ch, :], out2[:, ch, :], v[:, ch, :], ALU.mult).then_inc(s["prod_ready"], 1)
                block_pool(pool, l + 1)

            @block.scalar
            def _(act):
                condition_act(act, sig)
                act.activation(rest[:, 6:8], vecs[:, VEC["decay"][0]:VEC["decay"][0] + 2], ACT.Exp).then_inc(s["w_exp"], 1)
                act.wait_ge(xin_ready, l + 1)
                for j, n in enumerate(("mk", "mv", "mr")):
                    for ch in range(CH):
                        act.activation(mixed[:, j, ch, :], xin[:, ch, :], ACT.Identity, scale=vec(n, ch)).then_inc(s["scaled"], 1)
                for g in range(12):
                    dst, ch, h = (k, v, r)[g // 4], g // 2 % 2, g % 2
                    act.wait_ge(s["done"], g + 1)
                    act.activation(dst[:, ch, half(h)], ps[:, g % 8, :], ACT.Sigmoid if g >= 8 else ACT.Identity) \
                        .then_inc(s["evac"], 1)
                for ch in range(CH):
                    for j, pair in enumerate(((keep1, keep2), (out1, out2))):
                        act.wait_ge(s["diff_ready"], 2 * ch + j + 1)
                        for x in pair:
                            ins = act.activation(x[:, ch, :], x[:, ch, :], ACT.Exp)
                        ins.then_inc(s["exp_ready"], 1)
                block_act(act, l + 1)

            @block.vector
            def _(dve):
                condition_dve(dve, l, sig)
                dve.memset(top[:, :, :, 0:1], LOW)
                dve.memset(num[:, :, :, 0:1], 0.0)
                dve.memset(den[:, :, :, 0:1], 0.0)
                dstep.link(dve.tensor_scalar(rest[:, 0:6], vecs[:, VEC["mk"][0]:VEC["mk"][0] + 6], -1.0, 1.0, ALU.mult, ALU.add))
                for j in range(3):
                    for ch in range(CH):
                        dve.wait_ge(s["scaled"], 2 * j + ch + 1)
                        m = wave(mixed[:, j, ch, :])[:, :, 1:T]
                        ins = dve.scalar_tensor_tensor(out=m, in0=wave(xin[:, ch, :])[:, :, 0:T - 1],
                                                       scalar=rest[:, 2 * j + ch:2 * j + ch + 1], in1=m, op0=ALU.mult, op1=ALU.add)
                    ins.then_inc(s["mixed"], 1)
                dve.wait_ge(s["w_exp"], 1)
                dstep.link(dve.tensor_scalar(rest[:, 6:8], rest[:, 6:8], -1.0, None, ALU.mult))
                dve.wait_ge(s["done"], 12)
                dve.wait_ge(s["evac"], 4)
                for ch in range(CH):
                    decayed, first, kc = rest[:, 6 + ch:7 + ch], vec("first", ch), wave(k[:, ch, :])
                    for b in range(NB):
                        ins = dve.tensor_tensor_scan(top[:, ch, b, 1:T + 1], decayed.to_broadcast([P, T]),
                                                     k[:, ch, b * T:(b + 1) * T], LOW, ALU.add, ALU.max)
                    dstep.link(ins)
                    before, after = top[:, ch, :, 0:T], top[:, ch, :, 1:T + 1]
                    dve.scalar_tensor_tensor(out=wave(keep1[:, ch, :]), in0=before, scalar=decayed, in1=after,
                                             op0=ALU.add, op1=ALU.subtract)
                    dve.tensor_tensor(wave(keep2[:, ch, :]), kc, after, ALU.subtract).then_inc(s["diff_ready"], 1)
                    dstep.link(dve.scalar_tensor_tensor(out=wave(out2[:, ch, :]), in0=kc, scalar=first, in1=before,
                                                        op0=ALU.add, op1=ALU.max))
                    dstep.link(dve.tensor_tensor(wave(out1[:, ch, :]), before, wave(out2[:, ch, :]), ALU.subtract))
                    dve.scalar_tensor_tensor(out=wave(out2[:, ch, :]), in0=kc, scalar=first, in1=wave(out2[:, ch, :]),
                                             op0=ALU.add, op1=ALU.subtract).then_inc(s["diff_ready"], 1)
                for ch in range(CH):
                    dve.wait_ge(s["exp_ready"], 2 * ch + 1)
                    dve.wait_ge(s["prod_ready"], 2 * ch + 1)
                    for b in range(NB):
                        c = slice(b * T, (b + 1) * T)
                        dve.tensor_tensor_scan(num[:, ch, b, 1:T + 1], keep1[:, ch, c], grow[:, ch, c], 0.0, ALU.mult, ALU.add)
                        ins = dve.tensor_tensor_scan(den[:, ch, b, 1:T + 1], keep1[:, ch, c], keep2[:, ch, c], 0.0,
                                                     ALU.mult, ALU.add)
                    dstep.link(ins)
                    dve.wait_ge(s["exp_ready"], 2 * ch + 2)
                    n, d = num[:, ch, :, 0:T], den[:, ch, :, 0:T]
                    e1, e2 = wave(out1[:, ch, :]), wave(out2[:, ch, :])
                    dve.tensor_tensor(n, n, e1, ALU.mult)
                    dstep.link(dve.tensor_tensor(d, d, e1, ALU.mult))
                    dve.wait_ge(s["prod_ready"], 2 * ch + 2)
                    dve.tensor_tensor(n, n, wave(k[:, ch, :]), ALU.add)
                    dstep.link(dve.tensor_tensor(e2, d, e2, ALU.add))
                    dstep.link(dve.reciprocal(e2, e2))
                    dve.wait_ge(s["evac"], 12)
                    dstep.link(dve.tensor_tensor(e2, n, e2, ALU.mult))
                    dve.tensor_tensor(r[:, ch, :], r[:, ch, :], out2[:, ch, :], ALU.mult).then_inc(s["rwkv_ready"], 1)
                block_dve(dve, l + 1)
                for g in range(4):
                    dve.wait_ge(s["done"], 12 + g + 1)
                    x = xT[:, g // 2, half(g % 2)]
                    dstep.mark(dve.tensor_tensor(x, x, ps[:, (12 + g) % 8, :], ALU.add))

            @block.tensor
            def _(pe):
                pe.wait_ge(s["ld_w"], 16)
                for g in range(16):
                    j, m, h = g // 4, g // 2 % 2, g % 2
                    if j < 3:
                        pe.wait_ge(s["mixed"], j + 1)
                    elif g == 12:
                        pe.wait_ge(s["rwkv_ready"], 2)
                    if g >= 8:
                        pe.wait_ge(s["evac"], g - 7)
                    for c in range(CH):
                        src = mixed[:, j, c, half(h)] if j < 3 else r[:, c, half(h)]
                        ins = pe.matmul(ps[:, g % 8, :], w[:, j, c, m * P:(m + 1) * P], src, start=(c == 0), stop=(c == CH - 1))
                    ins.then_inc(s["done"], 1)

    def stage_last():
        with ExitStack() as st:
            stored = sem("stored")
            block = st.enter_context(nc.Block())

            @block.sync
            def _(sp):
                sp.dma_start(io["yT"], xT[:, :, :]).then_inc(stored, 16)
                sp.wait_ge(stored, 16)

    stage_l0_attn(0)
    stage_moe(1, "L0")
    stage_l1_attn(2)
    stage_l1_ffn(3)
    stage_l2_attn(4)
    stage_l2_ffn(5)
    stage_l3_attn(6)
    stage_moe(7, "L3")
    stage_last()
    outer.close()


def chunks(a, axis, n):
    pad = [(0, 0)] * a.ndim
    pad[axis] = (0, n * P - a.shape[axis])
    a = np.pad(a, pad)
    return a.reshape(a.shape[:axis] + (n, P) + a.shape[axis + 1:])


def features(a):
    n = -(-a.shape[0] // P)
    return chunks(a, 0, n).transpose(1, 0, 2)


def columns(v, n):
    return chunks(v.reshape(-1), 0, n).T


def lay_out(i):
    f = np.float32
    out = {}
    tokens = lambda a: a.reshape(NT, C).T.reshape(CH, P, NT).transpose(1, 0, 2)
    out["xT"], out["fT"] = tokens(i["x"]), tokens(i["fside_BxSxS_0"])
    out["cond"] = np.broadcast_to(i["cond_512"], (P, NB, 64))
    out["ident"] = np.eye(P, dtype=f)
    conds = ["L0_cond", "L0_cond2", "L1_cond", "L1_cond2", "L2_cond", "L2_cond2", "L3_cond", "L3_cond2"]
    pieces = {
        "w": np.concatenate([columns(i[c + "_w"], CH) for c in conds], 1),
        "u": np.repeat(np.concatenate([columns(i[c + "_u"], CH) for c in conds], 1), NB, axis=1),
        "bq": i["L0_attn_bq"].reshape(4, 2, 4, HD).transpose(1, 3, 0, 2).reshape(P, 16),
        "kw": np.repeat(i["L0_attn_key_weights"].reshape(4, 2, 4).transpose(1, 0, 2), HD, axis=0).reshape(P, 16),
        "bk": columns(i["L0_attn_bk"], 4), "bv": columns(i["L0_attn_bv"], 4), "bo0": columns(i["L0_attn_bo"], 2),
        "b1": columns(np.concatenate([i["L1_attn_b1"], i["L1_attn_b1"][2 * P:]]), 3), "convb": columns(i["L1_attn_conv_b"], 3),
        "ba": columns(i["L1_attn_ba"], 3), "bx": columns(i["L1_attn_bx"], 3), "lam": columns(i["L1_attn_lam"], 3),
        "b2": columns(i["L1_attn_b2"], 2), "fc1b": columns(i["L1_ffn_fc1_b"], NE * FF // P),
        "bo2": columns(i["L2_attn_bo"], 2), "fscale": columns(i["L2_ffn_scale_weight"], 2),
        "fbias": columns(i["L2_ffn_bias"], 2), "decay": columns(i["L3_attn_time_decay"], 2),
        "first": columns(i["L3_attn_time_first"], 2), "mk": columns(i["L3_attn_time_mix_k"], 2),
        "mv": columns(i["L3_attn_time_mix_v"], 2), "mr": columns(i["L3_attn_time_mix_r"], 2),
    }
    out["vecs"] = np.concatenate([pieces[n] for n in VEC], 1)
    inv = (f(1.0) / f(10000.0) ** (np.arange(0, HD, 2, dtype=f) / f(HD))).astype(f)
    ang = np.arange(T, dtype=f)[None, :] * inv[:, None]
    cos, sin = np.cos(ang), np.sin(ang)
    out["rope"] = np.stack([np.concatenate([cos] * 4), np.concatenate([-sin, sin] * 2)], 1).astype(f)
    out["mask"] = np.where(np.arange(P)[None, :] > np.arange(P)[:, None], f(NEG), f(0))
    wq = i["L0_attn_Wq"].reshape(4, 2, 4, HD, CH, P).transpose(0, 5, 2, 4, 1, 3).reshape(4, P, 1024)
    wk = i["L0_attn_Wk"].reshape(4, P, CH, P).transpose(0, 3, 2, 1).reshape(4, P, 256)
    wv = i["L0_attn_Wv"].reshape(4, P, CH, P).transpose(0, 3, 2, 1).reshape(4, P, 256)
    wo = i["L0_attn_Wo"].reshape(C, 4, 2, 4, HD).transpose(1, 2, 4, 3, 0).reshape(4, P, 1024)
    out["w_l0a"] = np.concatenate([wk, wv, wq, wo], 2)
    for name, sh in (("L0", ("shw_gate", "shw_up", "shw_down")), ("L3", ("sw_gate", "sw_up", "sw_down"))):
        g = lambda n: i[f"{name}_ffn_{n}"]
        shared = g("shgate_w" if name == "L0" else "shared_gate_w").reshape(C, 1)
        out[name + "_gate"] = features(np.concatenate([g("gate_w").T, shared], 1))
        up = []
        for a, b in (("w_gate", sh[0]), ("w_up", sh[1])):
            m = np.concatenate([g(a).transpose(1, 0, 2).reshape(C, NE * EH), g(b)], 1)
            n = -(-m.shape[1] // P)
            up.append(chunks(m, 1, n).reshape(CH, P, n, P).transpose(2, 1, 0, 3).reshape(n, P, 2 * P))
        down = chunks(np.concatenate([g("w_down").reshape(NE * EH, C), g(sh[2])], 0), 0, n)
        out[name + "_w"] = np.concatenate(up + [down], 2)
    out["rank"] = np.broadcast_to(np.arange(NE, 0, -1, dtype=f), (P, 8, NE))
    w1 = i["L1_attn_w1"].T
    out["l1_w1"] = features(np.concatenate([w1, w1[:, 2 * P:]], 1))
    cw = i["L1_attn_conv_w"].transpose(2, 1, 0)
    full = cw[:, :2 * P].reshape(TAPS * CH, P, R1)
    half = cw[:, 2 * P:].reshape(2, P, R1)
    out["l1_conv"] = np.concatenate([full, half], 0).transpose(1, 0, 2)
    out["l1_gate"] = np.stack([features(i["L1_attn_wa"].T), features(i["L1_attn_wx"].T)], 1)
    out["l1_w2"] = features(i["L1_attn_w2"].T)
    out["l1_wg"] = features(i["L1_ffn_wg"])
    first = np.zeros((NE, 4), f)
    first[:, 0], first[:, 1] = np.arange(NE) * CAP, 1.0
    out["base"] = first
    out["l1_fc1"] = i["L1_ffn_fc1_w"].reshape(NE, CH, P, FF).transpose(0, 2, 1, 3).reshape(NE, P, CH * FF)
    out["l1_fc2"] = i["L1_ffn_fc2_w"].reshape(NE, FF // P, P, C).transpose(0, 2, 1, 3).reshape(NE, P, FF // P * C)
    out["l1_fc2b"] = i["L1_ffn_fc2_b"].reshape(1, NE * C)
    w = np.stack([i["L2_attn_" + n].reshape(CH, P, L2_PAIRS, P) for n in ("Wq", "Wk", "Wv")], 3)
    out["l2_wqkv"] = w.transpose(2, 1, 0, 3, 4).reshape(L2_PAIRS, P, CH * 3 * P)
    out["l2_wo"] = i["L2_attn_Wo"].reshape(L2_PAIRS, P, C)
    out["l2_w"] = features(i["L2_ffn_weight"].T)
    out["l3_w"] = np.stack([features(i["L3_attn_" + n].T) for n in ("Wk", "Wv", "Wr", "Wo")], 1)
    return {k: np.ascontiguousarray(v) for k, v in out.items()}


def kernel(**inputs):
    import concourse.bacc as bacc
    from concourse.bass_utils import run_bass_kernel_spmd

    arrays = lay_out({k: np.asarray(v) for k, v in inputs.items()})
    nc = bacc.Bacc("TRN2", target_bir_lowering=False, num_devices=1)
    io = {n: nc.dram_tensor(n + "_dram", a.shape, mybir.dt.from_np(a.dtype), kind="ExternalInput").ap()
          for n, a in arrays.items()}
    io["yT"] = nc.dram_tensor("yT_dram", (P, CH, NT), F32, kind="ExternalOutput").ap()
    build_program(nc, io)
    r = run_bass_kernel_spmd(nc, [{n + "_dram": a for n, a in arrays.items()}], core_ids=[0])
    y = r.results[0]["yT_dram"]
    return y.transpose(1, 0, 2).reshape(C, NT).T.reshape(NB, T, C)
```

```python
from contextlib import ExitStack

import numpy as np

import concourse.bass as bass
from concourse import mybir

P = 128
NB, T, C = 4, 256, 256
NT = NB * T
CH = C // P
HALF = NT // 2
NL = 8
NP = CH * NB

HD = 64
L0_PAIRS, L0_GROUP = 4, 4
NE, EH = 8, 176
L0_SH, L3_SH = 352, 704
R1, TAPS = 320, 4
FF, CAP = 1024, 256
SLOTS = NE * CAP
L2_PAIRS = 16

F32 = mybir.dt.float32
U32 = mybir.dt.uint32
ALU = mybir.AluOpType
ACT = mybir.ActivationFunctionType
AX_X = mybir.AxisListType.X
ds = bass.ds
NEG = -1.0e30


def vec_columns():
    sizes = [("w", 2 * NL), ("u", NP * NL), ("bq", 16), ("kw", 16), ("bk", 4), ("bv", 4), ("bo0", 2),
             ("b1", 3), ("convb", 3), ("ba", 3), ("bx", 3), ("lam", 3), ("b2", 2), ("fc1b", NE * FF // P),
             ("bo2", 2), ("fscale", 2), ("fbias", 2), ("decay", 2), ("first", 2), ("mk", 2), ("mv", 2),
             ("mr", 2)]
    at, out = 0, {}
    for name, n in sizes:
        out[name] = (at, n)
        at += n
    return out, at


VEC, NVEC = vec_columns()


class Steps:

    def __init__(self, eng, sem):
        self.eng, self.sem, self.base, self.n = eng, sem, 0, 0

    def mark(self, ins):
        self.n += 1
        return ins.then_inc(self.sem, 1)

    def wait(self):
        self.eng.wait_ge(self.sem, self.base + self.n)

    def link(self, ins):
        self.mark(ins)
        self.wait()

    def enter(self, i, per):
        self.kept = self.base + self.n
        self.base, self.n, self.per = self.kept + i * per, 0, per

    def leave(self, count):
        assert self.n == self.per, (self.n, self.per)
        self.base, self.n = self.kept + count * self.per, 0


def build_program(nc, io):
    outer = ExitStack()

    def sem(name):
        return outer.enter_context(nc.semaphore(name))

    def keep(name, shape, dt=F32):
        return outer.enter_context(nc.sbuf_tensor(name, shape, dt))

    xT = keep("xT", [P, CH, NT])
    xin = keep("xin", [P, CH, NT])
    fside = keep("fside", [P, CH, NT])
    ek = keep("ek", [P, CH, NT])
    ekv = keep("ekv", [P, CH, NT])
    ek_back = keep("ek_back", [P, CH, NT])
    ekv_back = keep("ekv_back", [P, CH, NT])
    vecs = keep("vecs", [P, NVEC])
    ident = keep("ident", [P, P])
    decay = keep("decay", [P, NL * CH * NB])
    gain = keep("gain", [P, NB])
    mod = keep("mod", [P, 2, CH, NT])
    uk = keep("uk", [P, 2, T])
    scans = keep("scans", [P, 2, 2, 2, T])
    terms = keep("terms", [P, 2, 2, T])
    sums = keep("sums", [P, 2, 2, T])

    dve_steps_sem, act_steps_sem, pool_steps_sem = sem("dve_steps"), sem("act_steps"), sem("pool_steps")
    uk_ready = sem("uk_ready")
    euk_ready = sem("euk_ready")
    scans_ready = sem("scans_ready")
    sums_ready = sem("sums_ready")
    sig_ready = sem("sig_ready")
    xin_ready = sem("xin_ready")
    sub_ready = sem("sub_ready")
    exp_ready = sem("exp_ready")
    steps = {"dve": Steps(nc.vector, dve_steps_sem), "act": Steps(nc.scalar, act_steps_sem),
             "pool": Steps(nc.gpsimd, pool_steps_sem)}
    dstep, astep, pstep = steps["dve"], steps["act"], steps["pool"]

    def need(eng, semaphore, count):
        if not isinstance(count, int) or count > 0:
            eng.wait_ge(semaphore, count)

    def vec(name, i=0):
        return vecs[:, ds(VEC[name][0] + i, 1)]

    def part(x, i):
        return x[:, :, :].rearrange("p c t -> p (c t)")[:, ds(i * T, T)]

    def piece_scans(dve, l, i, k):
        dve.tensor_scalar(uk[:, k, :], part(fside, i), vec("u", NP * l + i), 30.0, ALU.add, ALU.min).then_inc(uk_ready, 1)
        dec = decay[:, ds(NP * l + i, 1)]
        for kind, src, back in ((0, ekv, ekv_back), (1, ek, ek_back)):
            dve.tensor_tensor_scan(scans[:, k, kind, 0, :], dec.to_broadcast([P, T]), part(src, i), 0.0, ALU.mult, ALU.add)
            ins = dve.tensor_tensor_scan(scans[:, k, kind, 1, 0:T - 1][:, ::-1], part(back, i)[:, 0:T - 1],
                                         dec.to_broadcast([P, T - 1]), 0.0, ALU.add, ALU.mult)
        ins.then_inc(scans_ready, 1)

    def piece_act(act, l, i, k):
        act.wait_ge(uk_ready, NP * l + i + 1)
        act.activation(terms[:, k, 1, :], uk[:, k, :], ACT.Exp).then_inc(euk_ready, 1)

    def piece_pool(pool, l, i, k):
        pool.wait_ge(euk_ready, NP * l + i + 1)
        pstep.mark(pool.tensor_tensor(terms[:, k, 0, :], terms[:, k, 1, :], part(fside, i), ALU.mult))
        pool.wait_ge(scans_ready, NP * l + i + 1)
        pstep.link(pool.tensor_tensor(sums[:, k, :, :], scans[:, k, :, 0, :], scans[:, k, :, 1, :], ALU.add))
        pool.tensor_tensor(sums[:, k, :, :], sums[:, k, :, :], terms[:, k, :, :], ALU.add).then_inc(sums_ready, 1)

    PIECE_POOL_STEPS = 2

    def piece_finish(dve, l, i, k):
        dve.wait_ge(sums_ready, NP * l + i + 1)
        den = sums[:, k, 1, :]
        dstep.link(dve.tensor_scalar(den, den, 1e-8, None, ALU.max))
        dstep.link(dve.reciprocal(den, den))
        dstep.mark(dve.tensor_tensor(part(mod[:, l % 2], i), sums[:, k, 0, :], den, ALU.mult))

    PIECE_DVE_STEPS = 3

    def block_dve(dve, l):
        for i in range(NP):
            piece_scans(dve, l, i, i % 2)
            if i:
                piece_finish(dve, l, i - 1, (i - 1) % 2)
        piece_finish(dve, l, NP - 1, (NP - 1) % 2)

    def block_act(act, l):
        for i in range(NP):
            piece_act(act, l, i, i % 2)

    def block_pool(pool, l):
        for i in range(NP):
            piece_pool(pool, l, i, i % 2)

    def condition_act(act, sig):
        act.activation(sig[:, :, :], xT[:, :, :], ACT.Sigmoid).then_inc(sig_ready, 1)

    def condition_dve(dve, l, sig):
        dve.wait_ge(sig_ready, l + 1)
        dstep.wait()
        for b in range(NB):
            c = slice(b * T, (b + 1) * T)
            ins = dve.scalar_tensor_tensor(out=xin[:, :, c], in0=sig[:, :, c], scalar=gain[:, b:b + 1],
                                           in1=mod[:, l % 2, :, c], op0=ALU.mult, op1=ALU.mult)
        ins.then_inc(xin_ready, 1)

    disp_dram = nc.dram_tensor("disp_scratch", (SLOTS, C), F32, kind="Internal").ap()
    eo_dram = nc.dram_tensor("expert_out_scratch", (SLOTS, C), F32, kind="Internal").ap()

    def stage_first():
        with ExitStack() as st:
            crep = st.enter_context(nc.sbuf_tensor("crep", [P, NB, 64], F32))
            small = st.enter_context(nc.sbuf_tensor("small", [P, 8 * NB], F32))
            wexp = st.enter_context(nc.sbuf_tensor("wexp", [P, 2, 2 * NL], F32))
            fmin = st.enter_context(nc.sbuf_tensor("fmin", [P, CH, NT], F32))
            s_vec, s_x, s_f, s_c, s_id = sem("ld_vecs"), sem("ld_x"), sem("ld_f"), sem("ld_cond"), sem("ld_ident")
            s_tfsum, s_tf, s_fmin, s_ek, s_wexp = (sem(n) for n in ("tf_sum", "tf", "f_min", "ek_rdy", "w_exp"))
            s_zero, s_back, s_blank, s_blanked = sem("zeroed"), sem("reversed"), sem("blank"), sem("slots_blanked")
            block = st.enter_context(nc.Block())

            @block.sync
            def _(sp):
                sp.dma_start(fside[:, :, :], io["fT"]).then_inc(s_f, 16)
                sp.dma_start(vecs[:, :], io["vecs"]).then_inc(s_vec, 16)
                sp.dma_start(crep[:, :, :], io["cond"]).then_inc(s_c, 16)
                sp.dma_start(xT[:, :, :], io["xT"]).then_inc(s_x, 16)
                sp.dma_start(ident[:, :], io["ident"]).then_inc(s_id, 16)
                sp.wait_ge(s_blank, 1)
                for i in range(2):
                    sp.dma_start(disp_dram.rearrange("(i p a) d -> i p (a d)", i=2, p=P)[i],
                                 xin[:, :, :].rearrange("p c t -> p (c t)")).then_inc(s_blanked, 16)
                sp.wait_ge(s_blanked, 32)
                sp.wait_ge(s_x, 16)
                sp.wait_ge(s_id, 16)

            @block.gpsimd
            def _(pool):
                pstep.link(pool.memset(scans[:, :, :, :, :], 0.0))
                pool.memset(xin[:, :, :], 0.0).then_inc(s_blank, 1)
                pool.wait_ge(s_ek, 1)
                pool.wait_ge(s_f, 16)
                pool.tensor_tensor(ekv[:, :, :], ek[:, :, :], fside[:, :, :], ALU.mult).then_inc(s_zero, 1)
                block_pool(pool, 0)

            @block.scalar
            def _(act):
                act.wait_ge(s_vec, 16)
                astep.link(act.activation(wexp[:, 0, :], vecs[:, 0:2 * NL], ACT.Exp))
                act.activation(wexp[:, 1, :], wexp[:, 0, :], ACT.Exp, scale=-1.0).then_inc(s_wexp, 1)
                act.wait_ge(s_fmin, 1)
                act.activation(ek[:, :, :], fmin[:, :, :], ACT.Exp).then_inc(s_ek, 1)
                back = lambda x: x[:, :, :].rearrange("p c (b t) -> p (c b) t", b=NB)[:, :, ::-1]
                ahead = lambda x: x[:, :, :].rearrange("p c (b t) -> p (c b) t", b=NB)
                act.activation(ahead(ek_back), back(fmin), ACT.Exp)
                act.wait_ge(s_tfsum, 1)
                act.activation(small[:, NB:2 * NB], small[:, 0:NB], ACT.Sigmoid).then_inc(s_tf, 1)
                act.wait_ge(s_zero, 1)
                act.activation(ahead(ekv_back), back(ekv), ACT.Identity).then_inc(s_back, 1)
                block_act(act, 0)

            @block.vector
            def _(dve):
                dve.wait_ge(s_f, 16)
                dve.tensor_scalar(fmin[:, :, :], fside[:, :, :], 30.0, None, ALU.min).then_inc(s_fmin, 1)
                dve.wait_ge(s_c, 16)
                dve.tensor_reduce(small[:, 0:NB], crep[:, :, :], AX_X, ALU.add).then_inc(s_tfsum, 1)
                dve.wait_ge(s_tf, 1)
                tf = small[:, NB:2 * NB]
                dve.tensor_scalar(gain[:, :], tf, 0.2, 0.8, ALU.mult, ALU.add)
                dstep.link(dve.tensor_scalar(small[:, 2 * NB:3 * NB], tf, 0.5, 0.5, ALU.mult, ALU.add))
                dve.wait_ge(s_wexp, 1)
                for b in range(NB):
                    ins = dve.tensor_scalar(decay[:, :].rearrange("p (c b) -> p c b", b=NB)[:, :, b], wexp[:, 1, :],
                                            small[:, 2 * NB + b:2 * NB + b + 1], None, ALU.mult)
                dstep.link(ins)
                dve.wait_ge(s_back, 1)
                block_dve(dve, 0)

    stage_first()

    def stage_l0_attn(l):
        NU = L0_GROUP * NB
        NPROJ = 4 + 2 * L0_GROUP
        with ExitStack() as st:
            def sb(name, shape, dt=F32):
                return st.enter_context(nc.sbuf_tensor(name, shape, dt))

            sig = sb("sigA", [P, CH, NT])
            wkvq = sb("wkvq", [P, 512 + 1024])
            wk = wkvq[:, 0:256].rearrange("p (k f) -> p k f", k=CH)
            wv = wkvq[:, 256:512].rearrange("p (k f) -> p k f", k=CH)
            wq = wkvq[:, 512:1536].rearrange("p (m k f) -> p m k f", m=L0_GROUP, k=CH)
            wo = sb("wo", [P, L0_GROUP, C])
            rope = sb("rope", [P, 2, T])
            mask = sb("mask", [P, T])
            kraw, kswap = sb("kraw", [P, NT]), sb("kswap", [P, NT])
            qraw, qswap = sb("qraw", [P, NT]), sb("qswap", [P, NT])
            t1, t2 = sb("t1", [P, NT]), sb("t2", [P, NT])
            kz = sb("kz", [P, NB, 2, T])
            vtok = sb("vtok", [P, 2 * NB, P])
            qr = sb("qr", [P, 2, NT])
            probs = sb("probs", [P, 4, 768])
            stats = sb("stats", [P, 4, 16])
            probT = sb("probT", [P, 2, 2, 384])
            oT = sb("oT", [P, L0_GROUP, NT])
            cols = sb("cols", [P, 9])
            colv = sb("colv", [P, 1])
            ps_s = st.enter_context(nc.psum_tensor("ps_s", [P, 2, 1024], F32))
            ps_t = st.enter_context(nc.psum_tensor("ps_t", [P, 2, 512], F32))
            ps_p = st.enter_context(nc.psum_tensor("ps_p", [P, HALF], F32))
            ps_o = st.enter_context(nc.psum_tensor("ps_o", [P, HALF], F32))
            names = ("w_kvq w_wo ld_rope proj_done proj_evac s_ready max_ready exp_done recip_ready norm_done "
                     "pt_ready pt_dve pt_act o_ready o_evac wo_done wo_added rope_done t1_ready swap_k swap_q "
                     "cols_ready colv_ready zeroed").split()
            s = {n: sem("A_" + n) for n in names}
            block = st.enter_context(nc.Block())
            LAST = L0_PAIRS - 1

            def proj_bank(g):
                return ps_o if g == 5 else ps_p

            def group(m):
                return 2 if m == 0 else 4 + 2 * m

            heads = lambda x, n: x.rearrange("p (b t) -> p b t", b=n)
            cosb = rope[:, 0:1, :].to_broadcast([P, NB, T])
            sinb = rope[:, 1:2, :].to_broadcast([P, NB, T])

            def scores(u):
                return (ps_s[:, u % 2, 0:512].rearrange("p (r t) -> p r t", r=2),
                        ps_s[:, u % 2, 512:768].rearrange("p (r t) -> p r t", r=2))

            def prob(u):
                return (probs[:, u % 4, 0:512].rearrange("p (r t) -> p r t", r=2),
                        probs[:, u % 4, 512:768].rearrange("p (r t) -> p r t", r=2))

            @block.sync
            def _(sp):
                def load_kvq(n):
                    need(sp, s["proj_done"], NPROJ * n)
                    sp.dma_start(wkvq[:, :], io["w_l0a"][n][:, 0:1536]).then_inc(s["w_kvq"], 16)

                def load_wo(n):
                    need(sp, s["wo_done"], 4 * n)
                    sp.dma_start(wo[:, :, :].rearrange("p m n -> p (m n)"),
                                 io["w_l0a"][n][:, 1536:2560]).then_inc(s["w_wo"], 16)

                def swap(n, j):
                    src, dst, done = (kraw, kswap, "swap_k") if j == 0 else (qraw, qswap, "swap_q")
                    sp.wait_ge(s["proj_evac"], NPROJ * n + (2 if j == 0 else group(j - 1) + 2))
                    for q in range(4):
                        sp.dma_start(dst[32 * q:32 * q + 32, :], src[32 * (q ^ 1):32 * (q ^ 1) + 32, :]) \
                            .then_inc(s[done], 16)

                def pair(c, more):
                    for j in range(2, 1 + L0_GROUP):
                        swap(c, j)
                    if more:
                        load_kvq(c + 1)
                        swap(c + 1, 0)
                        swap(c + 1, 1)
                        load_wo(c + 1)

                load_kvq(0)
                sp.dma_start(rope[:, :, :], io["rope"]).then_inc(s["ld_rope"], 16)
                sp.dma_start(mask[:, :], io["mask"]).then_inc(s["ld_rope"], 16)
                load_wo(0)
                swap(0, 0)
                swap(0, 1)
                with sp.Fori(0, LAST) as c:
                    pair(c, True)
                pair(LAST, False)

            @block.gpsimd
            def _(pool):
                def rope_cos(n, j):
                    src = kraw if j == 0 else qraw
                    pool.wait_ge(s["proj_evac"], NPROJ * n + (2 if j == 0 else group(j - 1) + 2))
                    pool.wait_ge(s["rope_done"], 5 * n + j + 1)
                    pool.tensor_tensor(heads(t1[:, :], NB), heads(src[:, :], NB), cosb, ALU.mult).then_inc(s["t1_ready"], 1)

                def pair(c, more):
                    for u in range(NU):
                        if u % NB == 1 and u < NU - NB:
                            rope_cos(c, 2 + u // NB)
                        pool.wait_ge(s["recip_ready"], NU * c + u + 1)
                        p1, p0 = prob(u)
                        rs = stats[:, u % 4, 12:16]
                        pstep.mark(pool.tensor_tensor(p1, p1, rs[:, 0:2].unsqueeze(2).to_broadcast([P, 2, T]), ALU.mult))
                        pool.tensor_tensor(p0, p0, rs[:, 2:4].unsqueeze(2).to_broadcast([P, 2, P]),
                                           ALU.mult).then_inc(s["norm_done"], 1)
                        if u in (6, 10):
                            piece_pool(pool, l + 1, 2 * c + u // 10, u // 10)
                    if more:
                        rope_cos(c + 1, 0)
                        rope_cos(c + 1, 1)

                pool.memset(kz[:, :, :, :], 0.0).then_inc(s["zeroed"], 1)
                pool.wait_ge(s["ld_rope"], 32)
                rope_cos(0, 0)
                rope_cos(0, 1)
                with pool.Fori(0, LAST) as c:
                    pstep.enter(c, 2 * PIECE_POOL_STEPS + NU)
                    pair(c, True)
                pstep.leave(LAST)
                pair(LAST, False)

            @block.scalar
            def _(act):
                def evac(n, g, out, **k):
                    act.wait_ge(s["proj_done"], NPROJ * n + g + 1)
                    act.activation(out, proj_bank(g)[:, :], ACT.Identity, **k).then_inc(s["proj_evac"], 1)

                def evac_k(n, h):
                    if h == 0:
                        act.wait_ge(s["cols_ready"], n + 1)
                        need(act, s["rope_done"], 5 * n - 3)
                    evac(n, h, kraw[:, h * HALF:(h + 1) * HALF], bias=cols[:, 0:1])

                def evac_q(n, m, h):
                    if h == 0:
                        act.wait_ge(s["rope_done"], 5 * n + (1 if m == 0 else m + 2))
                    evac(n, group(m) + h, qraw[:, h * HALF:(h + 1) * HALF], scale=cols[:, 1 + m:2 + m],
                         bias=cols[:, 5 + m:6 + m])

                def evac_v(n, h):
                    evac(n, 4 + h, vtok[:, NB * h:NB * h + NB, :].rearrange("p a f -> p (a f)"))

                def exps(c, u):
                    act.wait_ge(s["max_ready"], NU * c + u + 1)
                    for i in range(4):
                        src, dst = scores(u)[i // 2], prob(u)[i // 2]
                        ins = act.activation(dst[:, i % 2, :], src[:, i % 2, :], ACT.Exp,
                                             bias=stats[:, u % 4, 4 + i:5 + i], scale=-1.0,
                                             accum_out=stats[:, u % 4, 8 + i:9 + i])
                    ins.then_inc(s["exp_done"], 1)

                def pt_evac(c, u):
                    act.wait_ge(s["pt_ready"], NU * c + u + 1)
                    act.activation(probT[:, u % 2, 1, :], ps_t[:, 1, 0:384], ACT.Identity).then_inc(s["pt_act"], 1)

                def o_evac(c, u):
                    if u == 0:
                        act.wait_ge(s["colv_ready"], c + 1)
                    act.wait_ge(s["o_ready"], NU * c + u + 1)
                    act.activation(oT[:, u // NB, ds(u % NB * T, T)], ps_o[:, 0:T], ACT.Identity,
                                   bias=colv[:, :]).then_inc(s["o_evac"], 1)

                def pair(c, more):
                    for u in range(NU):
                        exps(c, u)
                        if u % NB < 2 and u < NU - NB:
                            evac_q(c, u // NB + 1, u % NB)
                        if u in (3, 7):
                            piece_act(act, l + 1, 2 * c + u // 7, u // 7)
                        if u >= 2:
                            pt_evac(c, u - 2)
                        if u >= 3:
                            o_evac(c, u - 3)
                    if more:
                        evac_k(c + 1, 0)
                    pt_evac(c, NU - 2)
                    if more:
                        evac_k(c + 1, 1)
                    o_evac(c, NU - 3)
                    if more:
                        evac_q(c + 1, 0, 0)
                    pt_evac(c, NU - 1)
                    o_evac(c, NU - 2)
                    if more:
                        evac_q(c + 1, 0, 1)
                    o_evac(c, NU - 1)
                    if more:
                        evac_v(c + 1, 0)
                        evac_v(c + 1, 1)

                act.sem_inc(s["exp_done"], 2)
                act.sem_inc(s["pt_act"], 1)
                act.sem_inc(s["o_evac"], 1)
                condition_act(act, sig)
                for h in range(2):
                    evac_k(0, h)
                for h in range(2):
                    evac_q(0, 0, h)
                for h in range(2):
                    evac_v(0, h)
                with act.Fori(0, LAST) as c:
                    pair(c, True)
                pair(LAST, False)

            @block.vector
            def _(dve):
                def columns_kq(n):
                    need(dve, s["proj_evac"], NPROJ * n)
                    dve.tensor_scalar(cols[:, 0:1], vec("bk", n), 1.0, None, ALU.mult)
                    four = lambda v: vecs[:, ds(4 * n + VEC[v][0], 4)]
                    dstep.link(dve.tensor_scalar(cols[:, 1:5], four("kw"), HD ** -0.5, None, ALU.mult))
                    dve.tensor_tensor(cols[:, 5:9], cols[:, 1:5], four("bq"), ALU.mult).then_inc(s["cols_ready"], 1)

                def column_v(n):
                    dve.wait_ge(s["o_evac"], NU * n + 1)
                    dve.tensor_scalar(colv[:, :], vec("bv", n), 1.0, None, ALU.mult).then_inc(s["colv_ready"], 1)

                def rope_sum(n, j):
                    swapped, done, count = (kswap, "swap_k", n + 1) if j == 0 else (qswap, "swap_q", 4 * n + j)
                    dve.wait_ge(s["rope_done"], 5 * n + j + 1)
                    dve.wait_ge(s[done], 64 * count)
                    dstep.link(dve.tensor_tensor(heads(t2[:, :], NB), heads(swapped[:, :], NB), sinb, ALU.mult))
                    dve.wait_ge(s["t1_ready"], 5 * n + j + 1)
                    if j == 0:
                        need(dve, s["s_ready"], NU * n)
                        for r in range(2):
                            h = slice(64 * r, 64 * r + 64)
                            ins = dve.tensor_tensor(kz[h, :, r, :], heads(t1[h, :], NB), heads(t2[h, :], NB), ALU.add)
                    else:
                        if j != 2:
                            need(dve, s["s_ready"], NU * n + NB * (j - 2))
                        ins = dve.tensor_tensor(qr[:, (j - 1) % 2, :], t1[:, :], t2[:, :], ALU.add)
                    ins.then_inc(s["rope_done"], 1)

                def max_rows(c, u):
                    dve.wait_ge(s["s_ready"], NU * c + u + 1)
                    dve.memset(stats[:, u % 4, 0:1], 0.0)
                    for i in range(4):
                        view, m = scores(u)[i // 2][:, i % 2, :], mask[:, 0:T] if i < 2 else mask[:, P:T]
                        ins = dve.tensor_tensor_reduce(out=view, in0=view, in1=m, scale=-1.0, scalar=-NEG, op0=ALU.add,
                                                       op1=ALU.min, accum_out=stats[:, u % 4, 4 + i:5 + i])
                    ins.then_inc(s["max_ready"], 1)

                def recip(c, u):
                    dve.wait_ge(s["exp_done"], NU * c + u + 3)
                    dve.reciprocal(stats[:, u % 4, 12:16], stats[:, u % 4, 8:12]).then_inc(s["recip_ready"], 1)

                def pt_evac(c, u):
                    dve.wait_ge(s["pt_ready"], NU * c + u + 1)
                    dve.tensor_copy(probT[:, u % 2, 0, :], ps_t[:, 0, 0:384]).then_inc(s["pt_dve"], 1)

                def pair(c, more):
                    for u in range(NU):
                        max_rows(c, u)
                        if u >= 1:
                            recip(c, u - 1)
                        if u >= 2:
                            pt_evac(c, u - 2)
                        if u % NB == 3 and u < NU - NB:
                            rope_sum(c, 2 + u // NB)
                        if u in (3, 7):
                            piece_scans(dve, l + 1, 2 * c + u // 7, u // 7)
                        if u in (9, 13):
                            piece_finish(dve, l + 1, 2 * c + u // 13, u // 13)
                        if u == 13 and more:
                            columns_kq(c + 1)
                    recip(c, NU - 1)
                    pt_evac(c, NU - 2)
                    pt_evac(c, NU - 1)
                    if more:
                        rope_sum(c + 1, 0)
                        rope_sum(c + 1, 1)
                    for j in range(4):
                        dve.wait_ge(s["wo_done"], 4 * c + j + 1)
                        half, ch = j % 2, j // 2
                        x = xT[:, ch, half * HALF:(half + 1) * HALF]
                        dve.tensor_tensor(x, x, (ps_o if j % 2 else ps_p)[:, :], ALU.add).then_inc(s["wo_added"], 1)
                    if more:
                        column_v(c + 1)

                dve.sem_inc(s["rope_done"], 1)
                dve.sem_inc(s["pt_dve"], 1)
                dve.sem_inc(s["wo_added"], 1)
                columns_kq(0)
                column_v(0)
                condition_dve(dve, l, sig)
                for ch in range(CH):
                    dstep.link(dve.tensor_scalar(xT[:, ch, :], xT[:, ch, :], vec("bo0", ch), None, ALU.add))
                dve.wait_ge(s["ld_rope"], 32)
                dve.wait_ge(s["zeroed"], 1)
                rope_sum(0, 0)
                rope_sum(0, 1)
                with dve.Fori(0, LAST) as c:
                    dstep.enter(c, 2 * PIECE_DVE_STEPS + 1 + L0_GROUP + 1)
                    pair(c, True)
                dstep.leave(LAST)
                pair(LAST, False)

            @block.tensor
            def _(pe):
                def project(n, g, w, h):
                    need(pe, s["proj_evac"], NPROJ * n + g)
                    for k in range(CH):
                        ins = pe.matmul(proj_bank(g)[:, :], w[:, k, :], xin[:, k, h * HALF:(h + 1) * HALF],
                                        start=(k == 0), stop=(k == CH - 1))
                    ins.then_inc(s["proj_done"], 1)

                def project_q(n, m, h):
                    project(n, group(m) + h, wq[:, m], h)

                def project_v(n, h):
                    need(pe, s["proj_evac"], NPROJ * n + 4)
                    if h == 1:
                        pe.wait_ge(s["o_evac"], NU * n + 1)
                    for t in range(NB):
                        for k in range(CH):
                            ins = pe.matmul(proj_bank(4 + h)[:, t * P:(t + 1) * P],
                                            xin[:, k, h * HALF + t * P:h * HALF + t * P + P], wv[:, k, :],
                                            start=(k == 0), stop=(k == CH - 1))
                    ins.then_inc(s["proj_done"], 1)

                def score(c, u):
                    m, b = divmod(u, NB)
                    if b == 0:
                        pe.wait_ge(s["rope_done"], 5 * c + m + 3)
                    pe.wait_ge(s["exp_done"], NU * c + u + 1)
                    for tile, view in zip((1, 0), scores(u)):
                        n = T if tile else P
                        ins = pe.matmul(view, qr[:, m % 2, b * T + tile * P:b * T + tile * P + P],
                                        kz[:, b, :, 0:n], start=True, stop=True)
                    ins.then_inc(s["s_ready"], 1)

                def turn(c, u):
                    pe.wait_ge(s["norm_done"], NU * c + u + 1)
                    pe.wait_ge(s["pt_dve"], NU * c + u + 1)
                    pe.wait_ge(s["pt_act"], NU * c + u + 1)
                    p1, p0 = prob(u)
                    for r in range(2):
                        pe.transpose(ps_t[:, r, 0:128], p0[:, r, :], ident[:, :])
                        pe.transpose(ps_t[:, r, 128:256], p1[:, r, 0:128], ident[:, :])
                        ins = pe.transpose(ps_t[:, r, 256:384], p1[:, r, 128:256], ident[:, :])
                    ins.then_inc(s["pt_ready"], 1)

                def weigh(c, u):
                    b = u % NB
                    if u == 0:
                        pe.wait_ge(s["proj_evac"], NPROJ * c + 6)
                        pe.wait_ge(s["wo_added"], 4 * c + 1)
                    pe.wait_ge(s["pt_dve"], NU * c + u + 2)
                    pe.wait_ge(s["pt_act"], NU * c + u + 2)
                    pe.wait_ge(s["o_evac"], NU * c + u + 1)
                    for key in range(2):
                        for r in range(2):
                            o = ps_o[64 * r:64 * r + 64, key * P:T]
                            ins = pe.matmul(o, vtok[:, 2 * b + key, 64 * r:64 * r + 64],
                                            probT[:, u % 2, r, 0:256] if key == 0 else probT[:, u % 2, r, 256:384],
                                            start=(key == 0), stop=(key == 1), skip_group_check=True)
                    ins.then_inc(s["o_ready"], 1)

                def pair(c, more):
                    n = c + 1
                    for u in range(NU):
                        score(c, u)
                        if u == 0:
                            pe.wait_ge(s["wo_added"], 4 * c + 1)
                        if u % NB < 2 and u < NU - NB:
                            project_q(c, u // NB + 1, u % NB)
                        if u >= 2:
                            turn(c, u - 2)
                        if u >= 3:
                            weigh(c, u - 3)
                    if more:
                        pe.wait_ge(s["w_kvq"], 16 * n + 16)
                        project(n, 0, wk, 0)
                    turn(c, NU - 2)
                    if more:
                        project(n, 1, wk, 1)
                    weigh(c, NU - 3)
                    if more:
                        project_q(n, 0, 0)
                    turn(c, NU - 1)
                    weigh(c, NU - 2)
                    if more:
                        project_q(n, 0, 1)
                    weigh(c, NU - 1)
                    if more:
                        project_v(n, 0)
                        project_v(n, 1)
                    pe.wait_ge(s["w_wo"], 16 * c + 16)
                    pe.wait_ge(s["o_evac"], NU * c + NU + 1)
                    for j in range(4):
                        half, ch = j % 2, j // 2
                        if j >= 2:
                            pe.wait_ge(s["wo_added"], 4 * c + j)
                        elif more:
                            pe.wait_ge(s["proj_evac"], NPROJ * n + 5 + j)
                        elif j == 0:
                            pe.wait_ge(s["proj_evac"], NPROJ * c + NPROJ)
                        for m in range(L0_GROUP):
                            ins = pe.matmul((ps_o if j % 2 else ps_p)[:, :], wo[:, m, ch * P:(ch + 1) * P],
                                            oT[:, m, half * HALF:(half + 1) * HALF],
                                            start=(m == 0), stop=(m == L0_GROUP - 1))
                        ins.then_inc(s["wo_done"], 1)

                pe.wait_ge(s["w_kvq"], 16)
                pe.wait_ge(xin_ready, l + 1)
                for h in range(2):
                    project(0, h, wk, h)
                for h in range(2):
                    project_q(0, 0, h)
                for h in range(2):
                    project_v(0, h)
                with pe.Fori(0, LAST) as c:
                    pair(c, True)
                pair(LAST, False)

    def route_act(act, lt, n):
        act.wait_ge(sub_ready, n)
        act.activation(lt[:, 1, :, :], lt[:, 1, :, :], ACT.Exp).then_inc(exp_ready, 1)

    def route_dve(dve, lt, one, rank, n):
        bc = lambda v: v.unsqueeze(2).to_broadcast([P, 8, NE])
        dstep.link(dve.tensor_reduce(one[:, 2, :], lt[:, 0, :, :], AX_X, ALU.max))
        dve.tensor_tensor(lt[:, 1, :, :], lt[:, 0, :, :], bc(one[:, 2, :]), ALU.subtract).then_inc(sub_ready, 1)
        dve.wait_ge(exp_ready, n)
        dstep.link(dve.tensor_reduce(one[:, 3, :], lt[:, 1, :, :], AX_X, ALU.add))
        dstep.link(dve.reciprocal(one[:, 3, :], one[:, 3, :]))
        dstep.link(dve.tensor_tensor(lt[:, 1, :, :], lt[:, 1, :, :], bc(one[:, 3, :]), ALU.mult))
        for k in range(2):
            p, hot = lt[:, 1, :, :], lt[:, 2 + k, :, :]
            dstep.link(dve.tensor_reduce(one[:, k, :], p, AX_X, ALU.max))
            dstep.link(dve.tensor_tensor(hot, p, bc(one[:, k, :]), ALU.is_equal))
            dstep.link(dve.tensor_tensor(hot, hot, rank, ALU.mult))
            dstep.link(dve.tensor_reduce(one[:, 2, :], hot, AX_X, ALU.max))
            dstep.link(dve.tensor_tensor(hot, hot, bc(one[:, 2, :]), ALU.is_equal))
            if k == 0:
                dstep.link(dve.scalar_tensor_tensor(out=p, in0=hot, scalar=-2.0, in1=p, op0=ALU.mult, op1=ALU.add))

    moe_names = ("ld_gate router_done shared_ready comb_ready rows_done rows_ready gu_done silu_done prod_ready "
                 "hid_ready down_done gu0 gu1 gu2 gu3 dn0 dn1 dn2 dn3").split()
    moe_sems = {n: sem("moe_" + n) for n in moe_names}
    moe_left = {n: 0 for n in moe_names}

    def stage_moe(l, name):
        NE_CH = EH * NE // P
        NCH = NE_CH + -(-(L0_SH if name == "L0" else L3_SH) // P)
        SLOT = 4
        more = l + 1 < NL
        with ExitStack() as st:
            def sb(n, shape, dt=F32):
                return st.enter_context(nc.sbuf_tensor(name + n, shape, dt))

            sig = sb("sig", [P, CH, NT])
            wgate = sb("wgate", [P, CH, NE + 1])
            wgu = sb("wgu", [P, SLOT, 2 * C])
            wdn = sb("wdn", [P, SLOT, C])
            rank = sb("rank", [P, 8, NE])
            lt = sb("lt", [P, 4, 8, NE])
            one = sb("one", [P, 6, 8])
            wide = sb("wide", [P, 2, 8, P])
            rowsb = sb("rows", [P, 2, NT])
            act_g = sb("actg", [P, 2, HALF])
            hid = sb("hid", [P, NCH, NT])
            ps_y = st.enter_context(nc.psum_tensor(name + "ps_y", [P, CH, 2, HALF], F32))
            ps_g = st.enter_context(nc.psum_tensor(name + "ps_g", [P, 2, HALF], F32))
            ps_u = st.enter_context(nc.psum_tensor(name + "ps_u", [P, 2, HALF], F32))
            s = moe_sems
            block = st.enter_context(nc.Block())

            def after(eng, n, count):
                if not isinstance(count, int) or count > 0:
                    eng.wait_ge(s[n], moe_left[n] + count)

            def fours(eng, body, mid=None):
                for ch in range(SLOT):
                    body(ch, ch, 0)
                    if mid and ch == 1:
                        mid()
                with eng.Fori(1, NCH // SLOT) as i:
                    for k in range(SLOT):
                        body(SLOT * i + k, k, i)
                for ch in range(NCH // SLOT * SLOT, NCH):
                    body(ch, ch % SLOT, ch // SLOT)

            def pairs(eng, body, before, behind, steps=None, per=0):
                n = NCH // 2

                def pair(i):
                    before(i)
                    for k in range(2):
                        body(2 * i + k)
                    behind(i)

                pair(0)
                with eng.Fori(1, n) as i:
                    if steps:
                        steps.enter(i - 1, per)
                    pair(i)
                if steps:
                    steps.leave(n - 1)
                if NCH % 2:
                    body(NCH - 1)
                for i in range(n, NP):
                    before(i)
                    behind(i)

            @block.sync
            def _(sp):
                sp.dma_start(wgate[:, :, :], io[name + "_gate"]).then_inc(s["ld_gate"], 16)
                sp.dma_start(rank[:, :, :], io["rank"]).then_inc(s["ld_gate"], 16)

                def load_gu(ch, k, n):
                    after(sp, "gu_done", 2 * (ch - SLOT + 1))
                    sp.dma_start(wgu[:, k, :], io[name + "_w"][ch][:, 0:2 * C]).then_inc(s[f"gu{k}"], 16)

                def load_dn(ch, k, n):
                    after(sp, "down_done", ch - SLOT + 1)
                    sp.dma_start(wdn[:, k, :], io[name + "_w"][ch][:, 2 * C:3 * C]).then_inc(s[f"dn{k}"], 16)

                fours(sp, load_gu)
                fours(sp, load_dn)

            @block.gpsimd
            def _(pool):
                def weigh(ch, which):
                    after(pool, "prod_ready", 2 * ch + 2)
                    h = hid[:, ds(ch, 1), :].rearrange("p a t -> p (a t)")
                    pool.tensor_tensor(h, h, rowsb[:, which, :], ALU.mult).then_inc(s["hid_ready"], 1)

                def piece(i):
                    if more:
                        piece_pool(pool, l + 1, i, 0)

                half = NE_CH // 2
                piece(0)
                after(pool, "rows_ready", 1)
                for ch in range(2):
                    weigh(ch, 0)
                with pool.Fori(1, half) as i:
                    pstep.enter(i - 1, PIECE_POOL_STEPS if more else 0)
                    piece(i)
                    for k in range(2):
                        weigh(2 * i + k, 0)
                pstep.leave(half - 1)
                weigh(NE_CH - 1, 0)
                for i in range(half, NP):
                    piece(i)
                with pool.Fori(NE_CH, NCH) as ch:
                    weigh(ch, 1)

            @block.scalar
            def _(act):
                condition_act(act, sig)
                route_act(act, lt, l // 6 * 2 + 1)
                after(act, "router_done", 1)
                logits = ps_y[:, 0, 0, 0:8 * (NE + 1)].rearrange("p (t e) -> p t e", t=8)
                act.activation(wide[:, 1, :, :], logits[:, :, NE:NE + 1].to_broadcast([P, 8, P]),
                               ACT.Sigmoid).then_inc(s["shared_ready"], 1)

                def silu(ch):
                    for h in range(2):
                        after(act, "gu_done", 2 * ch + h + 1)
                        after(act, "prod_ready", 2 * ch + h - 1)
                        act.activation(act_g[:, h, :], ps_g[:, h, :], ACT.Silu).then_inc(s["silu_done"], 1)

                def piece(i):
                    if more:
                        piece_act(act, l + 1, i, 0)

                def rows(i):
                    if isinstance(i, int) and i == 0:
                        after(act, "rows_done", 1)
                        for j in range(2):
                            ins = act.activation(rowsb[:, j, :], ps_y[:, j, :, :].rearrange("p a t -> p (a t)"), ACT.Identity)
                        ins.then_inc(s["rows_ready"], 1)

                pairs(act, silu, piece, rows)

            @block.vector
            def _(dve):
                condition_dve(dve, l, sig)
                after(dve, "router_done", 1)
                after(dve, "ld_gate", 32)
                logits = ps_y[:, 0, 0, 0:8 * (NE + 1)].rearrange("p (t e) -> p t e", t=8)
                dstep.link(dve.tensor_copy(lt[:, 0, :, :], logits[:, :, 0:NE]))
                route_dve(dve, lt, one, rank[:, :, :], l // 6 * 2 + 1)
                bc = lambda v: v.unsqueeze(2).to_broadcast([P, 8, NE])
                dstep.link(dve.tensor_tensor(one[:, 2, :], one[:, 0, :], one[:, 1, :], ALU.add))
                dstep.link(dve.reciprocal(one[:, 2, :], one[:, 2, :]))
                for k in range(2):
                    dstep.link(dve.tensor_tensor(one[:, 4 + k, :], one[:, k, :], one[:, 2, :], ALU.mult))
                    dstep.link(dve.tensor_tensor(lt[:, 2 + k, :, :], lt[:, 2 + k, :, :], bc(one[:, 4 + k, :]), ALU.mult))
                w16 = [lt[:, 2 + k, :, :].rearrange("p t e -> p (t e)").unsqueeze(2).to_broadcast([P, 8 * NE, P // NE])
                       for k in range(2)]
                dve.tensor_tensor(wide[:, 0, :, :].rearrange("p t (e i) -> p (t e) i", e=NE), w16[0], w16[1],
                                  ALU.add).then_inc(s["comb_ready"], 1)

                def multiply(ch):
                    for h in range(2):
                        after(dve, "silu_done", 2 * ch + h + 1)
                        dve.tensor_tensor(hid[:, ds(ch, 1), h * HALF:(h + 1) * HALF].rearrange("p a t -> p (a t)"),
                                          act_g[:, h, :], ps_u[:, h, :], ALU.mult).then_inc(s["prod_ready"], 1)

                def scans_of(i):
                    if more:
                        piece_scans(dve, l + 1, i, 0)

                def finish_of(i):
                    if more:
                        piece_finish(dve, l + 1, i, 0)

                pairs(dve, multiply, scans_of, finish_of, dstep, PIECE_DVE_STEPS if more else 0)
                after(dve, "down_done", NCH)
                for ch in range(CH):
                    x = xT[:, ch, :]
                    dstep.link(dve.tensor_tensor(x, x, ps_y[:, ch, :, :].rearrange("p a t -> p (a t)"), ALU.add))

            @block.tensor
            def _(pe):
                after(pe, "ld_gate", 32)
                pe.wait_ge(xin_ready, l + 1)
                for t in range(8):
                    for k in range(CH):
                        ins = pe.matmul(ps_y[:, 0, 0, t * (NE + 1):(t + 1) * (NE + 1)], xin[:, k, t * P:(t + 1) * P],
                                        wgate[:, k, :], start=(k == 0), stop=(k == CH - 1))
                ins.then_inc(s["router_done"], 1)

                def gate_up(ch, k, n):
                    after(pe, f"gu{k}", 16 * n + 16)
                    for h in range(2):
                        after(pe, "prod_ready", 2 * ch + h - 1)
                        for ps, o in ((ps_g, 0), (ps_u, C)):
                            for i in range(CH):
                                ins = pe.matmul(ps[:, h, :], wgu[:, k, o + i * P:o + (i + 1) * P],
                                                xin[:, i, h * HALF:(h + 1) * HALF], start=(i == 0), stop=(i == CH - 1))
                        ins.then_inc(s["gu_done"], 1)

                def rows():
                    after(pe, "comb_ready", 1)
                    after(pe, "shared_ready", 1)
                    for j in range(2):
                        for t in range(8):
                            ins = pe.transpose(ps_y[:, j, t // 4, t % 4 * P:t % 4 * P + P], wide[:, j, t, :], ident[:, :])
                    ins.then_inc(s["rows_done"], 1)

                def down(ch, k, n):
                    after(pe, f"dn{k}", 16 * n + 16)
                    after(pe, "hid_ready", ch + 1)
                    first, last = (isinstance(ch, int) and ch == c for c in (0, NCH - 1))
                    if first:
                        after(pe, "rows_ready", 1)
                    for h in range(2):
                        for m in range(CH):
                            ins = pe.matmul(ps_y[:, m, h, :], wdn[:, k, m * P:(m + 1) * P],
                                            hid[:, ds(ch, 1), h * HALF:(h + 1) * HALF].rearrange("p a t -> p (a t)"),
                                            start=first, stop=last)
                    ins.then_inc(s["down_done"], 1)

                fours(pe, gate_up, rows)
                fours(pe, down)

            left = {n: 1 for n in ("router_done", "shared_ready", "comb_ready", "rows_done", "rows_ready")}
            left.update(ld_gate=32, gu_done=2 * NCH, silu_done=2 * NCH, prod_ready=2 * NCH, hid_ready=NCH, down_done=NCH)
            for k in range(SLOT):
                left[f"gu{k}"] = left[f"dn{k}"] = 16 * len(range(k, NCH, SLOT))
            for n in moe_left:
                moe_left[n] += left[n]


    def stage_l1_attn(l):
        TP = T + 6
        RC = 3
        rows = (P, P, R1 - 2 * P)
        with ExitStack() as st:
            def sb(n, shape, dt=F32):
                return st.enter_context(nc.sbuf_tensor("R_" + n, shape, dt))

            sig = sb("sig", [P, CH, NT])
            w1 = sb("w1", [P, CH, RC * P])
            wconv = sb("wconv", [P, 10, R1])
            wgate = sb("wgate", [P, 2, RC, R1])
            w2 = sb("w2", [P, RC, C])
            hid = sb("hid", [P, CH, NB, TP])
            hid2 = sb("hid2", [P, NB, TP])
            conv = sb("conv", [P, RC, NT])
            rec = sb("rec", [P, RC, NT])
            inp = sb("inp", [P, RC, NT])
            mul = sb("mul", [P, RC, NT])
            lam = sb("lam", [P, 6, RC])
            ps = st.enter_context(nc.psum_tensor("R_ps", [P, 8, HALF], F32))
            names = ("ld_w1 ld_conv ld_gate ld_w2 zeroed done evac lam_ln "
                     "lam_ready a2_ready one_minus root_ready ix_ready scan_ready out_read").split()
            s = {n: sem("R_" + n) for n in names}
            block = st.enter_context(nc.Block())
            G_CONV, G_GATE, G_OUT = 6, 12, 24
            h512 = lambda h: slice(h * HALF, (h + 1) * HALF)

            @block.sync
            def _(sp):
                sp.dma_start(w1[:, :, :], io["l1_w1"]).then_inc(s["ld_w1"], 16)
                sp.dma_start(wconv[:, :, :], io["l1_conv"]).then_inc(s["ld_conv"], 16)
                sp.dma_start(wgate[:, :, :, :], io["l1_gate"]).then_inc(s["ld_gate"], 16)
                sp.dma_start(w2[:, :, :], io["l1_w2"]).then_inc(s["ld_w2"], 16)

            @block.gpsimd
            def _(pool):
                pool.memset(hid[:, :, :, :], 0.0)
                pstep.link(pool.memset(hid2[:, :, :], 0.0))
                pstep.link(pool.memset(conv[64:P, 2, :], 0.0))
                pool.memset(inp[64:P, 2, :], 0.0).then_inc(s["zeroed"], 1)
                for h in range(2):
                    pool.wait_ge(s["evac"], G_GATE + 6 * (h + 1))
                    for f in range(RC):
                        n = rows[f]
                        ins = pool.tensor_tensor(inp[0:n, f, h512(h)], inp[0:n, f, h512(h)], conv[0:n, f, h512(h)], ALU.mult)
                        if f == RC - 2:
                            pstep.link(ins)
                    ins.then_inc(s["ix_ready"], 1)
                    pool.wait_ge(s["ix_ready"], h + 1)
                block_pool(pool, l + 1)

            @block.scalar
            def _(act):
                condition_act(act, sig)
                astep.link(act.activation(lam[:, 0, :], vecs[:, VEC["lam"][0]:VEC["lam"][0] + RC], ACT.Abs))
                astep.link(act.activation(lam[:, 1, :], lam[:, 0, :], ACT.Exp, scale=-1.0))
                act.activation(lam[:, 2, :], lam[:, 1, :], ACT.Ln, bias=1.0).then_inc(s["lam_ln"], 1)
                act.wait_ge(s["zeroed"], 1)
                pair = lambda x: x.rearrange("p (b t) -> p b t", b=2)
                for h in range(2):
                    for f in range(RC):
                        g = 3 * h + f
                        act.wait_ge(s["done"], g + 1)
                        if f < 2:
                            ins = act.activation(hid[:, f, 2 * h:2 * h + 2, 3:3 + T], pair(ps[:, g, :]), ACT.Silu, bias=vec("b1", f))
                        else:
                            act.activation(hid2[0:64, 2 * h:2 * h + 2, 3:3 + T], pair(ps[0:64, g, :]), ACT.Silu,
                                           bias=vec("b1", f)[0:64, :])
                            ins = act.activation(hid2[64:P, 2 * h:2 * h + 2, 1:1 + T], pair(ps[64:P, g, :]), ACT.Silu,
                                                 bias=vec("b1", f)[64:P, :])
                        ins.then_inc(s["evac"], 1)
                for h in range(2):
                    for f in range(RC):
                        g, n = G_CONV + 3 * h + f, rows[f]
                        act.wait_ge(s["done"], g + 1)
                        act.activation(conv[0:n, f, h512(h)], ps[0:n, g % 8, :], ACT.Identity,
                                       bias=vec("convb", f)[0:n, :]).then_inc(s["evac"], 1)
                for h in range(2):
                    for f in range(RC):
                        for j, (dst, b) in enumerate(((rec, "ba"), (inp, "bx"))):
                            g, n = G_GATE + 6 * h + 2 * f + j, rows[f]
                            act.wait_ge(s["done"], g + 1)
                            act.activation(dst[0:n, f, h512(h)], ps[0:n, g % 8, :], ACT.Sigmoid,
                                           bias=vec(b, f)[0:n, :]).then_inc(s["evac"], 1)
                act.wait_ge(s["lam_ready"], 1)
                act.wait_ge(s["evac"], G_OUT)
                for h in range(2):
                    for f in range(RC):
                        n = rows[f]
                        astep.mark(act.activation(mul[0:n, f, h512(h)], rec[0:n, f, h512(h)], ACT.Exp, scale=lam[0:n, 5, f:f + 1]))
                    astep.wait()
                    for f in range(RC):
                        n = rows[f]
                        ins = act.activation(rec[0:n, f, h512(h)], rec[0:n, f, h512(h)], ACT.Exp, scale=lam[0:n, 4, f:f + 1])
                    ins.then_inc(s["a2_ready"], 1)
                for h in range(2):
                    act.wait_ge(s["one_minus"], h + 1)
                    for f in range(RC):
                        n = rows[f]
                        ins = act.activation(mul[0:n, f, h512(h)], mul[0:n, f, h512(h)], ACT.Sqrt, bias=1.0)
                    ins.then_inc(s["root_ready"], 1)
                block_act(act, l + 1)

            @block.vector
            def _(dve):
                lv = vecs[:, VEC["lam"][0]:VEC["lam"][0] + RC]
                condition_dve(dve, l, sig)
                dstep.link(dve.tensor_scalar(lam[:, 3, :], lv, 0.0, None, ALU.max))
                dve.wait_ge(s["lam_ln"], 1)
                dstep.link(dve.tensor_tensor(lam[:, 3, :], lam[:, 3, :], lam[:, 2, :], ALU.add))
                dstep.mark(dve.tensor_scalar(lam[:, 4, :], lam[:, 3, :], -8.0, None, ALU.mult))
                dve.tensor_scalar(lam[:, 5, :], lam[:, 3, :], -16.0, None, ALU.mult).then_inc(s["lam_ready"], 1)
                for h in range(2):
                    dve.wait_ge(s["a2_ready"], h + 1)
                    for f in range(RC):
                        n = rows[f]
                        ins = dve.tensor_scalar(mul[0:n, f, h512(h)], mul[0:n, f, h512(h)], 1.0, -1.0, ALU.min, ALU.mult)
                    ins.then_inc(s["one_minus"], 1)
                for h in range(2):
                    dve.wait_ge(s["root_ready"], h + 1)
                    dve.wait_ge(s["ix_ready"], h + 1)
                    for f in range(RC):
                        n = rows[f]
                        dstep.link(dve.tensor_tensor(mul[0:n, f, h512(h)], mul[0:n, f, h512(h)], inp[0:n, f, h512(h)], ALU.mult))
                    for f in range(RC):
                        n = rows[f]
                        for b in (2 * h, 2 * h + 1):
                            c = slice(b * T, (b + 1) * T)
                            ins = dve.tensor_tensor_scan(inp[0:n, f, c], rec[0:n, f, c], mul[0:n, f, c], 0.0, ALU.mult, ALU.add)
                    ins.then_inc(s["scan_ready"], 1)
                for h in range(2):
                    for m in range(CH):
                        dve.wait_ge(s["done"], G_OUT + 2 * h + m + 1)
                        x = xT[:, m, h512(h)]
                        dstep.link(dve.scalar_tensor_tensor(out=x, in0=ps[:, (G_OUT + 2 * h + m) % 8, :], scalar=vec("b2", m),
                                                            in1=x, op0=ALU.add, op1=ALU.add))
                block_dve(dve, l + 1)

            @block.tensor
            def _(pe):
                group = [0]

                def product(pairs, n):
                    g = group[0]
                    group[0] += 1
                    if g >= 8:
                        pe.wait_ge(s["evac"], g - 7)
                    for i, (w, x) in enumerate(pairs):
                        ins = pe.matmul(ps[0:n, g % 8, :], w, x, start=(i == 0), stop=(i == len(pairs) - 1))
                    ins.then_inc(s["done"], 1)

                pe.wait_ge(s["ld_w1"], 16)
                pe.wait_ge(xin_ready, l + 1)
                for h in range(2):
                    for f in range(RC):
                        product([(w1[:, k, f * P:(f + 1) * P], xin[:, k, h512(h)]) for k in range(CH)], P)
                pe.wait_ge(s["ld_conv"], 16)
                for h in range(2):
                    pe.wait_ge(s["evac"], 3 * (h + 1))
                    b = slice(2 * h, 2 * h + 2)
                    for f in range(RC):
                        c = slice(f * P, f * P + rows[f])
                        product([(wconv[:, 2 * k + i, c], hid[:, i, b, 2 * k:2 * k + T]) for k in range(TAPS) for i in range(CH)]
                                + [(wconv[:, 8 + q, c], hid2[:, b, 4 * q:4 * q + T]) for q in range(2)], rows[f])
                pe.wait_ge(s["ld_gate"], 16)
                for h in range(2):
                    pe.wait_ge(s["evac"], G_CONV + 3 * (h + 1))
                    for f in range(RC):
                        c = slice(f * P, f * P + rows[f])
                        for j in range(2):
                            product([(wgate[:, j, k, c], conv[:, k, h512(h)]) for k in range(RC)], rows[f])
                pe.wait_ge(s["ld_w2"], 16)
                for h in range(2):
                    pe.wait_ge(s["scan_ready"], h + 1)
                    for m in range(CH):
                        product([(w2[:, k, m * P:(m + 1) * P], inp[:, k, h512(h)]) for k in range(RC)], P)


    def stage_l1_ffn(l):
        HC = FF // P
        with ExitStack() as st:
            def sb(n, shape, dt=F32):
                return st.enter_context(nc.sbuf_tensor("E_" + n, shape, dt))

            tok = sb("tok", [P, 8, C])
            sig = tok[:, :, :].rearrange("p a b -> p (a b)").rearrange("p (c t) -> p c t", c=CH)
            wgate = sb("wgate", [P, CH, NE])
            rank = sb("rank", [P, 8, NE])
            base = sb("base", [NE, 4])
            lt = sb("lt", [P, 4, 8, NE])
            one = sb("one", [P, 4, 8])
            gates = sb("gates", [P, 16])
            slotf = sb("slotf", [P, 3, 16])
            sloti = sb("sloti", [P, 2, 16], U32)
            fc1 = sb("fc1", [P, 2, CH, FF])
            fc2 = sb("fc2", [P, 2, HC, C])
            fc2b = sb("fc2b", [P, NE, C])
            rows = sb("rows", [P, 16, C])
            dT = sb("dT", [P, CH, SLOTS])
            hid = sb("hid", [P, 2, HC, CAP])
            fc1b = sb("fc1b", [P, 2, HC])
            eo = sb("eo", [P, 2, 2, C])
            flat = rows[:, :, :].rearrange("p a b -> p (a b)")
            picks, count = flat[0:NE, 0:SLOTS], flat[0:NE, SLOTS:2 * SLOTS]
            fits, pos = dT[0:NE, 0, :], dT[0:NE, 1, :]
            ps = st.enter_context(nc.psum_tensor("E_ps", [P, 8, HALF], F32))
            names = ("ld_gate ld_fc2b fc1_0 fc1_1 fc2_0 fc2_1 router_done "
                     "x_turned tok_ready hot_ready hot_turned picks_ready slots_ready slots_ps sidx_ready scattered "
                     "rows_loaded rows_turned dT_act dT_dve fc1_done gelu_done fc2_done eo_ready eo_st0 eo_st1 "
                     "gathered bias_ready y_ready y_turned").split()
            s = {n: sem("E_" + n) for n in names}
            block = st.enter_context(nc.Block())

            def experts(eng, body):
                with eng.Fori(0, NE // 2) as j:
                    body(2 * j, 0, j)
                    body(2 * j + 1, 1, j)

            @block.sync
            def _(sp):
                sp.dma_start(wgate[:, :, :], io["l1_wg"]).then_inc(s["ld_gate"], 16)
                sp.dma_start(rank[:, :, :], io["rank"]).then_inc(s["ld_gate"], 16)
                sp.dma_start(base[:, :], io["base"]).then_inc(s["ld_gate"], 16)
                sp.dma_start(fc2b[:, :, :].rearrange("p e d -> p (e d)"), io["l1_fc2b"].to_broadcast([P, NE * C])) \
                    .then_inc(s["ld_fc2b"], 16)

                def load(e, k):
                    sp.wait_ge(s["fc1_done"], HC // 2 * (e + 1))
                    sp.dma_start(fc1[:, k, :, :].rearrange("p a f -> p (a f)"), io["l1_fc1"][e]).then_inc(s[f"fc1_{k}"], 16)
                    sp.wait_ge(s["fc2_done"], e + 1)
                    sp.dma_start(fc2[:, k, :, :].rearrange("p a f -> p (a f)"), io["l1_fc2"][e]).then_inc(s[f"fc2_{k}"], 16)

                def store(e, k):
                    sp.wait_ge(s["eo_ready"], e + 3)
                    sp.dma_start(eo_dram[ds(e * CAP, CAP), :].rearrange("(a p) d -> p a d", p=P), eo[:, k, :, :]) \
                        .then_inc(s[f"eo_st{k}"], 16)

                for k in range(2):
                    sp.sem_inc(s[f"eo_st{k}"], 16)
                load(0, 0)
                load(1, 1)
                with sp.Fori(1, NE // 2) as j:
                    for k in range(2):
                        load(2 * j + k, k)
                        store(2 * j + k - 2, k)
                for k in range(2):
                    store(NE - 2 + k, k)

            @block.gpsimd
            def _(pool):
                pool.wait_ge(s["tok_ready"], 1)
                pool.wait_ge(s["sidx_ready"], 1)
                for i in range(16):
                    pool.indirect_dma_start(out=disp_dram, out_offset=bass.IndirectOffsetOnAxis(ap=sloti[:, 1, i:i + 1], axis=0),
                                            in_=tok[:, i % 8, :], in_offset=None, bounds_check=SLOTS - 1,
                                            oob_is_err=False).then_inc(s["scattered"], 16)
                block_pool(pool, l + 1)
                for k in range(2):
                    pool.wait_ge(s[f"eo_st{k}"], 16 * (NE // 2 + 1))
                for i in range(16):
                    pool.indirect_dma_start(out=rows[:, i, :], out_offset=None, in_=eo_dram,
                                            in_offset=bass.IndirectOffsetOnAxis(ap=sloti[:, 0, i:i + 1], axis=0),
                                            bounds_check=SLOTS - 1, oob_is_err=False).then_inc(s["gathered"], 16)
                pool.wait_ge(s["gathered"], 16 * 16)

            @block.scalar
            def _(act):
                act.sem_inc(s["gelu_done"], HC // 2)
                condition_act(act, sig)
                route_act(act, lt, 2)
                act.wait_ge(s["x_turned"], 1)
                for j in range(4):
                    ins = act.activation(tok[:, 2 * j:2 * j + 2, :].rearrange("p a b -> p (a b)"), ps[:, 4 + j, :], ACT.Identity)
                ins.then_inc(s["tok_ready"], 1)
                act.wait_ge(s["hot_turned"], 1)
                for j in range(4):
                    ins = act.activation(picks[:, j * HALF:(j + 1) * HALF], ps[0:NE, 4 + j, :], ACT.Identity)
                ins.then_inc(s["picks_ready"], 1)
                act.wait_ge(s["scattered"], 16 * 16)
                act.dma_start(rows[:, :, :], disp_dram.rearrange("(a p) d -> p a d", p=P)).then_inc(s["rows_loaded"], 16)
                act.wait_ge(s["rows_turned"], 1)
                for j in range(4):
                    ins = act.activation(dT[:, 0, j * HALF:(j + 1) * HALF], ps[:, j, :], ACT.Identity)
                ins.then_inc(s["dT_act"], 1)
                block_act(act, l + 1)

                def gelu(e, k, j):
                    act.wait_ge(s["bias_ready"], e + 1)
                    act.wait_ge(s["fc2_done"], e + 1)
                    for h in range(HC // 2):
                        act.wait_ge(s["fc1_done"], HC // 2 * e + h + 1 + HC)
                        for i in range(2):
                            ins = act.activation(hid[:, k, 2 * h + i, :], ps[:, h, i * CAP:(i + 1) * CAP], ACT.Gelu,
                                                 bias=fc1b[:, k, 2 * h + i:2 * h + i + 1])
                        ins.then_inc(s["gelu_done"], 1)

                experts(act, gelu)

            @block.vector
            def _(dve):
                dve.sem_inc(s["eo_ready"], 2)
                condition_dve(dve, l, sig)
                dve.wait_ge(s["router_done"], 1)
                dve.wait_ge(s["ld_gate"], 48)
                dstep.link(dve.tensor_copy(lt[:, 0, :, :], ps[:, 0, 0:8 * NE].rearrange("p (t e) -> p t e", t=8)))
                route_dve(dve, lt, one, rank[:, :, :], 2)
                dve.nop().then_inc(s["hot_ready"], 1)
                dstep.link(dve.tensor_tensor(one[:, 2, :], one[:, 0, :], one[:, 1, :], ALU.add))
                dstep.link(dve.tensor_scalar(one[:, 2, :], one[:, 2, :], 1e-9, None, ALU.max))
                dstep.link(dve.reciprocal(one[:, 2, :], one[:, 2, :]))
                for k in range(2):
                    dstep.mark(dve.tensor_tensor(gates[:, 8 * k:8 * k + 8], one[:, k, :], one[:, 2, :], ALU.mult))
                dve.wait_ge(s["picks_ready"], 1)
                dstep.link(dve.tensor_tensor_scan(count, base[:, 1:2].to_broadcast([NE, SLOTS]), picks, 0.0, ALU.mult, ALU.add))
                dstep.link(dve.tensor_scalar(fits, count, float(CAP), None, ALU.is_le))
                dstep.link(dve.scalar_tensor_tensor(out=pos, in0=count, scalar=-1.0, in1=fits, op0=ALU.add, op1=ALU.mult))
                dstep.link(dve.scalar_tensor_tensor(out=count, in0=pos, scalar=base[:, 0:1], in1=picks, op0=ALU.add, op1=ALU.mult))
                dve.tensor_tensor(fits, fits, picks, ALU.mult).then_inc(s["slots_ready"], 1)
                dve.wait_ge(s["slots_ps"], 1)
                dstep.link(dve.tensor_copy(slotf[:, 0:2, :].rearrange("p a b -> p (a b)"), ps[:, 0, 0:32]))
                dstep.link(dve.tensor_tensor(gates[:, :], gates[:, :], slotf[:, 1, :], ALU.mult))
                dstep.link(dve.tensor_scalar(slotf[:, 2, :], slotf[:, 1, :], -2.0 * SLOTS, 2.0 * SLOTS, ALU.mult, ALU.add))
                dstep.link(dve.tensor_tensor(slotf[:, 2, :], slotf[:, 2, :], slotf[:, 0, :], ALU.add))
                dve.tensor_copy(sloti[:, 0, :], slotf[:, 0, :])
                dve.tensor_copy(sloti[:, 1, :], slotf[:, 2, :]).then_inc(s["sidx_ready"], 1)
                dve.wait_ge(s["rows_turned"], 1)
                for j in range(4):
                    ins = dve.tensor_copy(dT[:, 1, j * HALF:(j + 1) * HALF], ps[:, 4 + j, :])
                ins.then_inc(s["dT_dve"], 1)
                block_dve(dve, l + 1)
                dve.wait_ge(s["ld_fc2b"], 16)

                def biases(e, k):
                    dve.tensor_scalar(fc1b[:, k, :], vecs[:, ds(HC * e + VEC["fc1b"][0], HC)], 1.0, None, ALU.mult) \
                        .then_inc(s["bias_ready"], 1)

                def store_rows(e, k, j):
                    dve.wait_ge(s["fc2_done"], e + 3)
                    dve.wait_ge(s[f"eo_st{k}"], 16 * j + 16)
                    dve.tensor_tensor(eo[:, k, :, :], ps[:, 4 + k, :].rearrange("p (a d) -> p a d", a=2),
                                      fc2b[:, ds(e, 1), :].to_broadcast([P, 2, C]), ALU.add).then_inc(s["eo_ready"], 1)

                for k in range(2):
                    biases(k, k)
                with dve.Fori(0, NE // 2 - 1) as j:
                    for k in range(2):
                        store_rows(2 * j + k, k, j)
                        biases(2 * j + k + 2, k)
                for k in range(2):
                    store_rows(NE - 2 + k, k, NE // 2 - 1)
                dve.wait_ge(s["gathered"], 16 * 16)
                for k in range(2):
                    for t in range(8):
                        if k == 0:
                            ins = dve.tensor_scalar(tok[:, t, :], rows[:, t, :], gates[:, t:t + 1], None, ALU.mult)
                        else:
                            ins = dve.scalar_tensor_tensor(out=tok[:, t, :], in0=rows[:, 8 + t, :], scalar=gates[:, 8 + t:9 + t],
                                                           in1=tok[:, t, :], op0=ALU.mult, op1=ALU.add)
                    if k == 0:
                        dstep.link(ins)
                ins.then_inc(s["y_ready"], 1)
                dve.wait_ge(s["y_turned"], 1)
                for ch in range(CH):
                    for h in range(2):
                        x = xT[:, ch, h * HALF:(h + 1) * HALF]
                        dstep.link(dve.tensor_tensor(x, x, ps[:, 2 * ch + h, :], ALU.add))

            @block.tensor
            def _(pe):
                pe.sem_inc(s["fc1_done"], HC)
                pe.sem_inc(s["fc2_done"], 2)
                pe.wait_ge(s["ld_gate"], 48)
                pe.wait_ge(xin_ready, l + 1)
                for t in range(8):
                    for k in range(CH):
                        ins = pe.matmul(ps[:, 0, t * NE:(t + 1) * NE], xin[:, k, t * P:(t + 1) * P], wgate[:, k, :],
                                        start=(k == 0), stop=(k == CH - 1))
                ins.then_inc(s["router_done"], 1)
                for t in range(8):
                    for k in range(CH):
                        ins = pe.transpose(ps[:, 4 + t // 2, t % 2 * C + k * P:t % 2 * C + (k + 1) * P],
                                           xin[:, k, t * P:(t + 1) * P], ident[:, :])
                ins.then_inc(s["x_turned"], 1)
                pe.wait_ge(s["hot_ready"], 1)
                pe.wait_ge(s["tok_ready"], 1)
                for i in range(16):
                    ins = pe.transpose(ps[0:NE, 4 + i // 4, i % 4 * P:(i % 4 + 1) * P], lt[:, 2 + i // 8, i % 8, :], ident[:, :])
                ins.then_inc(s["hot_turned"], 1)
                pe.wait_ge(s["slots_ready"], 1)
                for a, src in enumerate((count, fits)):
                    for i in range(16):
                        ins = pe.matmul(ps[:, 0, 16 * a + i:16 * a + i + 1], src[:, i * P:(i + 1) * P], base[:, 1:2],
                                        start=True, stop=True)
                ins.then_inc(s["slots_ps"], 1)
                pe.wait_ge(s["rows_loaded"], 16)
                for a in range(16):
                    for k in range(CH):
                        ins = pe.transpose(ps[:, 4 * k + a // 4, a % 4 * P:(a % 4 + 1) * P], rows[:, a, k * P:(k + 1) * P], ident[:, :])
                ins.then_inc(s["rows_turned"], 1)
                pe.wait_ge(s["dT_act"], 1)
                pe.wait_ge(s["dT_dve"], 1)

                def up(e, k, n):
                    pe.wait_ge(s[f"fc1_{k}"], 16 * n + 16)
                    for h in range(HC // 2):
                        pe.wait_ge(s["gelu_done"], HC // 2 * e + h + 1)
                        for i in range(2):
                            f = (2 * h + i) * P
                            for c in range(CH):
                                ins = pe.matmul(ps[:, h, i * CAP:(i + 1) * CAP], fc1[:, k, c, f:f + P],
                                                dT[:, c, ds(e * CAP, CAP)], start=(c == 0), stop=(c == CH - 1))
                        ins.then_inc(s["fc1_done"], 1)

                def down(e, k, n):
                    pe.wait_ge(s[f"fc2_{k}"], 16 * n + 16)
                    pe.wait_ge(s["gelu_done"], HC // 2 * (e + 2))
                    pe.wait_ge(s["eo_ready"], e + 1)
                    for a in range(2):
                        for h in range(HC):
                            ins = pe.matmul(ps[:, 4 + k, a * C:(a + 1) * C], hid[:, k, h, a * P:(a + 1) * P], fc2[:, k, h, :],
                                            start=(h == 0), stop=(h == HC - 1))
                    ins.then_inc(s["fc2_done"], 1)

                up(0, 0, 0)
                with pe.Fori(0, NE // 2 - 1) as j:
                    up(2 * j + 1, 1, j)
                    down(2 * j, 0, j)
                    up(2 * j + 2, 0, j + 1)
                    down(2 * j + 1, 1, j)
                up(NE - 1, 1, NE // 2 - 1)
                down(NE - 2, 0, NE // 2 - 1)
                down(NE - 1, 1, NE // 2 - 1)
                pe.wait_ge(s["y_ready"], 1)
                for t in range(8):
                    for k in range(CH):
                        ins = pe.transpose(ps[:, 2 * k + t // 4, t % 4 * P:(t % 4 + 1) * P], tok[:, t, k * P:(k + 1) * P], ident[:, :])
                ins.then_inc(s["y_turned"], 1)


    def stage_l2_attn(l):
        PAIRS, PER, HS = L2_PAIRS, 4, HD + 1
        ITER = PAIRS // 2
        STEPS = PER * ITER
        with ExitStack() as st:
            def sb(n, shape, dt=F32):
                return st.enter_context(nc.sbuf_tensor("K_" + n, shape, dt))

            sig = sb("sig", [P, CH, NT])
            wqkv = sb("wqkv", [P, 2, CH, 3 * P])
            wo = sb("wo", [P, 2, C])
            qT = sb("qT", [P, 2, HALF])
            ks = sb("ks", [P, 2, 4, P])
            vs = sb("vs", [P, 2, 4, 2, HS])
            kv = sb("kv", [P, 2, 2, 2 * HS])
            quot = sb("quot", [P, 4, P])
            norm = sb("norm", [P, 2, 4])
            oT = sb("oT", [P, 2, HALF])
            ps_q = st.enter_context(nc.psum_tensor("K_ps_q", [P, HALF], F32))
            ps_kvp = st.enter_context(nc.psum_tensor("K_ps_kvp", [P, 2, 2, 2 * P], F32))
            ps_kv = st.enter_context(nc.psum_tensor("K_ps_kv", [P, HALF], F32))
            ps_o = st.enter_context(nc.psum_tensor("K_ps_o", [P, 2, HALF], F32))
            ps_t = st.enter_context(nc.psum_tensor("K_ps_t", [P, HALF], F32))
            ps_y = st.enter_context(nc.psum_tensor("K_ps_y", [P, HALF], F32))
            names = ("wqkv0 wqkv1 wo0 wo1 zeroed q_done q_evac kvp_done kvp_evac kv_done kv_evac o_done quot_ready "
                     "t_done t_evac y_done y_added").split()
            s = {n: sem("K_" + n) for n in names}
            block = st.enter_context(nc.Block())

            def loop(eng, step, per=0, count=None):
                for j in range(PER):
                    step(j, j, 0)
                if count:
                    assert count.n - loop.start == per, (count.n - loop.start, per)
                with eng.Fori(1, ITER) as i:
                    if count:
                        count.enter(i - 1, per)
                    for j in range(PER):
                        step(PER * i + j, j, i)
                if count:
                    count.leave(ITER - 1)

            @block.sync
            def _(sp):
                def load(p, k):
                    need(sp, s["kvp_done"], 4 * (p - 1))
                    sp.dma_start(wqkv[:, k, :, :].rearrange("p a b -> p (a b)"), io["l2_wqkv"][p]).then_inc(s[f"wqkv{k}"], 16)
                    need(sp, s["y_done"], 4 * (p - 1))
                    sp.dma_start(wo[:, k, :], io["l2_wo"][p]).then_inc(s[f"wo{k}"], 16)

                for k in range(2):
                    load(k, k)
                with sp.Fori(1, ITER) as i:
                    for k in range(2):
                        load(2 * i + k, k)

            @block.gpsimd
            def _(pool):
                pstep.mark(pool.memset(kv[:, :, :, :], 0.0))
                pool.memset(vs[:, :, :, :, HD:HS], 1.0).then_inc(s["zeroed"], 1)
                with pool.Fori(0, NP) as i:
                    pstep.enter(i, PIECE_POOL_STEPS)
                    piece_pool(pool, l + 1, i, 0)
                pstep.leave(NP)

            @block.scalar
            def _(act):
                condition_act(act, sig)
                act.wait_ge(s["zeroed"], 1)

                def step(n, j, i):
                    act.wait_ge(s["q_done"], n + 1)
                    need(act, s["o_done"], n - 1)
                    act.activation(qT[:, j % 2, :], ps_q[:, :], ACT.Relu).then_inc(s["q_evac"], 1)
                    need(act, s["kv_done"], n - 1)
                    for h in range(2):
                        act.wait_ge(s["kvp_done"], 2 * n + h + 1)
                        act.activation(ks[:, j % 2, 2 * h:2 * h + 2, :], ps_kvp[:, h, :, 0:P], ACT.Relu)
                        act.activation(vs[:, j % 2, 2 * h:2 * h + 2, :, 0:HD],
                                       ps_kvp[:, h, :, P:2 * P].rearrange("p a (r d) -> p a r d", r=2),
                                       ACT.Identity).then_inc(s["kvp_evac"], 1)
                    if j == 0:
                        piece_act(act, l + 1, i, 0)
                    if not isinstance(n, int) or n:
                        turned(n - 1, (j + 1) % 2)

                def turned(n, k):
                    act.wait_ge(s["t_done"], n + 1)
                    need(act, s["y_done"], 2 * (n - 1))
                    act.activation(oT[:, k, :], ps_t[:, :], ACT.Identity).then_inc(s["t_evac"], 1)

                loop(act, step)
                turned(STEPS - 1, 1)

            @block.vector
            def _(dve):
                condition_dve(dve, l, sig)
                for ch in range(CH):
                    dstep.link(dve.tensor_scalar(xT[:, ch, :], xT[:, ch, :], vec("bo2", ch), None, ALU.add))
                dve.wait_ge(s["zeroed"], 1)

                def add(n, j):
                    for ch in range(CH):
                        dve.wait_ge(s["y_done"], 2 * n + ch + 1)
                        x = xT[:, ch, j % 2 * HALF:(j % 2 + 1) * HALF]
                        dve.tensor_tensor(x, x, ps_y[:, :], ALU.add).then_inc(s["y_added"], 1)

                def step(n, j, i):
                    if j == 0:
                        piece_scans(dve, l + 1, i, 0)
                    dve.wait_ge(s["kv_done"], n + 1)
                    need(dve, s["o_done"], n - 1)
                    for r in range(2):
                        h = slice(HD * r, HD * r + HD)
                        ins = dve.tensor_copy(kv[h, j % 2, :, HS * r:HS * r + HS],
                                              ps_kv[h, 0:4 * HS].rearrange("p (b e) -> p b e", b=2)[:, :, HS * r:HS * r + HS])
                    ins.then_inc(s["kv_evac"], 1)
                    if j == 2:
                        piece_finish(dve, l + 1, i, 0)
                    dve.wait_ge(s["o_done"], n + 1)
                    o = ps_o[:, :, 0:4 * HS].rearrange("p a (q e) -> p a q e", e=HS)
                    dstep.link(dve.tensor_scalar(norm[:, :, :], o[:, :, :, HD], 1e-6, None, ALU.max))
                    dstep.link(dve.reciprocal(norm[:, :, :], norm[:, :, :]))
                    need(dve, s["t_done"], n)
                    dve.tensor_tensor(quot[:, :, :].rearrange("p (a b) (r e) -> p a (b r) e", a=2, r=2), o[:, :, :, 0:HD],
                                      norm[:, :, :].unsqueeze(3).to_broadcast([P, 2, 4, HD]),
                                      ALU.mult).then_inc(s["quot_ready"], 1)
                    if not isinstance(n, int) or n:
                        add(n - 1, j + 1)

                loop.start = dstep.n
                loop(dve, step, PIECE_DVE_STEPS + 2 * PER, dstep)
                add(STEPS - 1, 1)

            @block.tensor
            def _(pe):
                pe.wait_ge(xin_ready, l + 1)

                def queries(n, j):
                    need(pe, s["q_evac"], n)
                    for k in range(CH):
                        ins = pe.matmul(ps_q[:, :], wqkv[:, j // 2, k, 0:P], xin[:, k, j % 2 * HALF:(j % 2 + 1) * HALF],
                                        start=(k == 0), stop=(k == CH - 1))
                    ins.then_inc(s["q_done"], 1)

                def keys_values(n, j, h):
                    need(pe, s["kvp_evac"], 2 * n - 1 + h)
                    for a in range(2):
                        t = j % 2 * HALF + (2 * h + a) * P
                        for k in range(CH):
                            ins = pe.matmul(ps_kvp[:, h, a, :], xin[:, k, t:t + P], wqkv[:, j // 2, k, P:3 * P],
                                            start=(k == 0), stop=(k == CH - 1))
                    ins.then_inc(s["kvp_done"], 1)

                def key_value(n, j):
                    pe.wait_ge(s["kvp_evac"], 2 * n + 2)
                    need(pe, s["kv_evac"], n)
                    for b in range(2):
                        for t in range(2):
                            ins = pe.matmul(ps_kv[:, 2 * HS * b:2 * HS * (b + 1)], ks[:, j % 2, 2 * b + t, :],
                                            vs[:, j % 2, 2 * b + t, :, :].rearrange("p r e -> p (r e)"),
                                            start=(t == 0), stop=(t == 1))
                    ins.then_inc(s["kv_done"], 1)

                def weighted(n, j):
                    pe.wait_ge(s["kv_evac"], n + 1)
                    pe.wait_ge(s["q_evac"], n + 1)
                    need(pe, s["quot_ready"], n)
                    for t in range(4):
                        ins = pe.matmul(ps_o[:, t // 2, 2 * HS * (t % 2):2 * HS * (t % 2 + 1)], qT[:, j % 2, t * P:(t + 1) * P],
                                        kv[:, j % 2, t // 2, :], start=True, stop=True)
                    ins.then_inc(s["o_done"], 1)

                def turn(n):
                    pe.wait_ge(s["quot_ready"], n + 1)
                    need(pe, s["t_evac"], n)
                    for t in range(4):
                        ins = pe.transpose(ps_t[:, t * P:(t + 1) * P], quot[:, t, :], ident[:, :])
                    ins.then_inc(s["t_done"], 1)

                def output(n, j, ch):
                    need(pe, s["y_added"], 2 * n + ch)
                    pe.matmul(ps_y[:, :], wo[:, j // 2, ch * P:(ch + 1) * P], oT[:, j % 2, :],
                              start=True, stop=True).then_inc(s["y_done"], 1)

                def step(n, j, i):
                    first = isinstance(n, int)
                    if j % 2 == 0:
                        pe.wait_ge(s[f"wqkv{j // 2}"], 16 * i + 16)
                    queries(n, j)
                    if not (first and n < 1):
                        weighted(n - 1, (j + 3) % 4)
                    keys_values(n, j, 0)
                    if not (first and n < 2):
                        k = (j + 2) % 4
                        if k % 2 == 0:
                            pe.wait_ge(s[f"wo{k // 2}"], 16 * (i if j >= 2 else i - 1) + 16)
                        pe.wait_ge(s["t_evac"], n - 1)
                        output(n - 2, k, 0)
                    keys_values(n, j, 1)
                    if not (first and n < 1):
                        turn(n - 1)
                    if not (first and n < 2):
                        output(n - 2, (j + 2) % 4, 1)
                    key_value(n, j)

                loop(pe, step)
                weighted(STEPS - 1, 3)
                pe.wait_ge(s["wo1"], 16 * ITER)
                pe.wait_ge(s["t_evac"], STEPS - 1)
                for ch in range(CH):
                    output(STEPS - 2, 2, ch)
                turn(STEPS - 1)
                pe.wait_ge(s["t_evac"], STEPS)
                for ch in range(CH):
                    output(STEPS - 1, 3, ch)

    def stage_l2_ffn(l):
        with ExitStack() as st:
            sig = st.enter_context(nc.sbuf_tensor("F_sig", [P, CH, NT], F32))
            w = st.enter_context(nc.sbuf_tensor("F_w", [P, CH, C], F32))
            scaled = st.enter_context(nc.sbuf_tensor("F_scaled", [P, 4, HALF], F32))
            ps = st.enter_context(nc.psum_tensor("F_ps", [P, 4, HALF], F32))
            s = {n: sem("F_" + n) for n in ("ld_w", "done", "scaled")}
            block = st.enter_context(nc.Block())
            half = lambda h: slice(h * HALF, (h + 1) * HALF)

            @block.sync
            def _(sp):
                sp.dma_start(w[:, :, :], io["l2_w"]).then_inc(s["ld_w"], 16)

            @block.gpsimd
            def _(pool):
                block_pool(pool, l + 1)

            @block.scalar
            def _(act):
                condition_act(act, sig)
                for g in range(4):
                    act.wait_ge(s["done"], g + 1)
                    act.activation(scaled[:, g, :], ps[:, g, :], ACT.Identity, scale=vec("fscale", g % 2),
                                   bias=vec("fbias", g % 2)).then_inc(s["scaled"], 1)
                block_act(act, l + 1)

            @block.vector
            def _(dve):
                condition_dve(dve, l, sig)
                for g in range(4):
                    dve.wait_ge(s["scaled"], g + 1)
                    x = xT[:, g % 2, half(g // 2)]
                    dstep.mark(dve.tensor_tensor(x, x, scaled[:, g, :], ALU.add))
                block_dve(dve, l + 1)

            @block.tensor
            def _(pe):
                pe.wait_ge(s["ld_w"], 16)
                pe.wait_ge(xin_ready, l + 1)
                for g in range(4):
                    m = g % 2
                    for k in range(CH):
                        ins = pe.matmul(ps[:, g, :], w[:, k, m * P:(m + 1) * P], xin[:, k, half(g // 2)],
                                        start=(k == 0), stop=(k == CH - 1))
                    ins.then_inc(s["done"], 1)

    def stage_l3_attn(l):
        LOW = -1.0e38
        with ExitStack() as st:
            def sb(n, shape, dt=F32):
                return st.enter_context(nc.sbuf_tensor("V_" + n, shape, dt))

            sig = sb("sig", [P, CH, NT])
            w = sb("w", [P, 4, CH, C])
            mixed = sb("mixed", [P, 3, CH, NT])
            rest = sb("rest", [P, 8])
            k, v, r = sb("k", [P, CH, NT]), sb("v", [P, CH, NT]), sb("r", [P, CH, NT])
            top = sb("top", [P, CH, NB, T + 1])
            num = sb("num", [P, CH, NB, T + 1])
            den = sb("den", [P, CH, NB, T + 1])
            grow = sb("grow", [P, CH, NT])
            ps = st.enter_context(nc.psum_tensor("V_ps", [P, 8, HALF], F32))
            names = "ld_w w_exp scaled mixed done evac diff_ready exp_ready prod_ready rwkv_ready".split()
            s = {n: sem("V_" + n) for n in names}
            block = st.enter_context(nc.Block())
            half = lambda h: slice(h * HALF, (h + 1) * HALF)
            wave = lambda x: x.rearrange("p (b t) -> p b t", b=NB)
            keep1, keep2 = mixed[:, 0], mixed[:, 1]
            out1, out2 = mixed[:, 2], sig

            @block.sync
            def _(sp):
                sp.dma_start(w[:, :, :, :], io["l3_w"]).then_inc(s["ld_w"], 16)

            @block.gpsimd
            def _(pool):
                for ch in range(CH):
                    pool.wait_ge(s["exp_ready"], 2 * ch + 1)
                    pool.tensor_tensor(grow[:, ch, :], keep2[:, ch, :], v[:, ch, :], ALU.mult).then_inc(s["prod_ready"], 1)
                    pool.wait_ge(s["exp_ready"], 2 * ch + 2)
                    pool.tensor_tensor(k[:, ch, :], out2[:, ch, :], v[:, ch, :], ALU.mult).then_inc(s["prod_ready"], 1)
                block_pool(pool, l + 1)

            @block.scalar
            def _(act):
                condition_act(act, sig)
                act.activation(rest[:, 6:8], vecs[:, VEC["decay"][0]:VEC["decay"][0] + 2], ACT.Exp).then_inc(s["w_exp"], 1)
                act.wait_ge(xin_ready, l + 1)
                for j, n in enumerate(("mk", "mv", "mr")):
                    for ch in range(CH):
                        act.activation(mixed[:, j, ch, :], xin[:, ch, :], ACT.Identity, scale=vec(n, ch)).then_inc(s["scaled"], 1)
                for g in range(12):
                    dst, ch, h = (k, v, r)[g // 4], g // 2 % 2, g % 2
                    act.wait_ge(s["done"], g + 1)
                    act.activation(dst[:, ch, half(h)], ps[:, g % 8, :], ACT.Sigmoid if g >= 8 else ACT.Identity) \
                        .then_inc(s["evac"], 1)
                for ch in range(CH):
                    for j, pair in enumerate(((keep1, keep2), (out1, out2))):
                        act.wait_ge(s["diff_ready"], 2 * ch + j + 1)
                        for x in pair:
                            ins = act.activation(x[:, ch, :], x[:, ch, :], ACT.Exp)
                        ins.then_inc(s["exp_ready"], 1)
                block_act(act, l + 1)

            @block.vector
            def _(dve):
                condition_dve(dve, l, sig)
                dve.memset(top[:, :, :, 0:1], LOW)
                dve.memset(num[:, :, :, 0:1], 0.0)
                dve.memset(den[:, :, :, 0:1], 0.0)
                dstep.link(dve.tensor_scalar(rest[:, 0:6], vecs[:, VEC["mk"][0]:VEC["mk"][0] + 6], -1.0, 1.0, ALU.mult, ALU.add))
                for j in range(3):
                    for ch in range(CH):
                        dve.wait_ge(s["scaled"], 2 * j + ch + 1)
                        m = wave(mixed[:, j, ch, :])[:, :, 1:T]
                        ins = dve.scalar_tensor_tensor(out=m, in0=wave(xin[:, ch, :])[:, :, 0:T - 1],
                                                       scalar=rest[:, 2 * j + ch:2 * j + ch + 1], in1=m, op0=ALU.mult, op1=ALU.add)
                    ins.then_inc(s["mixed"], 1)
                dve.wait_ge(s["w_exp"], 1)
                dstep.link(dve.tensor_scalar(rest[:, 6:8], rest[:, 6:8], -1.0, None, ALU.mult))
                dve.wait_ge(s["done"], 12)
                dve.wait_ge(s["evac"], 4)
                for ch in range(CH):
                    decayed, first, kc = rest[:, 6 + ch:7 + ch], vec("first", ch), wave(k[:, ch, :])
                    for b in range(NB):
                        ins = dve.tensor_tensor_scan(top[:, ch, b, 1:T + 1], decayed.to_broadcast([P, T]),
                                                     k[:, ch, b * T:(b + 1) * T], LOW, ALU.add, ALU.max)
                    dstep.link(ins)
                    before, after = top[:, ch, :, 0:T], top[:, ch, :, 1:T + 1]
                    dve.scalar_tensor_tensor(out=wave(keep1[:, ch, :]), in0=before, scalar=decayed, in1=after,
                                             op0=ALU.add, op1=ALU.subtract)
                    dve.tensor_tensor(wave(keep2[:, ch, :]), kc, after, ALU.subtract).then_inc(s["diff_ready"], 1)
                    dstep.link(dve.scalar_tensor_tensor(out=wave(out2[:, ch, :]), in0=kc, scalar=first, in1=before,
                                                        op0=ALU.add, op1=ALU.max))
                    dstep.link(dve.tensor_tensor(wave(out1[:, ch, :]), before, wave(out2[:, ch, :]), ALU.subtract))
                    dve.scalar_tensor_tensor(out=wave(out2[:, ch, :]), in0=kc, scalar=first, in1=wave(out2[:, ch, :]),
                                             op0=ALU.add, op1=ALU.subtract).then_inc(s["diff_ready"], 1)
                for ch in range(CH):
                    dve.wait_ge(s["exp_ready"], 2 * ch + 1)
                    dve.wait_ge(s["prod_ready"], 2 * ch + 1)
                    for b in range(NB):
                        c = slice(b * T, (b + 1) * T)
                        dve.tensor_tensor_scan(num[:, ch, b, 1:T + 1], keep1[:, ch, c], grow[:, ch, c], 0.0, ALU.mult, ALU.add)
                        ins = dve.tensor_tensor_scan(den[:, ch, b, 1:T + 1], keep1[:, ch, c], keep2[:, ch, c], 0.0,
                                                     ALU.mult, ALU.add)
                    dstep.link(ins)
                    dve.wait_ge(s["exp_ready"], 2 * ch + 2)
                    n, d = num[:, ch, :, 0:T], den[:, ch, :, 0:T]
                    e1, e2 = wave(out1[:, ch, :]), wave(out2[:, ch, :])
                    dve.tensor_tensor(n, n, e1, ALU.mult)
                    dstep.link(dve.tensor_tensor(d, d, e1, ALU.mult))
                    dve.wait_ge(s["prod_ready"], 2 * ch + 2)
                    dve.tensor_tensor(n, n, wave(k[:, ch, :]), ALU.add)
                    dstep.link(dve.tensor_tensor(e2, d, e2, ALU.add))
                    dstep.link(dve.reciprocal(e2, e2))
                    dve.wait_ge(s["evac"], 12)
                    dstep.link(dve.tensor_tensor(e2, n, e2, ALU.mult))
                    dve.tensor_tensor(r[:, ch, :], r[:, ch, :], out2[:, ch, :], ALU.mult).then_inc(s["rwkv_ready"], 1)
                block_dve(dve, l + 1)
                for g in range(4):
                    dve.wait_ge(s["done"], 12 + g + 1)
                    x = xT[:, g // 2, half(g % 2)]
                    dstep.mark(dve.tensor_tensor(x, x, ps[:, (12 + g) % 8, :], ALU.add))

            @block.tensor
            def _(pe):
                pe.wait_ge(s["ld_w"], 16)
                for g in range(16):
                    j, m, h = g // 4, g // 2 % 2, g % 2
                    if j < 3:
                        pe.wait_ge(s["mixed"], j + 1)
                    elif g == 12:
                        pe.wait_ge(s["rwkv_ready"], 2)
                    if g >= 8:
                        pe.wait_ge(s["evac"], g - 7)
                    for c in range(CH):
                        src = mixed[:, j, c, half(h)] if j < 3 else r[:, c, half(h)]
                        ins = pe.matmul(ps[:, g % 8, :], w[:, j, c, m * P:(m + 1) * P], src, start=(c == 0), stop=(c == CH - 1))
                    ins.then_inc(s["done"], 1)

    def stage_last():
        with ExitStack() as st:
            stored = sem("stored")
            block = st.enter_context(nc.Block())

            @block.sync
            def _(sp):
                sp.dma_start(io["yT"], xT[:, :, :]).then_inc(stored, 16)
                sp.wait_ge(stored, 16)

    stage_l0_attn(0)
    stage_moe(1, "L0")
    stage_l1_attn(2)
    stage_l1_ffn(3)
    stage_l2_attn(4)
    stage_l2_ffn(5)
    stage_l3_attn(6)
    stage_moe(7, "L3")
    stage_last()
    outer.close()


def chunks(a, axis, n):
    pad = [(0, 0)] * a.ndim
    pad[axis] = (0, n * P - a.shape[axis])
    a = np.pad(a, pad)
    return a.reshape(a.shape[:axis] + (n, P) + a.shape[axis + 1:])


def features(a):
    n = -(-a.shape[0] // P)
    return chunks(a, 0, n).transpose(1, 0, 2)


def columns(v, n):
    return chunks(v.reshape(-1), 0, n).T


def lay_out(i):
    f = np.float32
    out = {}
    tokens = lambda a: a.reshape(NT, C).T.reshape(CH, P, NT).transpose(1, 0, 2)
    out["xT"], out["fT"] = tokens(i["x"]), tokens(i["fside_BxSxS_0"])
    out["cond"] = np.broadcast_to(i["cond_512"], (P, NB, 64))
    out["ident"] = np.eye(P, dtype=f)
    conds = ["L0_cond", "L0_cond2", "L1_cond", "L1_cond2", "L2_cond", "L2_cond2", "L3_cond", "L3_cond2"]
    pieces = {
        "w": np.concatenate([columns(i[c + "_w"], CH) for c in conds], 1),
        "u": np.repeat(np.concatenate([columns(i[c + "_u"], CH) for c in conds], 1), NB, axis=1),
        "bq": i["L0_attn_bq"].reshape(4, 2, 4, HD).transpose(1, 3, 0, 2).reshape(P, 16),
        "kw": np.repeat(i["L0_attn_key_weights"].reshape(4, 2, 4).transpose(1, 0, 2), HD, axis=0).reshape(P, 16),
        "bk": columns(i["L0_attn_bk"], 4), "bv": columns(i["L0_attn_bv"], 4), "bo0": columns(i["L0_attn_bo"], 2),
        "b1": columns(np.concatenate([i["L1_attn_b1"], i["L1_attn_b1"][2 * P:]]), 3), "convb": columns(i["L1_attn_conv_b"], 3),
        "ba": columns(i["L1_attn_ba"], 3), "bx": columns(i["L1_attn_bx"], 3), "lam": columns(i["L1_attn_lam"], 3),
        "b2": columns(i["L1_attn_b2"], 2), "fc1b": columns(i["L1_ffn_fc1_b"], NE * FF // P),
        "bo2": columns(i["L2_attn_bo"], 2), "fscale": columns(i["L2_ffn_scale_weight"], 2),
        "fbias": columns(i["L2_ffn_bias"], 2), "decay": columns(i["L3_attn_time_decay"], 2),
        "first": columns(i["L3_attn_time_first"], 2), "mk": columns(i["L3_attn_time_mix_k"], 2),
        "mv": columns(i["L3_attn_time_mix_v"], 2), "mr": columns(i["L3_attn_time_mix_r"], 2),
    }
    out["vecs"] = np.concatenate([pieces[n] for n in VEC], 1)
    inv = (f(1.0) / f(10000.0) ** (np.arange(0, HD, 2, dtype=f) / f(HD))).astype(f)
    ang = np.arange(T, dtype=f)[None, :] * inv[:, None]
    cos, sin = np.cos(ang), np.sin(ang)
    out["rope"] = np.stack([np.concatenate([cos] * 4), np.concatenate([-sin, sin] * 2)], 1).astype(f)
    out["mask"] = np.where(np.arange(T)[None, :] - P > np.arange(P)[:, None], f(NEG), f(0))
    wq = i["L0_attn_Wq"].reshape(4, 2, 4, HD, CH, P).transpose(0, 5, 2, 4, 1, 3).reshape(4, P, 1024)
    wk = i["L0_attn_Wk"].reshape(4, P, CH, P).transpose(0, 3, 2, 1).reshape(4, P, 256)
    wv = i["L0_attn_Wv"].reshape(4, P, CH, P).transpose(0, 3, 2, 1).reshape(4, P, 256)
    wo = i["L0_attn_Wo"].reshape(C, 4, 2, 4, HD).transpose(1, 2, 4, 3, 0).reshape(4, P, 1024)
    out["w_l0a"] = np.concatenate([wk, wv, wq, wo], 2)
    for name, sh in (("L0", ("shw_gate", "shw_up", "shw_down")), ("L3", ("sw_gate", "sw_up", "sw_down"))):
        g = lambda n: i[f"{name}_ffn_{n}"]
        shared = g("shgate_w" if name == "L0" else "shared_gate_w").reshape(C, 1)
        out[name + "_gate"] = features(np.concatenate([g("gate_w").T, shared], 1))
        n = -(-g(sh[0]).shape[1] // P)
        up = []
        for a, b in (("w_gate", sh[0]), ("w_up", sh[1])):
            experts = g(a).reshape(NE, C, EH * NE // P, P // NE).transpose(1, 2, 0, 3).reshape(C, -1, P)
            m = np.concatenate([experts, chunks(g(b), 1, n)], 1)
            up.append(m.reshape(CH, P, -1, P).transpose(2, 1, 0, 3).reshape(-1, P, 2 * P))
        experts = g("w_down").reshape(NE, EH * NE // P, P // NE, C).transpose(1, 0, 2, 3).reshape(-1, P, C)
        down = np.concatenate([experts, chunks(g(sh[2]), 0, n)], 0)
        out[name + "_w"] = np.concatenate(up + [down], 2)
    out["rank"] = np.broadcast_to(np.arange(NE, 0, -1, dtype=f), (P, 8, NE))
    w1 = i["L1_attn_w1"].T
    out["l1_w1"] = features(np.concatenate([w1, w1[:, 2 * P:]], 1))
    cw = i["L1_attn_conv_w"].transpose(2, 1, 0)
    full = cw[:, :2 * P].reshape(TAPS * CH, P, R1)
    half = cw[:, 2 * P:].reshape(2, P, R1)
    out["l1_conv"] = np.concatenate([full, half], 0).transpose(1, 0, 2)
    out["l1_gate"] = np.stack([features(i["L1_attn_wa"].T), features(i["L1_attn_wx"].T)], 1)
    out["l1_w2"] = features(i["L1_attn_w2"].T)
    out["l1_wg"] = features(i["L1_ffn_wg"])
    first = np.zeros((NE, 4), f)
    first[:, 0], first[:, 1] = np.arange(NE) * CAP, 1.0
    out["base"] = first
    out["l1_fc1"] = i["L1_ffn_fc1_w"].reshape(NE, CH, P, FF).transpose(0, 2, 1, 3).reshape(NE, P, CH * FF)
    out["l1_fc2"] = i["L1_ffn_fc2_w"].reshape(NE, FF // P, P, C).transpose(0, 2, 1, 3).reshape(NE, P, FF // P * C)
    out["l1_fc2b"] = i["L1_ffn_fc2_b"].reshape(1, NE * C)
    w = np.stack([i["L2_attn_" + n].reshape(CH, P, L2_PAIRS, P) for n in ("Wq", "Wk", "Wv")], 3)
    out["l2_wqkv"] = w.transpose(2, 1, 0, 3, 4).reshape(L2_PAIRS, P, CH * 3 * P)
    out["l2_wo"] = i["L2_attn_Wo"].reshape(L2_PAIRS, P, C)
    out["l2_w"] = features(i["L2_ffn_weight"].T)
    out["l3_w"] = np.stack([features(i["L3_attn_" + n].T) for n in ("Wk", "Wv", "Wr", "Wo")], 1)
    return {k: np.ascontiguousarray(v) for k, v in out.items()}


def kernel(**inputs):
    import concourse.bacc as bacc
    from concourse.bass_utils import run_bass_kernel_spmd

    arrays = lay_out({k: np.asarray(v) for k, v in inputs.items()})
    nc = bacc.Bacc("TRN2", target_bir_lowering=False, num_devices=1)
    io = {n: nc.dram_tensor(n + "_dram", a.shape, mybir.dt.from_np(a.dtype), kind="ExternalInput").ap()
          for n, a in arrays.items()}
    io["yT"] = nc.dram_tensor("yT_dram", (P, CH, NT), F32, kind="ExternalOutput").ap()
    build_program(nc, io)
    r = run_bass_kernel_spmd(nc, [{n + "_dram": a for n, a in arrays.items()}], core_ids=[0])
    y = r.results[0]["yT_dram"]
    return y.transpose(1, 0, 2).reshape(C, NT).T.reshape(NB, T, C)
```

```python
from contextlib import ExitStack

import numpy as np

import concourse.bass as bass
from concourse import mybir

P = 128
NB, T, C = 4, 256, 256
NT = NB * T
CH = C // P
HALF = NT // 2
NL = 8
NP = CH * NB
TOGETHER = ((0,), (1,), (2,), (3,), (4,), (5, 6, 7))

HD = 64
L0_PAIRS, L0_GROUP = 4, 4
NE, EH = 8, 176
L0_SH, L3_SH = 352, 704
R1, TAPS = 320, 4
FF, CAP = 1024, 256
SLOTS = NE * CAP
L2_PAIRS = 16

F32 = mybir.dt.float32
F32R = mybir.dt.float32r
U32 = mybir.dt.uint32
ALU = mybir.AluOpType
ACT = mybir.ActivationFunctionType
AX_X = mybir.AxisListType.X
ds = bass.ds
NEG = -1.0e30


def vec_columns():
    sizes = [("w", 2 * NL), ("u", NP * NL), ("bq", 16), ("kw", 16), ("bk", 4), ("bv", 4), ("bo0", 2),
             ("b1", 3), ("convb", 3), ("ba", 3), ("bx", 3), ("lam", 3), ("b2", 2), ("fc1b", NE * FF // P),
             ("bo2", 2), ("fscale", 2), ("fbias", 2), ("decay", 2), ("first", 2), ("mk", 2), ("mv", 2),
             ("mr", 2)]
    at, out = 0, {}
    for name, n in sizes:
        out[name] = (at, n)
        at += n
    return out, at


VEC, NVEC = vec_columns()


class Steps:

    def __init__(self, eng, sem):
        self.eng, self.sem, self.base, self.n = eng, sem, 0, 0

    def mark(self, ins):
        self.n += 1
        return ins.then_inc(self.sem, 1)

    def wait(self):
        self.eng.wait_ge(self.sem, self.base + self.n)

    def link(self, ins):
        self.mark(ins)
        self.wait()

    def enter(self, i, per):
        self.kept = self.base + self.n
        self.base, self.n, self.per = self.kept + i * per, 0, per

    def leave(self, count):
        assert self.n == self.per, (self.n, self.per)
        self.base, self.n = self.kept + count * self.per, 0


def build_program(nc, io):
    outer = ExitStack()

    def sem(name):
        return outer.enter_context(nc.semaphore(name))

    def keep(name, shape, dt=F32):
        return outer.enter_context(nc.sbuf_tensor(name, shape, dt))

    xT = keep("xT", [P, CH, NT])
    xin = keep("xin", [P, CH, NT])
    fside = keep("fside", [P, CH, NT])
    vecs = keep("vecs", [P, NVEC])
    ident = keep("ident", [P, P])
    decay = keep("decay", [P, NL * CH * NB])
    unread = keep("unread", [P, NL])
    gain = keep("gain", [P, NB])
    mod = keep("mod", [P, 3, CH, NT])
    uk = keep("uk", [P, 2, T])
    scans = keep("scans", [P, 2, 2, 2, T])
    terms = keep("terms", [P, 2, 2, T])
    sums = keep("sums", [P, 2, 2, T])
    scan_inputs = ExitStack()
    ek, ekv, ek_back, ekv_back = (scan_inputs.enter_context(nc.sbuf_tensor(n, [P, CH, NT], F32))
                                  for n in ("ek", "ekv", "ek_back", "ekv_back"))

    dve_steps_sem, act_steps_sem, pool_steps_sem = sem("dve_steps"), sem("act_steps"), sem("pool_steps")
    uk_ready = sem("uk_ready")
    euk_ready = sem("euk_ready")
    scans_ready = sem("scans_ready")
    sums_ready = sem("sums_ready")
    sig_ready = sem("sig_ready")
    xin_ready = sem("xin_ready")
    sub_ready = sem("sub_ready")
    exp_ready = sem("exp_ready")
    steps = {"dve": Steps(nc.vector, dve_steps_sem), "act": Steps(nc.scalar, act_steps_sem),
             "pool": Steps(nc.gpsimd, pool_steps_sem)}
    dstep, astep, pstep = steps["dve"], steps["act"], steps["pool"]

    def need(eng, semaphore, count):
        if not isinstance(count, int) or count > 0:
            eng.wait_ge(semaphore, count)

    def vec(name, i=0):
        return vecs[:, ds(VEC[name][0] + i, 1)]

    def part(x, i):
        return x[:, :, :].rearrange("p c t -> p (c t)")[:, ds(i * T, T)]

    def turn_of(l, i):
        group = next(g for g in TOGETHER if l in g)
        return NP * group[0] + len(group) * i + l - group[0]

    def piece_scans(dve, l, i, k):
        dve.tensor_scalar(uk[:, k, :], part(fside, i), vec("u", NP * l + i), 30.0, ALU.add, ALU.min).then_inc(uk_ready, 1)
        dec = decay[:, ds(NP * l + i, 1)]
        for kind, src, back in ((0, ekv, ekv_back), (1, ek, ek_back)):
            dve.tensor_tensor_scan(scans[:, k, kind, 0, :], dec.to_broadcast([P, T]), part(src, i), 0.0, ALU.mult, ALU.add)
            ins = dve.tensor_tensor_scan(scans[:, k, kind, 1, 0:T - 1][:, ::-1], part(back, i)[:, 0:T - 1],
                                         dec.to_broadcast([P, T - 1]), 0.0, ALU.add, ALU.mult)
        ins.then_inc(scans_ready, 1)

    def piece_act(act, l, i, k):
        act.wait_ge(uk_ready, turn_of(l, i) + 1)
        act.activation(terms[:, k, 1, :], uk[:, k, :], ACT.Exp).then_inc(euk_ready, 1)

    def piece_pool(pool, l, i, k):
        pool.wait_ge(euk_ready, turn_of(l, i) + 1)
        pool.wait_ge(scans_ready, turn_of(l, i) + 1)
        pstep.mark(pool.tensor_tensor(sums[:, k, :, :], scans[:, k, :, 0, :], scans[:, k, :, 1, :], ALU.add))
        pstep.link(pool.tensor_tensor(terms[:, k, 0, :], terms[:, k, 1, :], part(fside, i), ALU.mult))
        pool.tensor_tensor(sums[:, k, :, :], sums[:, k, :, :], terms[:, k, :, :], ALU.add).then_inc(sums_ready, 1)

    PIECE_POOL_STEPS = 2

    def piece_finish(dve, l, i, k):
        dve.wait_ge(sums_ready, turn_of(l, i) + 1)
        den = sums[:, k, 1, :]
        dstep.link(dve.tensor_scalar(den, den, 1e-8, None, ALU.max))
        dstep.link(dve.reciprocal(den, den))
        dstep.mark(dve.tensor_tensor(part(mod[:, l % 3], i), sums[:, k, 0, :], den, ALU.mult))

    PIECE_DVE_STEPS = 3

    def block_dve(dve, l):
        for i in range(NP):
            piece_scans(dve, l, i, i % 2)
            if i:
                piece_finish(dve, l, i - 1, (i - 1) % 2)
        piece_finish(dve, l, NP - 1, (NP - 1) % 2)

    def block_act(act, l):
        for i in range(NP):
            piece_act(act, l, i, i % 2)

    def block_pool(pool, l):
        for i in range(NP):
            piece_pool(pool, l, i, i % 2)

    def next_sigmoid(act, l):
        act.activation(unread[:, l:l + 1], vecs[:, 0:1], ACT.Sigmoid)

    def condition_act(act, sig):
        for h in range(2):
            half = slice(h * HALF, (h + 1) * HALF)
            act.activation(sig[:, :, half], xT[:, :, half], ACT.Sigmoid).then_inc(sig_ready, 1)

    def condition_dve(dve, l, sig):
        dstep.wait()
        for b in range(NB):
            if b % 2 == 0:
                dve.wait_ge(sig_ready, 2 * l + b // 2 + 1)
            c = slice(b * T, (b + 1) * T)
            ins = dve.scalar_tensor_tensor(out=xin[:, :, c], in0=sig[:, :, c], scalar=gain[:, b:b + 1],
                                           in1=mod[:, l % 3, :, c], op0=ALU.mult, op1=ALU.mult)
            if b % 2:
                ins.then_inc(xin_ready, 1)

    tok_dram = nc.dram_tensor("token_scratch", (NT, C), F32, kind="Internal").ap()
    eo_dram = nc.dram_tensor("expert_out_scratch", (SLOTS, C), F32, kind="Internal").ap()

    def stage_first():
        with ExitStack() as st:
            crep = st.enter_context(nc.sbuf_tensor("crep", [P, NB, 64], F32))
            small = st.enter_context(nc.sbuf_tensor("small", [P, 8 * NB], F32))
            wexp = st.enter_context(nc.sbuf_tensor("wexp", [P, 2, 2 * NL], F32))
            fmin = st.enter_context(nc.sbuf_tensor("fmin", [P, CH, NT], F32))
            s_vec, s_x, s_f, s_c, s_id = sem("ld_vecs"), sem("ld_x"), sem("ld_f"), sem("ld_cond"), sem("ld_ident")
            s_tfsum, s_tf, s_fmin, s_ek, s_wexp = (sem(n) for n in ("tf_sum", "tf", "f_min", "ek_rdy", "w_exp"))
            s_zero, s_ekv, s_back = sem("zeroed"), sem("ekv_rdy"), sem("reversed")
            block = st.enter_context(nc.Block())

            @block.sync
            def _(sp):
                sp.dma_start(fside[:, :, :], io["fT"]).then_inc(s_f, 16)
                sp.dma_start(vecs[:, :], io["vecs"]).then_inc(s_vec, 16)
                sp.dma_start(crep[:, :, :], io["cond"]).then_inc(s_c, 16)
                sp.dma_start(xT[:, :, :], io["xT"]).then_inc(s_x, 16)
                sp.dma_start(ident[:, :], io["ident"]).then_inc(s_id, 16)
                sp.wait_ge(s_x, 16)
                sp.wait_ge(s_id, 16)

            @block.gpsimd
            def _(pool):
                pool.memset(scans[:, :, :, :, :], 0.0).then_inc(s_zero, 1)
                block_pool(pool, 0)

            @block.scalar
            def _(act):
                act.wait_ge(s_vec, 16)
                astep.link(act.activation(wexp[:, 0, :], vecs[:, 0:2 * NL], ACT.Exp))
                act.activation(wexp[:, 1, :], wexp[:, 0, :], ACT.Exp, scale=-1.0).then_inc(s_wexp, 1)
                act.wait_ge(s_fmin, 1)
                act.activation(ek[:, :, :], fmin[:, :, :], ACT.Exp).then_inc(s_ek, 1)
                back = lambda x: x[:, :, :].rearrange("p c (b t) -> p (c b) t", b=NB)[:, :, ::-1]
                ahead = lambda x: x[:, :, :].rearrange("p c (b t) -> p (c b) t", b=NB)
                act.activation(ahead(ek_back), back(fmin), ACT.Exp)
                act.wait_ge(s_tfsum, 1)
                act.activation(small[:, NB:2 * NB], small[:, 0:NB], ACT.Sigmoid).then_inc(s_tf, 1)
                act.wait_ge(s_ekv, 1)
                act.activation(ahead(ekv_back), back(ekv), ACT.Identity).then_inc(s_back, 1)
                block_act(act, 0)
                next_sigmoid(act, 0)

            @block.vector
            def _(dve):
                dve.wait_ge(s_f, 16)
                dve.tensor_scalar(fmin[:, :, :], fside[:, :, :], 30.0, None, ALU.min).then_inc(s_fmin, 1)
                dve.wait_ge(s_c, 16)
                dve.tensor_reduce(small[:, 0:NB], crep[:, :, :], AX_X, ALU.add).then_inc(s_tfsum, 1)
                dve.wait_ge(s_ek, 1)
                dve.tensor_tensor(ekv[:, :, :], ek[:, :, :], fside[:, :, :], ALU.mult).then_inc(s_ekv, 1)
                dve.wait_ge(s_tf, 1)
                tf = small[:, NB:2 * NB]
                dve.tensor_scalar(gain[:, :], tf, 0.2, 0.8, ALU.mult, ALU.add)
                dstep.link(dve.tensor_scalar(small[:, 2 * NB:3 * NB], tf, 0.5, 0.5, ALU.mult, ALU.add))
                dve.wait_ge(s_wexp, 1)
                for b in range(NB):
                    ins = dve.tensor_scalar(decay[:, :].rearrange("p (c b) -> p c b", b=NB)[:, :, b], wexp[:, 1, :],
                                            small[:, 2 * NB + b:2 * NB + b + 1], None, ALU.mult)
                dstep.link(ins)
                dve.wait_ge(s_back, 1)
                dve.wait_ge(s_zero, 1)
                block_dve(dve, 0)

    stage_first()

    def stage_l0_attn(l):
        NU = L0_GROUP * NB
        NPROJ = 4 + 2 * L0_GROUP
        with ExitStack() as st:
            def sb(name, shape, dt=F32):
                return st.enter_context(nc.sbuf_tensor(name, shape, dt))

            sig = sb("sigA", [P, CH, NT])
            wkvq = sb("wkvq", [P, 512 + 1024])
            wk = wkvq[:, 0:256].rearrange("p (k f) -> p k f", k=CH)
            wv = wkvq[:, 256:512].rearrange("p (k f) -> p k f", k=CH)
            wq = wkvq[:, 512:1536].rearrange("p (m k f) -> p m k f", m=L0_GROUP, k=CH)
            wo = sb("wo", [P, L0_GROUP, C])
            rope = sb("rope", [P, 2, T])
            mask = sb("mask", [P, T])
            kraw, kswap = sb("kraw", [P, NT]), sb("kswap", [P, NT])
            qraw, qswap = sb("qraw", [P, NT]), sb("qswap", [P, NT])
            t1, t2 = sb("t1", [P, NT]), sb("t2", [P, NT])
            kz = sb("kz", [P, NB, 2, T])
            vtok = sb("vtok", [P, 2 * NB, P])
            qr = sb("qr", [P, 2, NT])
            probs = sb("probs", [P, 4, 768])
            stats = sb("stats", [P, 4, 16])
            probT = sb("probT", [P, 2, 2, 384])
            oT = sb("oT", [P, L0_GROUP, NT])
            cols = sb("cols", [P, 9])
            colv = sb("colv", [P, 1])
            ps_s = st.enter_context(nc.psum_tensor("ps_s", [P, 2, 1024], F32))
            ps_t = st.enter_context(nc.psum_tensor("ps_t", [P, 2, 512], F32))
            ps_p = st.enter_context(nc.psum_tensor("ps_p", [P, HALF], F32))
            ps_o = st.enter_context(nc.psum_tensor("ps_o", [P, HALF], F32))
            names = ("w_kvq w_wo ld_rope proj_done proj_evac s_ready max_ready exp_done recip_ready norm_done "
                     "pt_ready pt_dve pt_act o_ready o_evac wo_done wo_added rope_done t1_ready swap_k swap_q "
                     "cols_ready colv_ready zeroed").split()
            s = {n: sem("A_" + n) for n in names}
            block = st.enter_context(nc.Block())
            LAST = L0_PAIRS - 1

            def proj_bank(g):
                return ps_o if g == 5 else ps_p

            def group(m):
                return 2 if m == 0 else 4 + 2 * m

            heads = lambda x, n: x.rearrange("p (b t) -> p b t", b=n)
            cosb = rope[:, 0:1, :].to_broadcast([P, NB, T])
            sinb = rope[:, 1:2, :].to_broadcast([P, NB, T])

            def scores(u):
                return (ps_s[:, u % 2, 0:512].rearrange("p (r t) -> p r t", r=2),
                        ps_s[:, u % 2, 512:768].rearrange("p (r t) -> p r t", r=2))

            def prob(u):
                return (probs[:, u % 4, 0:512].rearrange("p (r t) -> p r t", r=2),
                        probs[:, u % 4, 512:768].rearrange("p (r t) -> p r t", r=2))

            @block.sync
            def _(sp):
                def load_kvq(n):
                    need(sp, s["proj_done"], NPROJ * n)
                    sp.dma_start(wkvq[:, :], io["w_l0a"][n][:, 0:1536]).then_inc(s["w_kvq"], 16)

                def load_wo(n):
                    need(sp, s["wo_done"], 4 * n)
                    sp.dma_start(wo[:, :, :].rearrange("p m n -> p (m n)"),
                                 io["w_l0a"][n][:, 1536:2560]).then_inc(s["w_wo"], 16)

                def swap(n, j):
                    src, dst, done = (kraw, kswap, "swap_k") if j == 0 else (qraw, qswap, "swap_q")
                    sp.wait_ge(s["proj_evac"], NPROJ * n + (2 if j == 0 else group(j - 1) + 2))
                    for q in range(4):
                        sp.dma_start(dst[32 * q:32 * q + 32, :], src[32 * (q ^ 1):32 * (q ^ 1) + 32, :]) \
                            .then_inc(s[done], 16)

                def pair(c, more):
                    for j in range(2, 1 + L0_GROUP):
                        swap(c, j)
                    if more:
                        load_kvq(c + 1)
                        swap(c + 1, 0)
                        swap(c + 1, 1)
                        load_wo(c + 1)

                load_kvq(0)
                sp.dma_start(rope[:, :, :], io["rope"]).then_inc(s["ld_rope"], 16)
                sp.dma_start(mask[:, :], io["mask"]).then_inc(s["ld_rope"], 16)
                load_wo(0)
                swap(0, 0)
                swap(0, 1)
                with sp.Fori(0, LAST) as c:
                    pair(c, True)
                pair(LAST, False)

            @block.gpsimd
            def _(pool):
                def rope_cos(n, j):
                    src = kraw if j == 0 else qraw
                    pool.wait_ge(s["proj_evac"], NPROJ * n + (2 if j == 0 else group(j - 1) + 2))
                    pool.wait_ge(s["rope_done"], 5 * n + j + 1)
                    pool.tensor_tensor(heads(t1[:, :], NB), heads(src[:, :], NB), cosb, ALU.mult).then_inc(s["t1_ready"], 1)

                def pair(c, more):
                    for u in range(NU):
                        if u % NB == 1 and u < NU - NB:
                            rope_cos(c, 2 + u // NB)
                        pool.wait_ge(s["recip_ready"], NU * c + u + 1)
                        p1, p0 = prob(u)
                        rs = stats[:, u % 4, 12:16]
                        pstep.mark(pool.tensor_tensor(p1, p1, rs[:, 0:2].unsqueeze(2).to_broadcast([P, 2, T]), ALU.mult))
                        pool.tensor_tensor(p0, p0, rs[:, 2:4].unsqueeze(2).to_broadcast([P, 2, P]),
                                           ALU.mult).then_inc(s["norm_done"], 1)
                        if u in (6, 10):
                            piece_pool(pool, l + 1, 2 * c + u // 10, u // 10)
                    if more:
                        rope_cos(c + 1, 0)
                        rope_cos(c + 1, 1)

                pool.memset(kz[:, :, :, :], 0.0).then_inc(s["zeroed"], 1)
                pool.wait_ge(s["ld_rope"], 32)
                rope_cos(0, 0)
                rope_cos(0, 1)
                with pool.Fori(0, LAST) as c:
                    pstep.enter(c, 2 * PIECE_POOL_STEPS + NU)
                    pair(c, True)
                pstep.leave(LAST)
                pair(LAST, False)

            @block.scalar
            def _(act):
                def evac(n, g, out, **k):
                    act.wait_ge(s["proj_done"], NPROJ * n + g + 1)
                    act.activation(out, proj_bank(g)[:, :], ACT.Identity, **k).then_inc(s["proj_evac"], 1)

                def evac_k(n, h):
                    if h == 0:
                        act.wait_ge(s["cols_ready"], n + 1)
                        need(act, s["rope_done"], 5 * n - 3)
                    evac(n, h, kraw[:, h * HALF:(h + 1) * HALF], bias=cols[:, 0:1])

                def evac_q(n, m, h):
                    if h == 0:
                        act.wait_ge(s["rope_done"], 5 * n + (1 if m == 0 else m + 2))
                    evac(n, group(m) + h, qraw[:, h * HALF:(h + 1) * HALF], scale=cols[:, 1 + m:2 + m],
                         bias=cols[:, 5 + m:6 + m])

                def evac_v(n, h):
                    evac(n, 4 + h, vtok[:, NB * h:NB * h + NB, :].rearrange("p a f -> p (a f)"))

                def exps(c, u):
                    act.wait_ge(s["max_ready"], NU * c + u + 1)
                    for i in range(4):
                        src, dst = scores(u)[i // 2], prob(u)[i // 2]
                        ins = act.activation(dst[:, i % 2, :], src[:, i % 2, :], ACT.Exp,
                                             bias=stats[:, u % 4, 4 + i:5 + i], scale=-1.0,
                                             accum_out=stats[:, u % 4, 8 + i:9 + i])
                    ins.then_inc(s["exp_done"], 1)

                def pt_evac(c, u):
                    act.wait_ge(s["pt_ready"], NU * c + u + 1)
                    act.activation(probT[:, u % 2, 1, :], ps_t[:, 1, 0:384], ACT.Identity).then_inc(s["pt_act"], 1)

                def o_evac(c, u):
                    if u == 0:
                        act.wait_ge(s["colv_ready"], c + 1)
                    act.wait_ge(s["o_ready"], NU * c + u + 1)
                    act.activation(oT[:, u // NB, ds(u % NB * T, T)], ps_o[:, 0:T], ACT.Identity,
                                   bias=colv[:, :]).then_inc(s["o_evac"], 1)

                def pair(c, more):
                    for u in range(NU):
                        exps(c, u)
                        if u % NB < 2 and u < NU - NB:
                            evac_q(c, u // NB + 1, u % NB)
                        if u in (3, 7):
                            piece_act(act, l + 1, 2 * c + u // 7, u // 7)
                        if u >= 2:
                            pt_evac(c, u - 2)
                        if u >= 3:
                            o_evac(c, u - 3)
                    if more:
                        evac_k(c + 1, 0)
                    pt_evac(c, NU - 2)
                    if more:
                        evac_k(c + 1, 1)
                    o_evac(c, NU - 3)
                    if more:
                        evac_q(c + 1, 0, 0)
                    pt_evac(c, NU - 1)
                    o_evac(c, NU - 2)
                    if more:
                        evac_q(c + 1, 0, 1)
                    o_evac(c, NU - 1)
                    if more:
                        evac_v(c + 1, 0)
                        evac_v(c + 1, 1)

                act.sem_inc(s["exp_done"], 2)
                act.sem_inc(s["pt_act"], 1)
                act.sem_inc(s["o_evac"], 1)
                condition_act(act, sig)
                for h in range(2):
                    evac_k(0, h)
                for h in range(2):
                    evac_q(0, 0, h)
                for h in range(2):
                    evac_v(0, h)
                with act.Fori(0, LAST) as c:
                    pair(c, True)
                pair(LAST, False)
                next_sigmoid(act, l + 1)

            @block.vector
            def _(dve):
                def columns_kq(n):
                    need(dve, s["proj_evac"], NPROJ * n)
                    dve.tensor_scalar(cols[:, 0:1], vec("bk", n), 1.0, None, ALU.mult)
                    four = lambda v: vecs[:, ds(4 * n + VEC[v][0], 4)]
                    dstep.link(dve.tensor_scalar(cols[:, 1:5], four("kw"), HD ** -0.5, None, ALU.mult))
                    dve.tensor_tensor(cols[:, 5:9], cols[:, 1:5], four("bq"), ALU.mult).then_inc(s["cols_ready"], 1)

                def column_v(n):
                    dve.wait_ge(s["o_evac"], NU * n + 1)
                    dve.tensor_scalar(colv[:, :], vec("bv", n), 1.0, None, ALU.mult).then_inc(s["colv_ready"], 1)

                def rope_sum(n, j):
                    swapped, done, count = (kswap, "swap_k", n + 1) if j == 0 else (qswap, "swap_q", 4 * n + j)
                    dve.wait_ge(s["rope_done"], 5 * n + j + 1)
                    dve.wait_ge(s[done], 64 * count)
                    dstep.link(dve.tensor_tensor(heads(t2[:, :], NB), heads(swapped[:, :], NB), sinb, ALU.mult))
                    dve.wait_ge(s["t1_ready"], 5 * n + j + 1)
                    if j == 0:
                        need(dve, s["s_ready"], NU * n)
                        for r in range(2):
                            h = slice(64 * r, 64 * r + 64)
                            ins = dve.tensor_tensor(kz[h, :, r, :], heads(t1[h, :], NB), heads(t2[h, :], NB), ALU.add)
                    else:
                        if j != 2:
                            need(dve, s["s_ready"], NU * n + NB * (j - 2))
                        ins = dve.tensor_tensor(qr[:, (j - 1) % 2, :], t1[:, :], t2[:, :], ALU.add)
                    ins.then_inc(s["rope_done"], 1)

                def max_rows(c, u):
                    dve.wait_ge(s["s_ready"], NU * c + u + 1)
                    dve.memset(stats[:, u % 4, 0:1], 0.0)
                    for i in range(4):
                        view, m = scores(u)[i // 2][:, i % 2, :], mask[:, 0:T] if i < 2 else mask[:, P:T]
                        ins = dve.tensor_tensor_reduce(out=view, in0=view, in1=m, scale=-1.0, scalar=-NEG, op0=ALU.add,
                                                       op1=ALU.min, accum_out=stats[:, u % 4, 4 + i:5 + i])
                    ins.then_inc(s["max_ready"], 1)

                def recip(c, u):
                    dve.wait_ge(s["exp_done"], NU * c + u + 3)
                    dve.reciprocal(stats[:, u % 4, 12:16], stats[:, u % 4, 8:12]).then_inc(s["recip_ready"], 1)

                def pt_evac(c, u):
                    dve.wait_ge(s["pt_ready"], NU * c + u + 1)
                    dve.tensor_copy(probT[:, u % 2, 0, :], ps_t[:, 0, 0:384]).then_inc(s["pt_dve"], 1)

                def pair(c, more):
                    for u in range(NU):
                        max_rows(c, u)
                        if u >= 1:
                            recip(c, u - 1)
                        if u >= 2:
                            pt_evac(c, u - 2)
                        if u % NB == 3 and u < NU - NB:
                            rope_sum(c, 2 + u // NB)
                        if u in (3, 7):
                            piece_scans(dve, l + 1, 2 * c + u // 7, u // 7)
                        if u in (9, 13):
                            piece_finish(dve, l + 1, 2 * c + u // 13, u // 13)
                        if u == 13 and more:
                            columns_kq(c + 1)
                    recip(c, NU - 1)
                    pt_evac(c, NU - 2)
                    pt_evac(c, NU - 1)
                    if more:
                        rope_sum(c + 1, 0)
                        rope_sum(c + 1, 1)
                    for j in range(4):
                        dve.wait_ge(s["wo_done"], 4 * c + j + 1)
                        half, ch = j % 2, j // 2
                        x = xT[:, ch, half * HALF:(half + 1) * HALF]
                        dve.tensor_tensor(x, x, (ps_o if j % 2 else ps_p)[:, :], ALU.add).then_inc(s["wo_added"], 1)
                    if more:
                        column_v(c + 1)

                dve.sem_inc(s["rope_done"], 1)
                dve.sem_inc(s["pt_dve"], 1)
                dve.sem_inc(s["wo_added"], 1)
                columns_kq(0)
                column_v(0)
                condition_dve(dve, l, sig)
                for ch in range(CH):
                    dstep.link(dve.tensor_scalar(xT[:, ch, :], xT[:, ch, :], vec("bo0", ch), None, ALU.add))
                dve.wait_ge(s["ld_rope"], 32)
                dve.wait_ge(s["zeroed"], 1)
                rope_sum(0, 0)
                rope_sum(0, 1)
                with dve.Fori(0, LAST) as c:
                    dstep.enter(c, 2 * PIECE_DVE_STEPS + 1 + L0_GROUP + 1)
                    pair(c, True)
                dstep.leave(LAST)
                pair(LAST, False)

            @block.tensor
            def _(pe):
                def project(n, g, w, h):
                    need(pe, s["proj_evac"], NPROJ * n + g)
                    for k in range(CH):
                        ins = pe.matmul(proj_bank(g)[:, :], w[:, k, :], xin[:, k, h * HALF:(h + 1) * HALF],
                                        start=(k == 0), stop=(k == CH - 1))
                    ins.then_inc(s["proj_done"], 1)

                def project_q(n, m, h):
                    project(n, group(m) + h, wq[:, m], h)

                def project_v(n, h):
                    need(pe, s["proj_evac"], NPROJ * n + 4)
                    if h == 1:
                        pe.wait_ge(s["o_evac"], NU * n + 1)
                    for t in range(NB):
                        for k in range(CH):
                            ins = pe.matmul(proj_bank(4 + h)[:, t * P:(t + 1) * P],
                                            xin[:, k, h * HALF + t * P:h * HALF + t * P + P], wv[:, k, :],
                                            start=(k == 0), stop=(k == CH - 1))
                    ins.then_inc(s["proj_done"], 1)

                def score(c, u):
                    m, b = divmod(u, NB)
                    if b == 0:
                        pe.wait_ge(s["rope_done"], 5 * c + m + 3)
                    pe.wait_ge(s["exp_done"], NU * c + u + 1)
                    for tile, view in zip((1, 0), scores(u)):
                        n = T if tile else P
                        ins = pe.matmul(view, qr[:, m % 2, b * T + tile * P:b * T + tile * P + P],
                                        kz[:, b, :, 0:n], start=True, stop=True)
                    ins.then_inc(s["s_ready"], 1)

                def turn(c, u):
                    pe.wait_ge(s["norm_done"], NU * c + u + 1)
                    pe.wait_ge(s["pt_dve"], NU * c + u + 1)
                    pe.wait_ge(s["pt_act"], NU * c + u + 1)
                    p1, p0 = prob(u)
                    for r in range(2):
                        pe.transpose(ps_t[:, r, 0:128], p0[:, r, :], ident[:, :])
                        pe.transpose(ps_t[:, r, 128:256], p1[:, r, 0:128], ident[:, :])
                        ins = pe.transpose(ps_t[:, r, 256:384], p1[:, r, 128:256], ident[:, :])
                    ins.then_inc(s["pt_ready"], 1)

                def weigh(c, u):
                    b = u % NB
                    if u == 0:
                        pe.wait_ge(s["proj_evac"], NPROJ * c + 6)
                        pe.wait_ge(s["wo_added"], 4 * c + 1)
                    pe.wait_ge(s["pt_dve"], NU * c + u + 2)
                    pe.wait_ge(s["pt_act"], NU * c + u + 2)
                    pe.wait_ge(s["o_evac"], NU * c + u + 1)
                    for key in range(2):
                        for r in range(2):
                            o = ps_o[64 * r:64 * r + 64, key * P:T]
                            ins = pe.matmul(o, vtok[:, 2 * b + key, 64 * r:64 * r + 64],
                                            probT[:, u % 2, r, 0:256] if key == 0 else probT[:, u % 2, r, 256:384],
                                            start=(key == 0), stop=(key == 1), skip_group_check=True)
                    ins.then_inc(s["o_ready"], 1)

                def pair(c, more):
                    n = c + 1
                    for u in range(NU):
                        score(c, u)
                        if u == 0:
                            pe.wait_ge(s["wo_added"], 4 * c + 1)
                        if u % NB < 2 and u < NU - NB:
                            project_q(c, u // NB + 1, u % NB)
                        if u >= 2:
                            turn(c, u - 2)
                        if u >= 3:
                            weigh(c, u - 3)
                    if more:
                        pe.wait_ge(s["w_kvq"], 16 * n + 16)
                        project(n, 0, wk, 0)
                    turn(c, NU - 2)
                    if more:
                        project(n, 1, wk, 1)
                    weigh(c, NU - 3)
                    if more:
                        project_q(n, 0, 0)
                    turn(c, NU - 1)
                    weigh(c, NU - 2)
                    if more:
                        project_q(n, 0, 1)
                    weigh(c, NU - 1)
                    if more:
                        project_v(n, 0)
                        project_v(n, 1)
                    pe.wait_ge(s["w_wo"], 16 * c + 16)
                    pe.wait_ge(s["o_evac"], NU * c + NU + 1)
                    for j in range(4):
                        half, ch = j % 2, j // 2
                        if j >= 2:
                            pe.wait_ge(s["wo_added"], 4 * c + j)
                        elif more:
                            pe.wait_ge(s["proj_evac"], NPROJ * n + 5 + j)
                        elif j == 0:
                            pe.wait_ge(s["proj_evac"], NPROJ * c + NPROJ)
                        for m in range(L0_GROUP):
                            ins = pe.matmul((ps_o if j % 2 else ps_p)[:, :], wo[:, m, ch * P:(ch + 1) * P],
                                            oT[:, m, half * HALF:(half + 1) * HALF],
                                            start=(m == 0), stop=(m == L0_GROUP - 1))
                        ins.then_inc(s["wo_done"], 1)

                pe.wait_ge(s["w_kvq"], 16)
                for h in range(2):
                    pe.wait_ge(xin_ready, 2 * l + 1 + h)
                    project(0, h, wk, h)
                for h in range(2):
                    project_q(0, 0, h)
                for h in range(2):
                    project_v(0, h)
                with pe.Fori(0, LAST) as c:
                    pair(c, True)
                pair(LAST, False)

    def route_act(act, lt, n):
        act.wait_ge(sub_ready, n)
        act.activation(lt[:, 1, :, :], lt[:, 1, :, :], ACT.Exp).then_inc(exp_ready, 1)

    def route_dve(dve, lt, one, rank, n):
        bc = lambda v: v.unsqueeze(2).to_broadcast([P, 8, NE])
        dstep.link(dve.tensor_reduce(one[:, 2, :], lt[:, 0, :, :], AX_X, ALU.max))
        dve.tensor_tensor(lt[:, 1, :, :], lt[:, 0, :, :], bc(one[:, 2, :]), ALU.subtract).then_inc(sub_ready, 1)
        dve.wait_ge(exp_ready, n)
        dstep.link(dve.tensor_reduce(one[:, 3, :], lt[:, 1, :, :], AX_X, ALU.add))
        dstep.link(dve.reciprocal(one[:, 3, :], one[:, 3, :]))
        dstep.link(dve.tensor_tensor(lt[:, 1, :, :], lt[:, 1, :, :], bc(one[:, 3, :]), ALU.mult))
        for k in range(2):
            p, hot = lt[:, 1, :, :], lt[:, 2 + k, :, :]
            dstep.link(dve.tensor_reduce(one[:, k, :], p, AX_X, ALU.max))
            dstep.link(dve.tensor_tensor(hot, p, bc(one[:, k, :]), ALU.is_equal))
            dstep.link(dve.tensor_tensor(hot, hot, rank, ALU.mult))
            dstep.link(dve.tensor_reduce(one[:, 2, :], hot, AX_X, ALU.max))
            dstep.link(dve.tensor_tensor(hot, hot, bc(one[:, 2, :]), ALU.is_equal))
            if k == 0:
                dstep.link(dve.scalar_tensor_tensor(out=p, in0=hot, scalar=-2.0, in1=p, op0=ALU.mult, op1=ALU.add))

    moe_names = ("ld_gate router_done shared_ready comb_ready rows_done rows_ready gu_done silu_done prod_ready "
                 "hid_ready down_done gu0 gu1 dn0 dn1 x_hi x_lo gu_hi gu_lo dn_hi dn_lo").split()
    moe_sems = {n: sem("moe_" + n) for n in moe_names}
    moe_left = {n: 0 for n in moe_names}

    def stage_moe(l, name):
        NE_CH = EH * NE // P
        NCH = NE_CH + -(-(L0_SH if name == "L0" else L3_SH) // P)
        more = l + 1 < NL
        with ExitStack() as st:
            def sb(n, shape, dt=F32):
                return st.enter_context(nc.sbuf_tensor(name + n, shape, dt))

            sig = sb("sig", [P, CH, NT])
            wgate = sb("wgate", [P, CH, NE + 1])
            wgu = sb("wgu", [P, 2, 2 * C])
            wgu_hi, wgu_lo = sb("wgu_hi", [P, 2, 2 * C], F32R), sb("wgu_lo", [P, 2, 2 * C], F32R)
            wdn = sb("wdn", [P, 2, C])
            xin_hi, xin_lo = sb("xin_hi", [P, CH, NT], F32R), sb("xin_lo", [P, CH, NT], F32R)
            wdn_hi, wdn_lo = sb("wdn_hi", [P, 2, C], F32R), sb("wdn_lo", [P, 2, C], F32R)
            hid_hi, hid_lo = xin_hi, xin_lo
            rank = sb("rank", [P, 8, NE])
            lt = sb("lt", [P, 4, 8, NE])
            one = sb("one", [P, 6, 8])
            wide = sig[:, :, :].rearrange("p c (t r) -> p c t r", t=8)
            rowsb = sig
            act_g = sb("actg", [P, 2, HALF])
            hid = sb("hid", [P, NCH, NT])
            ps_y = st.enter_context(nc.psum_tensor(name + "ps_y", [P, CH, 2, HALF], F32))
            ps_g = st.enter_context(nc.psum_tensor(name + "ps_g", [P, 2, HALF], F32))
            ps_u = st.enter_context(nc.psum_tensor(name + "ps_u", [P, 2, HALF], F32))
            s = moe_sems
            block = st.enter_context(nc.Block())

            def after(eng, n, count):
                if not isinstance(count, int) or count > 0:
                    eng.wait_ge(s[n], moe_left[n] + count)

            def twos(eng, body, mid=None):
                for ch in range(2):
                    body(ch, ch, 0)
                if mid:
                    mid()
                end = (NCH - 1) // 2
                with eng.Fori(1, end) as i:
                    for k in range(2):
                        body(2 * i + k, k, i)
                for ch in range(2 * end, NCH):
                    body(ch, ch % 2, ch // 2)

            def pairs(eng, body, steps=None, per=0):
                n = NCH // 2

                def pair(i):
                    for q in range(4):
                        body(2 * i + q // 2, q % 2, i, q)

                pair(0)
                end = n - 1 + NCH % 2
                with eng.Fori(1, end) as i:
                    if steps:
                        steps.enter(i - 1, per)
                    pair(i)
                if steps:
                    steps.leave(end - 1)
                if NCH % 2:
                    for h in range(2):
                        body(NCH - 1, h, n, h)
                else:
                    pair(n - 1)

            assert not more or NCH // 2 == NP - 1

            def half_of(x, h):
                return x[:, :, h * HALF:(h + 1) * HALF]

            def hid_of(ch):
                return hid[:, ds(ch, 1), :].rearrange("p a t -> p (a t)")

            def next_split(split, ch, q):
                if q % 2 == 0 and not (isinstance(ch, int) and ch == NCH - 1):
                    split(ch + 1, (q // 2 + 1) % 2)

            @block.sync
            def _(sp):
                sp.dma_start(wgate[:, :, :], io[name + "_gate"]).then_inc(s["ld_gate"], 16)
                sp.dma_start(rank[:, :, :], io["rank"]).then_inc(s["ld_gate"], 16)

                def load_gu(ch, k, n):
                    after(sp, "gu_lo", ch - 1)
                    sp.dma_start(wgu[:, k, :], io[name + "_w"][ch][:, 0:2 * C]).then_inc(s[f"gu{k}"], 16)

                def load_dn(ch, k, n):
                    after(sp, "dn_lo", 2 * ch - 2)
                    sp.dma_start(wdn[:, k, :], io[name + "_w"][ch][:, 2 * C:3 * C]).then_inc(s[f"dn{k}"], 16)

                twos(sp, load_gu)
                twos(sp, load_dn)

            @block.gpsimd
            def _(pool):
                def weigh(ch, which):
                    after(pool, "prod_ready", 2 * ch + 2)
                    h = hid_of(ch)
                    pool.tensor_tensor(h, h, rowsb[:, which, :], ALU.mult).then_inc(s["hid_ready"], 1)

                def piece(i, k=0):
                    if more:
                        piece_pool(pool, l + 1, i, k)

                half = NE_CH // 2
                piece(0)
                after(pool, "rows_ready", 1)
                for ch in range(2):
                    weigh(ch, 0)
                with pool.Fori(1, half) as i:
                    pstep.enter(i - 1, PIECE_POOL_STEPS if more else 0)
                    piece(i)
                    for k in range(2):
                        weigh(2 * i + k, 0)
                pstep.leave(half - 1)
                weigh(NE_CH - 1, 0)
                for i in range(half, NCH // 2):
                    piece(i)
                with pool.Fori(NE_CH, NCH) as ch:
                    weigh(ch, 1)
                piece(NP - 1, 1)

            @block.scalar
            def _(act):
                def gu_split(ch, k):
                    after(act, f"gu{k}", 16 * (ch // 2) + 16 if isinstance(ch, int) else 8 * (ch - k) + 16)
                    after(act, "gu_done", 2 * ch - 2)
                    act.activation(wgu_hi[:, k, :], wgu[:, k, :], ACT.Identity).then_inc(s["gu_hi"], 1)

                def dn_split(ch, k, n):
                    after(act, f"dn{k}", 16 * n + 16)
                    after(act, "hid_ready", ch + 1)
                    if isinstance(ch, int) and ch == 0:
                        after(act, "gu_done", 2 * NCH)
                    after(act, "down_done", ch - 1)
                    act.activation(wdn_hi[:, k, :], wdn[:, k, :], ACT.Identity)
                    for h in range(2):
                        half = slice(h * HALF, (h + 1) * HALF)
                        act.activation(hid_hi[:, k, half], hid_of(ch)[:, half], ACT.Identity).then_inc(s["dn_hi"], 1)

                condition_act(act, sig)
                gu_split(0, 0)
                for h in range(2):
                    act.wait_ge(xin_ready, 2 * l + 1 + h)
                    act.activation(half_of(xin_hi, h), half_of(xin, h), ACT.Identity).then_inc(s["x_hi"], 1)
                route_act(act, lt, l // 6 * 2 + 1)
                after(act, "router_done", 1)
                logits = ps_y[:, 0, 0, 0:8 * (NE + 1)].rearrange("p (t e) -> p t e", t=8)
                act.activation(wide[:, 1, :, :], logits[:, :, NE:NE + 1].to_broadcast([P, 8, P]),
                               ACT.Sigmoid).then_inc(s["shared_ready"], 1)

                def silu(ch, h, i, q):
                    next_split(gu_split, ch, q)
                    after(act, "gu_done", 2 * ch + h + 1)
                    after(act, "prod_ready", 2 * ch + h - 1)
                    act.activation(act_g[:, h, :], ps_g[:, h, :], ACT.Silu).then_inc(s["silu_done"], 1)
                    if more and q == 1:
                        piece_act(act, l + 1, i, 0)
                    if isinstance(i, int) and i == 0 and q == 3:
                        after(act, "rows_done", 1)
                        for j in range(2):
                            ins = act.activation(rowsb[:, j, :], ps_y[:, j, :, :].rearrange("p a t -> p (a t)"), ACT.Identity)
                        ins.then_inc(s["rows_ready"], 1)

                pairs(act, silu)
                twos(act, dn_split, (lambda: piece_act(act, l + 1, NP - 1, 1)) if more else None)
                if more:
                    next_sigmoid(act, l + 1)

            @block.vector
            def _(dve):
                def gu_split(ch, k):
                    after(dve, "gu_hi", ch + 1)
                    dve.tensor_tensor(wgu_lo[:, k, :], wgu[:, k, :], wgu_hi[:, k, :], ALU.subtract).then_inc(s["gu_lo"], 1)

                def dn_split(ch, k, n):
                    for h in range(2):
                        half = slice(h * HALF, (h + 1) * HALF)
                        after(dve, "dn_hi", 2 * ch + h + 1)
                        if h == 0:
                            dve.tensor_tensor(wdn_lo[:, k, :], wdn[:, k, :], wdn_hi[:, k, :], ALU.subtract)
                        dve.tensor_tensor(hid_lo[:, k, half], hid_of(ch)[:, half], hid_hi[:, k, half],
                                          ALU.subtract).then_inc(s["dn_lo"], 1)

                condition_dve(dve, l, sig)
                gu_split(0, 0)
                for h in range(2):
                    after(dve, "x_hi", h + 1)
                    dve.tensor_tensor(half_of(xin_lo, h), half_of(xin, h), half_of(xin_hi, h),
                                      ALU.subtract).then_inc(s["x_lo"], 1)
                after(dve, "router_done", 1)
                after(dve, "ld_gate", 32)
                logits = ps_y[:, 0, 0, 0:8 * (NE + 1)].rearrange("p (t e) -> p t e", t=8)
                dstep.link(dve.tensor_copy(lt[:, 0, :, :], logits[:, :, 0:NE]))
                route_dve(dve, lt, one, rank[:, :, :], l // 6 * 2 + 1)
                bc = lambda v: v.unsqueeze(2).to_broadcast([P, 8, NE])
                dstep.link(dve.tensor_tensor(one[:, 2, :], one[:, 0, :], one[:, 1, :], ALU.add))
                dstep.link(dve.reciprocal(one[:, 2, :], one[:, 2, :]))
                for k in range(2):
                    dstep.link(dve.tensor_tensor(one[:, 4 + k, :], one[:, k, :], one[:, 2, :], ALU.mult))
                    dstep.link(dve.tensor_tensor(lt[:, 2 + k, :, :], lt[:, 2 + k, :, :], bc(one[:, 4 + k, :]), ALU.mult))
                w16 = [lt[:, 2 + k, :, :].rearrange("p t e -> p (t e)").unsqueeze(2).to_broadcast([P, 8 * NE, P // NE])
                       for k in range(2)]
                dve.tensor_tensor(wide[:, 0, :, :].rearrange("p t (e i) -> p (t e) i", e=NE), w16[0], w16[1],
                                  ALU.add).then_inc(s["comb_ready"], 1)

                def multiply(ch, h, i, q):
                    next_split(gu_split, ch, q)
                    after(dve, "silu_done", 2 * ch + h + 1)
                    dve.tensor_tensor(hid[:, ds(ch, 1), h * HALF:(h + 1) * HALF].rearrange("p a t -> p (a t)"),
                                      act_g[:, h, :], ps_u[:, h, :], ALU.mult).then_inc(s["prod_ready"], 1)
                    if more and q in (0, 2):
                        (piece_scans if q == 0 else piece_finish)(dve, l + 1, i, 0)

                pairs(dve, multiply, dstep, PIECE_DVE_STEPS if more else 0)
                twos(dve, dn_split, (lambda: piece_scans(dve, l + 1, NP - 1, 1)) if more else None)
                if more:
                    piece_finish(dve, l + 1, NP - 1, 1)
                after(dve, "down_done", NCH)
                for ch in range(CH):
                    x = xT[:, ch, :]
                    dstep.link(dve.tensor_tensor(x, x, ps_y[:, ch, :, :].rearrange("p a t -> p (a t)"), ALU.add))

            @block.tensor
            def _(pe):
                after(pe, "ld_gate", 32)
                pe.wait_ge(xin_ready, 2 * l + 2)
                for t in range(8):
                    for k in range(CH):
                        ins = pe.matmul(ps_y[:, 0, 0, t * (NE + 1):(t + 1) * (NE + 1)], xin[:, k, t * P:(t + 1) * P],
                                        wgate[:, k, :], start=(k == 0), stop=(k == CH - 1))
                ins.then_inc(s["router_done"], 1)

                def gate_up(ch, k, n):
                    after(pe, "gu_lo", ch + 1)
                    for h in range(2):
                        after(pe, "prod_ready", 2 * ch + h - 1)
                        if isinstance(ch, int) and ch == 0:
                            after(pe, "x_lo", h + 1)
                        for ps, o in ((ps_g, 0), (ps_u, C)):
                            for i in range(CH):
                                for j, (w, x) in enumerate(((wgu_hi, xin_hi), (wgu_hi, xin_lo), (wgu_lo, xin_hi))):
                                    ins = pe.matmul(ps[:, h, :], w[:, k, o + i * P:o + (i + 1) * P], half_of(x, h)[:, i, :],
                                                    start=(i + j == 0), stop=(i == CH - 1 and j == 2))
                        ins.then_inc(s["gu_done"], 1)

                def rows():
                    after(pe, "comb_ready", 1)
                    after(pe, "shared_ready", 1)
                    for j in range(2):
                        for t in range(8):
                            ins = pe.transpose(ps_y[:, j, t // 4, t % 4 * P:t % 4 * P + P], wide[:, j, t, :], ident[:, :])
                    ins.then_inc(s["rows_done"], 1)

                def down(ch, k, n):
                    first, last = (isinstance(ch, int) and ch == c for c in (0, NCH - 1))
                    if first:
                        after(pe, "rows_ready", 1)
                    terms = ((wdn_hi, hid_hi[:, k, :]), (wdn_hi, hid_lo[:, k, :]), (wdn_lo, hid_hi[:, k, :]))
                    for h in range(2):
                        after(pe, "dn_lo", 2 * ch + h + 1)
                        for m in range(CH):
                            for j, (w, x) in enumerate(terms):
                                ins = pe.matmul(ps_y[:, m, h, :], w[:, k, m * P:(m + 1) * P], x[:, h * HALF:(h + 1) * HALF],
                                                start=(first and j == 0), stop=(last and j == 2))
                    ins.then_inc(s["down_done"], 1)

                twos(pe, gate_up, rows)
                twos(pe, down)

            left = {n: 1 for n in ("router_done", "shared_ready", "comb_ready", "rows_done", "rows_ready")}
            left.update(ld_gate=32, gu_done=2 * NCH, silu_done=2 * NCH, prod_ready=2 * NCH, hid_ready=NCH, down_done=NCH)
            left.update(x_hi=2, x_lo=2, gu_hi=NCH, gu_lo=NCH, dn_hi=2 * NCH, dn_lo=2 * NCH)
            for k in range(2):
                left[f"gu{k}"] = left[f"dn{k}"] = 16 * len(range(k, NCH, 2))
            for n in moe_left:
                moe_left[n] += left[n]


    def stage_l1_attn(l):
        TP = T + 6
        RC = 3
        rows = (P, P, R1 - 2 * P)
        with ExitStack() as st:
            def sb(n, shape, dt=F32):
                return st.enter_context(nc.sbuf_tensor("R_" + n, shape, dt))

            sig = sb("sig", [P, CH, NT])
            w1 = sb("w1", [P, CH, RC * P])
            wconv = sb("wconv", [P, 10, R1])
            wgate = sb("wgate", [P, 2, RC, R1])
            w2 = sb("w2", [P, RC, C])
            hid = sb("hid", [P, CH, NB, TP])
            hid2 = sb("hid2", [P, NB, TP])
            conv = sb("conv", [P, RC, NT])
            rec = sb("rec", [P, RC, NT])
            inp = sb("inp", [P, RC, NT])
            mul = sb("mul", [P, RC, NT])
            lam = sb("lam", [P, 6, RC])
            ps = st.enter_context(nc.psum_tensor("R_ps", [P, 8, HALF], F32))
            names = ("ld_w1 ld_conv ld_gate ld_w2 zeroed done evac lam_ln "
                     "lam_ready a2_ready one_minus root_ready ix_ready scan_ready out_read").split()
            s = {n: sem("R_" + n) for n in names}
            block = st.enter_context(nc.Block())
            G_CONV, G_GATE, G_OUT = 6, 12, 24
            h512 = lambda h: slice(h * HALF, (h + 1) * HALF)

            @block.sync
            def _(sp):
                sp.dma_start(w1[:, :, :], io["l1_w1"]).then_inc(s["ld_w1"], 16)
                sp.wait_ge(s["ld_w1"], 16)
                sp.dma_start(wconv[:, :, :], io["l1_conv"]).then_inc(s["ld_conv"], 16)
                sp.dma_start(wgate[:, :, :, :], io["l1_gate"]).then_inc(s["ld_gate"], 16)
                sp.dma_start(w2[:, :, :], io["l1_w2"]).then_inc(s["ld_w2"], 16)

            @block.gpsimd
            def _(pool):
                pool.memset(hid[:, :, :, :], 0.0)
                pstep.link(pool.memset(hid2[:, :, :], 0.0))
                pstep.link(pool.memset(conv[64:P, 2, :], 0.0))
                pool.memset(inp[64:P, 2, :], 0.0).then_inc(s["zeroed"], 1)
                block_pool(pool, l + 1)
                for h in range(2):
                    pool.wait_ge(s["evac"], G_GATE + 6 * (h + 1))
                    for f in range(RC):
                        n = rows[f]
                        ins = pool.tensor_tensor(inp[0:n, f, h512(h)], inp[0:n, f, h512(h)], conv[0:n, f, h512(h)], ALU.mult)
                        if f == RC - 2:
                            pstep.link(ins)
                    ins.then_inc(s["ix_ready"], 1)
                    pool.wait_ge(s["ix_ready"], h + 1)

            @block.scalar
            def _(act):
                condition_act(act, sig)
                astep.link(act.activation(lam[:, 0, :], vecs[:, VEC["lam"][0]:VEC["lam"][0] + RC], ACT.Abs))
                astep.link(act.activation(lam[:, 1, :], lam[:, 0, :], ACT.Exp, scale=-1.0))
                act.activation(lam[:, 2, :], lam[:, 1, :], ACT.Ln, bias=1.0).then_inc(s["lam_ln"], 1)
                act.wait_ge(s["zeroed"], 1)
                pair = lambda x: x.rearrange("p (b t) -> p b t", b=2)
                for h in range(2):
                    for f in range(RC):
                        g = 3 * h + f
                        act.wait_ge(s["done"], g + 1)
                        if f < 2:
                            ins = act.activation(hid[:, f, 2 * h:2 * h + 2, 3:3 + T], pair(ps[:, g, :]), ACT.Silu, bias=vec("b1", f))
                        else:
                            act.activation(hid2[0:64, 2 * h:2 * h + 2, 3:3 + T], pair(ps[0:64, g, :]), ACT.Silu,
                                           bias=vec("b1", f)[0:64, :])
                            ins = act.activation(hid2[64:P, 2 * h:2 * h + 2, 1:1 + T], pair(ps[64:P, g, :]), ACT.Silu,
                                                 bias=vec("b1", f)[64:P, :])
                        ins.then_inc(s["evac"], 1)
                for h in range(2):
                    for f in range(RC):
                        g, n = G_CONV + 3 * h + f, rows[f]
                        for i in range(NP * (g - G_CONV) // 6, NP * (g - G_CONV + 1) // 6):
                            piece_act(act, l + 1, i, i % 2)
                        act.wait_ge(s["done"], g + 1)
                        act.activation(conv[0:n, f, h512(h)], ps[0:n, g % 8, :], ACT.Identity,
                                       bias=vec("convb", f)[0:n, :]).then_inc(s["evac"], 1)
                for h in range(2):
                    for f in range(RC):
                        for j, (dst, b) in enumerate(((rec, "ba"), (inp, "bx"))):
                            g, n = G_GATE + 6 * h + 2 * f + j, rows[f]
                            act.wait_ge(s["done"], g + 1)
                            act.activation(dst[0:n, f, h512(h)], ps[0:n, g % 8, :], ACT.Sigmoid,
                                           bias=vec(b, f)[0:n, :]).then_inc(s["evac"], 1)
                act.wait_ge(s["lam_ready"], 1)
                act.wait_ge(s["evac"], G_OUT)
                for h in range(2):
                    for f in range(RC):
                        n = rows[f]
                        astep.mark(act.activation(mul[0:n, f, h512(h)], rec[0:n, f, h512(h)], ACT.Exp, scale=lam[0:n, 5, f:f + 1]))
                    astep.wait()
                    for f in range(RC):
                        n = rows[f]
                        ins = act.activation(rec[0:n, f, h512(h)], rec[0:n, f, h512(h)], ACT.Exp, scale=lam[0:n, 4, f:f + 1])
                    ins.then_inc(s["a2_ready"], 1)
                for h in range(2):
                    act.wait_ge(s["one_minus"], h + 1)
                    for f in range(RC):
                        n = rows[f]
                        ins = act.activation(mul[0:n, f, h512(h)], mul[0:n, f, h512(h)], ACT.Sqrt, bias=1.0)
                    ins.then_inc(s["root_ready"], 1)
                next_sigmoid(act, l + 1)

            @block.vector
            def _(dve):
                lv = vecs[:, VEC["lam"][0]:VEC["lam"][0] + RC]
                condition_dve(dve, l, sig)
                dstep.link(dve.tensor_scalar(lam[:, 3, :], lv, 0.0, None, ALU.max))
                dve.wait_ge(s["lam_ln"], 1)
                dstep.link(dve.tensor_tensor(lam[:, 3, :], lam[:, 3, :], lam[:, 2, :], ALU.add))
                dstep.mark(dve.tensor_scalar(lam[:, 4, :], lam[:, 3, :], -8.0, None, ALU.mult))
                dve.tensor_scalar(lam[:, 5, :], lam[:, 3, :], -16.0, None, ALU.mult).then_inc(s["lam_ready"], 1)
                block_dve(dve, l + 1)
                for h in range(2):
                    dve.wait_ge(s["a2_ready"], h + 1)
                    for f in range(RC):
                        n = rows[f]
                        ins = dve.tensor_scalar(mul[0:n, f, h512(h)], mul[0:n, f, h512(h)], 1.0, -1.0, ALU.min, ALU.mult)
                    ins.then_inc(s["one_minus"], 1)
                for h in range(2):
                    dve.wait_ge(s["root_ready"], h + 1)
                    dve.wait_ge(s["ix_ready"], h + 1)
                    for f in range(RC):
                        n = rows[f]
                        dstep.link(dve.tensor_tensor(mul[0:n, f, h512(h)], mul[0:n, f, h512(h)], inp[0:n, f, h512(h)], ALU.mult))
                    for f in range(RC):
                        n = rows[f]
                        for b in (2 * h, 2 * h + 1):
                            c = slice(b * T, (b + 1) * T)
                            ins = dve.tensor_tensor_scan(inp[0:n, f, c], rec[0:n, f, c], mul[0:n, f, c], 0.0, ALU.mult, ALU.add)
                    ins.then_inc(s["scan_ready"], 1)
                for h in range(2):
                    for m in range(CH):
                        dve.wait_ge(s["done"], G_OUT + 2 * h + m + 1)
                        x = xT[:, m, h512(h)]
                        dstep.link(dve.scalar_tensor_tensor(out=x, in0=ps[:, (G_OUT + 2 * h + m) % 8, :], scalar=vec("b2", m),
                                                            in1=x, op0=ALU.add, op1=ALU.add))

            @block.tensor
            def _(pe):
                group = [0]

                def product(pairs, n):
                    g = group[0]
                    group[0] += 1
                    if g >= 8:
                        pe.wait_ge(s["evac"], g - 7)
                    for i, (w, x) in enumerate(pairs):
                        ins = pe.matmul(ps[0:n, g % 8, :], w, x, start=(i == 0), stop=(i == len(pairs) - 1))
                    ins.then_inc(s["done"], 1)

                pe.wait_ge(s["ld_w1"], 16)
                for h in range(2):
                    pe.wait_ge(xin_ready, 2 * l + 1 + h)
                    for f in range(RC):
                        product([(w1[:, k, f * P:(f + 1) * P], xin[:, k, h512(h)]) for k in range(CH)], P)
                pe.wait_ge(s["ld_conv"], 16)
                for h in range(2):
                    pe.wait_ge(s["evac"], 3 * (h + 1))
                    b = slice(2 * h, 2 * h + 2)
                    for f in range(RC):
                        c = slice(f * P, f * P + rows[f])
                        product([(wconv[:, 2 * k + i, c], hid[:, i, b, 2 * k:2 * k + T]) for k in range(TAPS) for i in range(CH)]
                                + [(wconv[:, 8 + q, c], hid2[:, b, 4 * q:4 * q + T]) for q in range(2)], rows[f])
                pe.wait_ge(s["ld_gate"], 16)
                for h in range(2):
                    pe.wait_ge(s["evac"], G_CONV + 3 * (h + 1))
                    for f in range(RC):
                        c = slice(f * P, f * P + rows[f])
                        for j in range(2):
                            product([(wgate[:, j, k, c], conv[:, k, h512(h)]) for k in range(RC)], rows[f])
                pe.wait_ge(s["ld_w2"], 16)
                for h in range(2):
                    pe.wait_ge(s["scan_ready"], h + 1)
                    for m in range(CH):
                        product([(w2[:, k, m * P:(m + 1) * P], inp[:, k, h512(h)]) for k in range(RC)], P)


    def stage_l1_ffn(l):
        HC = FF // P
        with ExitStack() as st:
            def sb(n, shape, dt=F32):
                return st.enter_context(nc.sbuf_tensor("E_" + n, shape, dt))

            tok = sb("tok", [P, 8, C])
            sig = tok[:, :, :].rearrange("p a b -> p (a b)").rearrange("p (c t) -> p c t", c=CH)
            wgate = sb("wgate", [P, CH, NE])
            rank = sb("rank", [P, 8, NE])
            seq = sb("seq", [P, 4, 8 * 2 * NE])
            ids = sb("ids", [P, CAP + 16])
            lt = sb("lt", [P, 4, 8, NE])
            one = sb("one", [P, 4, 8])
            gates = sb("gates", [P, 16])
            hot = sb("hot", [P, NE * 16])
            before = sb("before", [P, NE * 16])
            token = sb("token", [P, 16, NE])
            part16 = sb("part16", [P, 2, 16, NE])
            col = sb("col", [P, 6, 16])
            sloti = sb("sloti", [P, 16], U32)
            tokeni = sb("tokeni", [P, 16], U32)
            fc1 = sb("fc1", [P, 2, CH, FF])
            fc2 = sb("fc2", [P, 2, HC, C])
            fc2b = sb("fc2b", [P, NE, C])
            rows = sb("rows", [P, 16, C])
            dT = sb("dT", [P, CH, SLOTS])
            hid = sb("hid", [P, 2, HC, CAP])
            fc1b = sb("fc1b", [P, 2, HC])
            eo = sb("eo", [P, 2, 2, C])
            same = rows
            choice = lt[:, 2:4, :, :].rearrange("p k t e -> p (k t) e")
            ps = st.enter_context(nc.psum_tensor("E_ps", [P, 8, HALF], F32))
            names = ("ld_gate ld_fc2b fc1_0 fc1_1 fc2_0 fc2_1 router_done x_turned tok_ready tok_stored "
                     "before_ready count_done same_ready token_done token_ready slot_ready rows0 rows1 rows2 rows3 "
                     "rows_turned dT_act dT_dve fc1_done gelu_done fc2_done eo_ready eo_st0 eo_st1 bias_ready "
                     "y_ready y_turned").split()
            s = {n: sem("E_" + n) for n in names}
            block = st.enter_context(nc.Block())

            def experts(eng, body):
                with eng.Fori(0, NE // 2) as j:
                    body(2 * j, 0, j)
                    body(2 * j + 1, 1, j)

            @block.sync
            def _(sp):
                sp.dma_start(wgate[:, :, :], io["l1_wg"]).then_inc(s["ld_gate"], 16)
                sp.dma_start(rank[:, :, :], io["rank"]).then_inc(s["ld_gate"], 16)
                sp.dma_start(seq[:, :, :], io["seq"]).then_inc(s["ld_gate"], 16)
                sp.dma_start(ids[:, :], io["ids"]).then_inc(s["ld_gate"], 16)
                sp.dma_start(fc2b[:, :, :].rearrange("p e d -> p (e d)"), io["l1_fc2b"].to_broadcast([P, NE * C])) \
                    .then_inc(s["ld_fc2b"], 16)

                def load(e, k):
                    sp.wait_ge(s["fc1_done"], HC // 2 * (e + 1))
                    sp.dma_start(fc1[:, k, :, :].rearrange("p a f -> p (a f)"), io["l1_fc1"][e]).then_inc(s[f"fc1_{k}"], 16)
                    sp.wait_ge(s["fc2_done"], e + 1)
                    sp.dma_start(fc2[:, k, :, :].rearrange("p a f -> p (a f)"), io["l1_fc2"][e]).then_inc(s[f"fc2_{k}"], 16)

                def store(e, k):
                    sp.wait_ge(s["eo_ready"], e + 3)
                    sp.dma_start(eo_dram[ds(e * CAP, CAP), :].rearrange("(a p) d -> p a d", p=P), eo[:, k, :, :]) \
                        .then_inc(s[f"eo_st{k}"], 16)

                for k in range(2):
                    sp.sem_inc(s[f"eo_st{k}"], 16)
                load(0, 0)
                load(1, 1)
                with sp.Fori(1, NE // 2) as j:
                    for k in range(2):
                        load(2 * j + k, k)
                        store(2 * j + k - 2, k)
                for k in range(2):
                    store(NE - 2 + k, k)

            @block.gpsimd
            def _(pool):
                pool.wait_ge(s["tok_stored"], 16)
                pool.wait_ge(s["token_ready"], 1)
                for i in range(16):
                    pool.indirect_dma_start(out=rows[:, i, :], out_offset=None, in_=tok_dram,
                                            in_offset=bass.IndirectOffsetOnAxis(ap=tokeni[:, i:i + 1], axis=0),
                                            bounds_check=NT - 1, oob_is_err=False).then_inc(s[f"rows{i // 4}"], 16)
                with pool.Fori(0, NE // 2) as j:
                    pstep.enter(j, 2 * PIECE_POOL_STEPS)
                    for k in range(2):
                        piece_pool(pool, l + 1, 2 * j + k, k)
                pstep.leave(NE // 2)
                for k in range(2):
                    pool.wait_ge(s[f"eo_st{k}"], 16 * (NE // 2 + 1))
                pool.wait_ge(s["slot_ready"], 1)
                for q in range(4):
                    for i in (2 * q, 2 * q + 1, 8 + 2 * q, 9 + 2 * q):
                        pool.indirect_dma_start(out=rows[:, i, :], out_offset=None, in_=eo_dram,
                                                in_offset=bass.IndirectOffsetOnAxis(ap=sloti[:, i:i + 1], axis=0),
                                                bounds_check=SLOTS - 1, oob_is_err=False).then_inc(s[f"rows{q}"], 16)

            @block.scalar
            def _(act):
                act.sem_inc(s["gelu_done"], HC // 2)
                condition_act(act, sig)
                route_act(act, lt, 2)
                act.wait_ge(s["x_turned"], 1)
                for j in range(4):
                    ins = act.activation(tok[:, 2 * j:2 * j + 2, :].rearrange("p a b -> p (a b)"), ps[:, 4 + j, :], ACT.Identity)
                ins.then_inc(s["tok_ready"], 1)
                act.wait_ge(s["tok_ready"], 1)
                act.dma_start(tok_dram.rearrange("(t p) d -> p t d", p=P), tok[:, :, :]).then_inc(s["tok_stored"], 16)

                def turned(g):
                    act.wait_ge(s["rows_turned"], g + 1)
                    act.activation(dT[:, 0, g * HALF:(g + 1) * HALF], ps[:, 6, :], ACT.Identity).then_inc(s["dT_act"], 1)

                def gelu(e, k, j):
                    act.wait_ge(s["bias_ready"], e + 1)
                    act.wait_ge(s["fc2_done"], e + 1)
                    for h in range(HC // 2):
                        act.wait_ge(s["fc1_done"], HC // 2 * e + h + 1 + HC)
                        for i in range(2):
                            ins = act.activation(hid[:, k, 2 * h + i, :], ps[:, h, i * CAP:(i + 1) * CAP], ACT.Gelu,
                                                 bias=fc1b[:, k, 2 * h + i:2 * h + i + 1])
                        ins.then_inc(s["gelu_done"], 1)

                def gelu_piece(e, k, j):
                    gelu(e, k, j)
                    piece_act(act, l + 1, e, k)

                turned(0)
                turned(1)
                gelu(0, 0, 0)
                turned(2)
                turned(3)
                piece_act(act, l + 1, 0, 0)
                gelu_piece(1, 1, 0)
                with act.Fori(1, NE // 2) as j:
                    for k in range(2):
                        gelu_piece(2 * j + k, k, j)
                next_sigmoid(act, l + 1)

            @block.vector
            def _(dve):
                dve.sem_inc(s["eo_ready"], 2)
                condition_dve(dve, l, sig)
                dve.wait_ge(s["router_done"], 1)
                dve.wait_ge(s["ld_gate"], 64)
                dstep.link(dve.tensor_copy(lt[:, 0, :, :], ps[:, 0, 0:8 * NE].rearrange("p (t e) -> p t e", t=8)))
                route_dve(dve, lt, one, rank[:, :, :], 2)
                dstep.link(dve.tensor_copy(hot[:, :].rearrange("p (e i) -> p i e", e=NE), choice))
                dve.tensor_tensor_scan(before[:, :], seq[:, 2, :], hot[:, :], 0.0, ALU.mult, ALU.add).then_inc(s["before_ready"], 1)
                of = lambda v: v.unsqueeze(2).to_broadcast([P, 16, NE])
                dve.tensor_tensor(token[:, :, :], choice, of(ids[:, CAP:CAP + 16]), ALU.mult)
                dstep.link(dve.tensor_tensor(part16[:, 0, :, :], choice, seq[:, 3, :].rearrange("p (i e) -> p i e", e=NE), ALU.mult))
                dstep.mark(dve.tensor_reduce(col[:, 3, :], part16[:, 0, :, :], AX_X, ALU.add))
                dve.wait_ge(s["count_done"], 1)
                dstep.link(dve.tensor_tensor(part16[:, 1, :, :], choice, ps[:, 1, 0:16 * NE].rearrange("p (e i) -> p i e", e=NE), ALU.mult))
                dstep.link(dve.tensor_reduce(col[:, 0, :], part16[:, 1, :, :], AX_X, ALU.add))
                dstep.link(dve.tensor_scalar(col[:, 1, :], col[:, 0, :], -1.0, None, ALU.add))
                for i in range(16):
                    dve.tensor_scalar(same[:, i, :], ids[:, 0:CAP], col[:, 1, i:i + 1], None,
                                      ALU.is_equal).then_inc(s["same_ready"], 1)
                dve.wait_ge(s["token_done"], 1)
                dve.tensor_copy(tokeni[:, :].rearrange("p (e a) -> p a e", a=2),
                                ps[:, 2, 0:16].rearrange("p (a e) -> p a e", a=2)).then_inc(s["token_ready"], 1)
                dstep.link(dve.tensor_tensor(one[:, 2, :], one[:, 0, :], one[:, 1, :], ALU.add))
                dstep.link(dve.tensor_scalar(one[:, 2, :], one[:, 2, :], 1e-9, None, ALU.max))
                dstep.link(dve.reciprocal(one[:, 2, :], one[:, 2, :]))
                for k in range(2):
                    dstep.mark(dve.tensor_tensor(gates[:, 8 * k:8 * k + 8], one[:, k, :], one[:, 2, :], ALU.mult))
                dstep.link(dve.tensor_scalar(col[:, 2, :], col[:, 0, :], float(CAP), None, ALU.is_le))
                dstep.mark(dve.tensor_tensor(gates[:, :], gates[:, :], col[:, 2, :], ALU.mult))
                dstep.link(dve.tensor_tensor(col[:, 4, :], col[:, 1, :], col[:, 2, :], ALU.mult))
                dstep.link(dve.tensor_tensor(col[:, 4, :], col[:, 4, :], col[:, 3, :], ALU.add))
                dve.tensor_copy(sloti[:, :], col[:, 4, :]).then_inc(s["slot_ready"], 1)
                def biases(e, k):
                    dve.tensor_scalar(fc1b[:, k, :], vecs[:, ds(HC * e + VEC["fc1b"][0], HC)], 1.0, None, ALU.mult) \
                        .then_inc(s["bias_ready"], 1)

                def store_rows(e, k, j):
                    piece_scans(dve, l + 1, e, k)
                    dve.wait_ge(s["fc2_done"], e + 3)
                    dve.wait_ge(s[f"eo_st{k}"], 16 * j + 16)
                    dve.tensor_tensor(eo[:, k, :, :], ps[:, 4 + k, :].rearrange("p (a d) -> p a d", a=2),
                                      fc2b[:, ds(e, 1), :].to_broadcast([P, 2, C]), ALU.add).then_inc(s["eo_ready"], 1)
                    piece_finish(dve, l + 1, e, k)

                for k in range(2):
                    biases(k, k)
                for g in range(4):
                    dve.wait_ge(s["rows_turned"], g + 1)
                    dve.tensor_copy(dT[:, 1, g * HALF:(g + 1) * HALF], ps[:, 7, :]).then_inc(s["dT_dve"], 1)
                dve.wait_ge(s["ld_fc2b"], 16)
                with dve.Fori(0, NE // 2 - 1) as j:
                    dstep.enter(j, 2 * PIECE_DVE_STEPS)
                    for k in range(2):
                        store_rows(2 * j + k, k, j)
                        biases(2 * j + k + 2, k)
                dstep.leave(NE // 2 - 1)
                for k in range(2):
                    store_rows(NE - 2 + k, k, NE // 2 - 1)
                for q in range(4):
                    dve.wait_ge(s[f"rows{q}"], 128)
                    for t in (2 * q, 2 * q + 1):
                        ins = dve.tensor_scalar(tok[:, t, :], rows[:, t, :], gates[:, t:t + 1], None, ALU.mult)
                    dstep.link(ins)
                    for t in (2 * q, 2 * q + 1):
                        ins = dve.scalar_tensor_tensor(out=tok[:, t, :], in0=rows[:, 8 + t, :], scalar=gates[:, 8 + t:9 + t],
                                                       in1=tok[:, t, :], op0=ALU.mult, op1=ALU.add)
                    ins.then_inc(s["y_ready"], 1)
                for h in range(2):
                    dve.wait_ge(s["y_turned"], 2 * h + 2)
                    for ch in range(CH):
                        x = xT[:, ch, h * HALF:(h + 1) * HALF]
                        dstep.link(dve.tensor_tensor(x, x, ps[:, 2 * ch + h, :], ALU.add))

            @block.tensor
            def _(pe):
                pe.sem_inc(s["fc1_done"], HC)
                pe.sem_inc(s["fc2_done"], 2)
                pe.wait_ge(s["ld_gate"], 64)
                pe.wait_ge(xin_ready, 2 * l + 2)
                for t in range(8):
                    for k in range(CH):
                        ins = pe.matmul(ps[:, 0, t * NE:(t + 1) * NE], xin[:, k, t * P:(t + 1) * P], wgate[:, k, :],
                                        start=(k == 0), stop=(k == CH - 1))
                ins.then_inc(s["router_done"], 1)
                for t in range(8):
                    for k in range(CH):
                        ins = pe.transpose(ps[:, 4 + t // 2, t % 2 * C + k * P:t % 2 * C + (k + 1) * P],
                                           xin[:, k, t * P:(t + 1) * P], ident[:, :])
                ins.then_inc(s["x_turned"], 1)
                pe.wait_ge(s["before_ready"], 1)
                pe.matmul(ps[:, 1, 0:16 * NE], seq[:, 1, :], before[:, :], start=True, stop=False)
                pe.matmul(ps[:, 1, 0:16 * NE], seq[:, 0, :], hot[:, :],
                          start=False, stop=True).then_inc(s["count_done"], 1)
                for a in range(2):
                    for i in range(16):
                        if a == 0:
                            pe.wait_ge(s["same_ready"], i + 1)
                        ins = pe.matmul(ps[:, 2, a * NE:(a + 1) * NE], same[:, i, a * P:(a + 1) * P], token[:, i, :],
                                        start=(i == 0), stop=(i == 15))
                ins.then_inc(s["token_done"], 1)

                def turn(g):
                    pe.wait_ge(s[f"rows{g}"], 64)
                    if g == 0:
                        pe.wait_ge(s["tok_ready"], 1)
                    else:
                        pe.wait_ge(s["dT_act"], g)
                        pe.wait_ge(s["dT_dve"], g)
                    for a in range(4):
                        for k in range(CH):
                            ins = pe.transpose(ps[:, 6 + k, a * P:(a + 1) * P], rows[:, 4 * g + a, k * P:(k + 1) * P], ident[:, :])
                    ins.then_inc(s["rows_turned"], 1)

                def up(e, k, n):
                    pe.wait_ge(s[f"fc1_{k}"], 16 * n + 16)
                    for h in range(HC // 2):
                        pe.wait_ge(s["gelu_done"], HC // 2 * e + h + 1)
                        for i in range(2):
                            f = (2 * h + i) * P
                            for c in range(CH):
                                ins = pe.matmul(ps[:, h, i * CAP:(i + 1) * CAP], fc1[:, k, c, f:f + P],
                                                dT[:, c, ds(e * CAP, CAP)], start=(c == 0), stop=(c == CH - 1))
                        ins.then_inc(s["fc1_done"], 1)

                def down(e, k, n):
                    pe.wait_ge(s[f"fc2_{k}"], 16 * n + 16)
                    pe.wait_ge(s["gelu_done"], HC // 2 * (e + 2))
                    pe.wait_ge(s["eo_ready"], e + 1)
                    for a in range(2):
                        for h in range(HC):
                            ins = pe.matmul(ps[:, 4 + k, a * C:(a + 1) * C], hid[:, k, h, a * P:(a + 1) * P], fc2[:, k, h, :],
                                            start=(h == 0), stop=(h == HC - 1))
                    ins.then_inc(s["fc2_done"], 1)

                turn(0)
                turn(1)
                pe.wait_ge(s["dT_act"], 1)
                pe.wait_ge(s["dT_dve"], 1)
                up(0, 0, 0)
                turn(2)
                turn(3)
                pe.wait_ge(s["dT_act"], 4)
                pe.wait_ge(s["dT_dve"], 4)
                with pe.Fori(0, NE // 2 - 1) as j:
                    up(2 * j + 1, 1, j)
                    down(2 * j, 0, j)
                    up(2 * j + 2, 0, j + 1)
                    down(2 * j + 1, 1, j)
                up(NE - 1, 1, NE // 2 - 1)
                down(NE - 2, 0, NE // 2 - 1)
                down(NE - 1, 1, NE // 2 - 1)
                for q in range(4):
                    pe.wait_ge(s["y_ready"], q + 1)
                    for t in (2 * q, 2 * q + 1):
                        for k in range(CH):
                            ins = pe.transpose(ps[:, 2 * k + t // 4, t % 4 * P:(t % 4 + 1) * P], tok[:, t, k * P:(k + 1) * P],
                                               ident[:, :])
                    ins.then_inc(s["y_turned"], 1)


    def stage_l2_attn(l):
        PAIRS, PER, HS = L2_PAIRS, 4, HD + 1
        ITER = PAIRS // 2
        STEPS = PER * ITER
        with ExitStack() as st:
            def sb(n, shape, dt=F32):
                return st.enter_context(nc.sbuf_tensor("K_" + n, shape, dt))

            sig = sb("sig", [P, CH, NT])
            wqkv = sb("wqkv", [P, 2, CH, 3 * P])
            wo = sb("wo", [P, 2, C])
            qT = sb("qT", [P, 2, HALF])
            ks = sb("ks", [P, 2, 4, P])
            vs = sb("vs", [P, 2, 4, 2, HS])
            kv = sb("kv", [P, 2, 2, 2 * HS])
            quot = sb("quot", [P, 4, P])
            norm = sb("norm", [P, 2, 4])
            oT_hi, oT_lo = sb("oT_hi", [P, 2, HALF], F32R), sb("oT_lo", [P, 2, HALF], F32R)
            xin_hi, xin_lo = sb("xin_hi", [P, CH, NT], F32R), sb("xin_lo", [P, CH, NT], F32R)
            wqkv_hi, wqkv_lo = sb("wqkv_hi", [P, 2, CH, 3 * P], F32R), sb("wqkv_lo", [P, 2, CH, 3 * P], F32R)
            wo_hi, wo_lo = sb("wo_hi", [P, 2, C], F32R), sb("wo_lo", [P, 2, C], F32R)
            ps_q = st.enter_context(nc.psum_tensor("K_ps_q", [P, HALF], F32))
            ps_kvp = st.enter_context(nc.psum_tensor("K_ps_kvp", [P, 2, 2, 2 * P], F32))
            ps_kv = st.enter_context(nc.psum_tensor("K_ps_kv", [P, HALF], F32))
            ps_o = st.enter_context(nc.psum_tensor("K_ps_o", [P, 2, HALF], F32))
            ps_t = st.enter_context(nc.psum_tensor("K_ps_t", [P, HALF], F32))
            ps_y = st.enter_context(nc.psum_tensor("K_ps_y", [P, HALF], F32))
            names = ("wqkv0 wqkv1 wo0 wo1 zeroed q_done q_evac kvp_done kvp_evac kv_done kv_evac o_done quot_ready "
                     "t_done t_evac t_low y_done y_added x_hi x_lo w_hi w_lo wo_hi wo_lo").split()
            s = {n: sem("K_" + n) for n in names}
            block = st.enter_context(nc.Block())

            def loop(eng, step, per=0, count=None):
                for j in range(PER):
                    step(j, j, 0)
                if count:
                    assert count.n - loop.start == per, (count.n - loop.start, per)
                with eng.Fori(1, ITER - 1) as i:
                    if count:
                        count.enter(i - 1, per)
                    for j in range(PER):
                        step(PER * i + j, j, i)
                if count:
                    count.leave(ITER - 2)
                for j in range(PER):
                    step(PER * (ITER - 1) + j, j, ITER - 1)

            def half_of(x, h):
                return x[:, :, h * HALF:(h + 1) * HALF]

            def next_split(split, j, i):
                if j % 2 == 0 and not (isinstance(i, int) and 2 * i + j // 2 == PAIRS - 1):
                    split(2 * i + j // 2 + 1, 1 - j // 2, i + j // 2)

            @block.sync
            def _(sp):
                def load(p, k):
                    need(sp, s["w_lo"], p - 1)
                    sp.dma_start(wqkv[:, k, :, :].rearrange("p a b -> p (a b)"), io["l2_wqkv"][p]).then_inc(s[f"wqkv{k}"], 16)
                    need(sp, s["wo_lo"], p - 1)
                    sp.dma_start(wo[:, k, :], io["l2_wo"][p]).then_inc(s[f"wo{k}"], 16)

                for k in range(2):
                    load(k, k)
                with sp.Fori(1, ITER) as i:
                    for k in range(2):
                        load(2 * i + k, k)

            @block.gpsimd
            def _(pool):
                pstep.mark(pool.memset(kv[:, :, :, :], 0.0))
                pool.memset(vs[:, :, :, :, HD:HS], 1.0).then_inc(s["zeroed"], 1)

                def split(p, k, n):
                    pool.wait_ge(s["w_hi"], p + 1)
                    pool.tensor_tensor(wqkv_lo[:, k, :, :], wqkv[:, k, :, :], wqkv_hi[:, k, :, :],
                                       ALU.subtract).then_inc(s["w_lo"], 1)

                def split_wo(p, k):
                    pool.wait_ge(s["wo_hi"], p + 1)
                    pool.tensor_tensor(wo_lo[:, k, :], wo[:, k, :], wo_hi[:, k, :], ALU.subtract).then_inc(s["wo_lo"], 1)

                def parts(i):
                    for j in range(0, PER, 2):
                        next_split(split, j, i)
                        split_wo(2 * i + j // 2, j // 2)
                        for k in ((0, 1), (2,))[j // 2]:
                            piece_pool(pool, l + 1 + k, i, k % 2)

                split(0, 0, 0)
                with pool.Fori(0, ITER - 1) as i:
                    pstep.enter(i, 3 * PIECE_POOL_STEPS)
                    parts(i)
                pstep.leave(ITER - 1)
                parts(ITER - 1)

            @block.scalar
            def _(act):
                def split(p, k, n):
                    act.wait_ge(s[f"wqkv{k}"], 16 * n + 16)
                    need(act, s["kvp_done"], 4 * (p - 1))
                    act.activation(wqkv_hi[:, k, :, :], wqkv[:, k, :, :], ACT.Identity).then_inc(s["w_hi"], 1)

                def split_wo(p, k, n):
                    act.wait_ge(s[f"wo{k}"], 16 * n + 16)
                    need(act, s["y_done"], 4 * (p - 1))
                    act.activation(wo_hi[:, k, :], wo[:, k, :], ACT.Identity).then_inc(s["wo_hi"], 1)

                condition_act(act, sig)
                split(0, 0, 0)
                for h in range(2):
                    act.wait_ge(xin_ready, 2 * l + 1 + h)
                    act.activation(half_of(xin_hi, h), half_of(xin, h), ACT.Identity).then_inc(s["x_hi"], 1)
                act.wait_ge(s["zeroed"], 1)

                def step(n, j, i):
                    act.wait_ge(s["q_done"], n + 1)
                    need(act, s["o_done"], n - 1)
                    act.activation(qT[:, j % 2, :], ps_q[:, :], ACT.Relu).then_inc(s["q_evac"], 1)
                    need(act, s["kv_done"], n - 1)
                    for h in range(2):
                        act.wait_ge(s["kvp_done"], 2 * n + h + 1)
                        act.activation(ks[:, j % 2, 2 * h:2 * h + 2, :], ps_kvp[:, h, :, 0:P], ACT.Relu)
                        act.activation(vs[:, j % 2, 2 * h:2 * h + 2, :, 0:HD],
                                       ps_kvp[:, h, :, P:2 * P].rearrange("p a (r d) -> p a r d", r=2),
                                       ACT.Identity).then_inc(s["kvp_evac"], 1)
                    if j > 0:
                        piece_act(act, l + j, i, (j - 1) % 2)
                    if not isinstance(n, int) or n:
                        turned(n - 1, (j + 1) % 2)
                    next_split(split, j, i)
                    if j % 2 == 0:
                        split_wo(2 * i + j // 2, j // 2, i)

                def turned(n, k):
                    act.wait_ge(s["t_done"], n + 1)
                    need(act, s["y_done"], 2 * (n - 1))
                    act.activation(oT_hi[:, k, :], ps_t[:, :], ACT.Identity).then_inc(s["t_evac"], 1)

                loop(act, step)
                turned(STEPS - 1, 1)
                next_sigmoid(act, l + 1)

            @block.vector
            def _(dve):
                def turned(n, k):
                    dve.wait_ge(s["t_evac"], n + 1)
                    dve.tensor_tensor(oT_lo[:, k, :], ps_t[:, :], oT_hi[:, k, :], ALU.subtract).then_inc(s["t_low"], 1)

                condition_dve(dve, l, sig)
                for h in range(2):
                    dve.wait_ge(s["x_hi"], h + 1)
                    dve.tensor_tensor(half_of(xin_lo, h), half_of(xin, h), half_of(xin_hi, h),
                                      ALU.subtract).then_inc(s["x_lo"], 1)
                for ch in range(CH):
                    dstep.link(dve.tensor_scalar(xT[:, ch, :], xT[:, ch, :], vec("bo2", ch), None, ALU.add))
                dve.wait_ge(s["zeroed"], 1)

                def add(n, j, ch):
                    dve.wait_ge(s["y_done"], 2 * n + ch + 1)
                    x = xT[:, ch, j % 2 * HALF:(j % 2 + 1) * HALF]
                    dve.tensor_tensor(x, x, ps_y[:, :], ALU.add).then_inc(s["y_added"], 1)

                def step(n, j, i):
                    dve.wait_ge(s["kv_done"], n + 1)
                    need(dve, s["o_done"], n - 1)
                    for r in range(2):
                        h = slice(HD * r, HD * r + HD)
                        ins = dve.tensor_copy(kv[h, j % 2, :, HS * r:HS * r + HS],
                                              ps_kv[h, 0:4 * HS].rearrange("p (b e) -> p b e", b=2)[:, :, HS * r:HS * r + HS])
                    ins.then_inc(s["kv_evac"], 1)
                    earlier = not isinstance(n, int) or n
                    if earlier:
                        turned(n - 1, (j + 1) % 2)
                    dve.wait_ge(s["o_done"], n + 1)
                    o = ps_o[:, :, 0:4 * HS].rearrange("p a (q e) -> p a q e", e=HS)
                    dstep.link(dve.tensor_scalar(norm[:, :, :], o[:, :, :, HD], 1e-6, None, ALU.max))
                    dstep.link(dve.reciprocal(norm[:, :, :], norm[:, :, :]))
                    need(dve, s["t_done"], n)
                    dve.tensor_tensor(quot[:, :, :].rearrange("p (a b) (r e) -> p a (b r) e", a=2, r=2), o[:, :, :, 0:HD],
                                      norm[:, :, :].unsqueeze(3).to_broadcast([P, 2, 4, HD]),
                                      ALU.mult).then_inc(s["quot_ready"], 1)
                    if j < 3:
                        piece_scans(dve, l + 1 + j, i, j % 2)
                    if earlier:
                        add(n - 1, j + 1, 0)
                    if j > 0:
                        piece_finish(dve, l + j, i, (j - 1) % 2)
                    if earlier:
                        add(n - 1, j + 1, 1)

                loop.start = dstep.n
                loop(dve, step, 3 * PIECE_DVE_STEPS + 2 * PER, dstep)
                turned(STEPS - 1, 1)
                for ch in range(CH):
                    add(STEPS - 1, 1, ch)

            @block.tensor
            def _(pe):
                products = lambda w, x: ((w[0], x[0]), (w[0], x[1]), (w[1], x[0]))
                wqkv2, xin2, wo2, oT2 = (wqkv_hi, wqkv_lo), (xin_hi, xin_lo), (wo_hi, wo_lo), (oT_hi, oT_lo)

                def queries(n, j):
                    need(pe, s["q_evac"], n)
                    for k in range(CH):
                        for m, (w, x) in enumerate(products(wqkv2, xin2)):
                            ins = pe.matmul(ps_q[:, :], w[:, j // 2, k, 0:P], half_of(x, j % 2)[:, k, :],
                                            start=(k + m == 0), stop=(k == CH - 1 and m == 2))
                    ins.then_inc(s["q_done"], 1)

                def keys_values(n, j, h):
                    need(pe, s["kvp_evac"], 2 * n - 1 + h)
                    for a in range(2):
                        t = j % 2 * HALF + (2 * h + a) * P
                        for k in range(CH):
                            for m, (w, x) in enumerate(products(wqkv2, xin2)):
                                ins = pe.matmul(ps_kvp[:, h, a, :], x[:, k, t:t + P], w[:, j // 2, k, P:3 * P],
                                                start=(k + m == 0), stop=(k == CH - 1 and m == 2))
                    ins.then_inc(s["kvp_done"], 1)

                def key_value(n, j):
                    pe.wait_ge(s["kvp_evac"], 2 * n + 2)
                    need(pe, s["kv_evac"], n)
                    for b in range(2):
                        for t in range(2):
                            ins = pe.matmul(ps_kv[:, 2 * HS * b:2 * HS * (b + 1)], ks[:, j % 2, 2 * b + t, :],
                                            vs[:, j % 2, 2 * b + t, :, :].rearrange("p r e -> p (r e)"),
                                            start=(t == 0), stop=(t == 1))
                    ins.then_inc(s["kv_done"], 1)

                def weighted(n, j):
                    pe.wait_ge(s["kv_evac"], n + 1)
                    pe.wait_ge(s["q_evac"], n + 1)
                    need(pe, s["quot_ready"], n)
                    for t in range(4):
                        ins = pe.matmul(ps_o[:, t // 2, 2 * HS * (t % 2):2 * HS * (t % 2 + 1)], qT[:, j % 2, t * P:(t + 1) * P],
                                        kv[:, j % 2, t // 2, :], start=True, stop=True)
                    ins.then_inc(s["o_done"], 1)

                def turn(n):
                    pe.wait_ge(s["quot_ready"], n + 1)
                    need(pe, s["t_low"], n)
                    for t in range(4):
                        ins = pe.transpose(ps_t[:, t * P:(t + 1) * P], quot[:, t, :], ident[:, :])
                    ins.then_inc(s["t_done"], 1)

                def output(n, j, ch):
                    need(pe, s["y_added"], 2 * n + ch)
                    for m, (w, o) in enumerate(products(wo2, oT2)):
                        ins = pe.matmul(ps_y[:, :], w[:, j // 2, ch * P:(ch + 1) * P], o[:, j % 2, :],
                                        start=(m == 0), stop=(m == 2))
                    ins.then_inc(s["y_done"], 1)

                def step(n, j, i):
                    first = isinstance(n, int)
                    if j % 2 == 0:
                        pe.wait_ge(s["w_lo"], 2 * i + j // 2 + 1)
                    if first and n < 2:
                        pe.wait_ge(s["x_lo"], n + 1)
                    queries(n, j)
                    if not (first and n < 1):
                        weighted(n - 1, (j + 3) % 4)
                    keys_values(n, j, 0)
                    if not (first and n < 2):
                        k = (j + 2) % 4
                        if k % 2 == 0:
                            pe.wait_ge(s["wo_lo"], 2 * i + 1 if j >= 2 else 2 * i)
                        pe.wait_ge(s["t_low"], n - 1)
                        output(n - 2, k, 0)
                    keys_values(n, j, 1)
                    if not (first and n < 1):
                        turn(n - 1)
                    if not (first and n < 2):
                        output(n - 2, (j + 2) % 4, 1)
                    key_value(n, j)

                loop(pe, step)
                weighted(STEPS - 1, 3)
                pe.wait_ge(s["wo_lo"], PAIRS)
                pe.wait_ge(s["t_low"], STEPS - 1)
                for ch in range(CH):
                    output(STEPS - 2, 2, ch)
                turn(STEPS - 1)
                pe.wait_ge(s["t_low"], STEPS)
                for ch in range(CH):
                    output(STEPS - 1, 3, ch)

    def stage_l2_ffn(l):
        with ExitStack() as st:
            sig = st.enter_context(nc.sbuf_tensor("F_sig", [P, CH, NT], F32))
            w = st.enter_context(nc.sbuf_tensor("F_w", [P, CH, C], F32))
            scaled = st.enter_context(nc.sbuf_tensor("F_scaled", [P, 4, HALF], F32))
            ps = st.enter_context(nc.psum_tensor("F_ps", [P, 4, HALF], F32))
            s = {n: sem("F_" + n) for n in ("ld_w", "done", "scaled")}
            block = st.enter_context(nc.Block())
            half = lambda h: slice(h * HALF, (h + 1) * HALF)

            @block.sync
            def _(sp):
                sp.dma_start(w[:, :, :], io["l2_w"]).then_inc(s["ld_w"], 16)

            @block.scalar
            def _(act):
                condition_act(act, sig)
                for g in range(4):
                    act.wait_ge(s["done"], g + 1)
                    act.activation(scaled[:, g, :], ps[:, g, :], ACT.Identity, scale=vec("fscale", g % 2),
                                   bias=vec("fbias", g % 2)).then_inc(s["scaled"], 1)

            @block.vector
            def _(dve):
                condition_dve(dve, l, sig)
                for g in range(4):
                    dve.wait_ge(s["scaled"], g + 1)
                    x = xT[:, g % 2, half(g // 2)]
                    dstep.mark(dve.tensor_tensor(x, x, scaled[:, g, :], ALU.add))

            @block.tensor
            def _(pe):
                pe.wait_ge(s["ld_w"], 16)
                for g in range(4):
                    m = g % 2
                    if m == 0:
                        pe.wait_ge(xin_ready, 2 * l + 1 + g // 2)
                    for k in range(CH):
                        ins = pe.matmul(ps[:, g, :], w[:, k, m * P:(m + 1) * P], xin[:, k, half(g // 2)],
                                        start=(k == 0), stop=(k == CH - 1))
                    ins.then_inc(s["done"], 1)

    def stage_l3_attn(l):
        LOW = -1.0e38
        with ExitStack() as st:
            def sb(n, shape, dt=F32):
                return st.enter_context(nc.sbuf_tensor("V_" + n, shape, dt))

            sig = sb("sig", [P, CH, NT])
            w = sb("w", [P, 4, CH, C])
            mixed = sb("mixed", [P, 3, CH, NT])
            rest = sb("rest", [P, 8])
            k, v, r = sb("k", [P, CH, NT]), sb("v", [P, CH, NT]), sb("r", [P, CH, NT])
            top = sb("top", [P, CH, NB, T + 1])
            num = sb("num", [P, CH, NB, T + 1])
            den = sb("den", [P, CH, NB, T + 1])
            grow = sb("grow", [P, CH, NT])
            ps = st.enter_context(nc.psum_tensor("V_ps", [P, 8, HALF], F32))
            keep1, keep2 = sb("keep1", [P, CH, NT]), sb("keep2", [P, CH, NT])
            out1, out2 = sb("out1", [P, CH, NT]), sig
            names = "ld_w w_exp scaled mixed done evac diff_ready exp_ready prod_ready num_ready top_ready rwkv_ready".split()
            s = {n: sem("V_" + n) for n in names}
            block = st.enter_context(nc.Block())
            half = lambda h: slice(h * HALF, (h + 1) * HALF)
            wave = lambda x: x.rearrange("p (b t) -> p b t", b=NB)

            @block.sync
            def _(sp):
                sp.dma_start(w[:, :, :, :], io["l3_w"]).then_inc(s["ld_w"], 16)

            @block.gpsimd
            def _(pool):
                for ch in range(CH):
                    pool.wait_ge(s["exp_ready"], 2 * ch + 1)
                    pool.tensor_tensor(grow[:, ch, :], keep2[:, ch, :], v[:, ch, :], ALU.mult).then_inc(s["prod_ready"], 1)
                    pool.wait_ge(s["exp_ready"], 2 * ch + 2)
                    pool.tensor_tensor(k[:, ch, :], out2[:, ch, :], v[:, ch, :], ALU.mult).then_inc(s["prod_ready"], 1)
                pool.wait_ge(s["prod_ready"], 2 * CH)
                pool.wait_ge(s["evac"], 12)
                for ch in range(CH):
                    pool.wait_ge(s["num_ready"], ch + 1)
                    n = num[:, ch, :, 0:T]
                    pstep.link(pool.tensor_tensor(n, n, wave(out1[:, ch, :]), ALU.mult))
                    pstep.link(pool.tensor_tensor(n, n, wave(k[:, ch, :]), ALU.add))
                    pool.tensor_tensor(wave(r[:, ch, :]), wave(r[:, ch, :]), n, ALU.mult).then_inc(s["top_ready"], 1)

            @block.scalar
            def _(act):
                condition_act(act, sig)
                act.activation(rest[:, 6:8], vecs[:, VEC["decay"][0]:VEC["decay"][0] + 2], ACT.Exp).then_inc(s["w_exp"], 1)
                act.wait_ge(xin_ready, 2 * l + 2)
                for j, n in enumerate(("mk", "mv", "mr")):
                    for ch in range(CH):
                        act.activation(mixed[:, j, ch, :], xin[:, ch, :], ACT.Identity, scale=vec(n, ch)).then_inc(s["scaled"], 1)

                def evac(g):
                    dst, ch, h = (k, v, r)[g // 4], g // 2 % 2, g % 2
                    act.wait_ge(s["done"], g + 1)
                    act.activation(dst[:, ch, half(h)], ps[:, g % 8, :], ACT.Sigmoid if g >= 8 else ACT.Identity) \
                        .then_inc(s["evac"], 1)

                for g in range(8):
                    evac(g)
                for ch in range(CH):
                    for j, pair in enumerate(((keep1, keep2), (out1, out2))):
                        act.wait_ge(s["diff_ready"], 2 * ch + j + 1)
                        for x in pair:
                            ins = act.activation(x[:, ch, :], x[:, ch, :], ACT.Exp)
                        ins.then_inc(s["exp_ready"], 1)
                for g in range(8, 12):
                    evac(g)

            @block.vector
            def _(dve):
                condition_dve(dve, l, sig)
                dve.memset(top[:, :, :, 0:1], LOW)
                dve.memset(num[:, :, :, 0:1], 0.0)
                dve.memset(den[:, :, :, 0:1], 0.0)
                dstep.link(dve.tensor_scalar(rest[:, 0:6], vecs[:, VEC["mk"][0]:VEC["mk"][0] + 6], -1.0, 1.0, ALU.mult, ALU.add))
                for j in range(3):
                    for ch in range(CH):
                        dve.wait_ge(s["scaled"], 2 * j + ch + 1)
                        m = wave(mixed[:, j, ch, :])[:, :, 1:T]
                        ins = dve.scalar_tensor_tensor(out=m, in0=wave(xin[:, ch, :])[:, :, 0:T - 1],
                                                       scalar=rest[:, 2 * j + ch:2 * j + ch + 1], in1=m, op0=ALU.mult, op1=ALU.add)
                    ins.then_inc(s["mixed"], 1)
                dve.wait_ge(s["w_exp"], 1)
                dstep.link(dve.tensor_scalar(rest[:, 6:8], rest[:, 6:8], -1.0, None, ALU.mult))
                dve.wait_ge(s["evac"], 4)
                for ch in range(CH):
                    decayed, first, kc = rest[:, 6 + ch:7 + ch], vec("first", ch), wave(k[:, ch, :])
                    for b in range(NB):
                        ins = dve.tensor_tensor_scan(top[:, ch, b, 1:T + 1], decayed.to_broadcast([P, T]),
                                                     k[:, ch, b * T:(b + 1) * T], LOW, ALU.add, ALU.max)
                    dstep.link(ins)
                    before, after = top[:, ch, :, 0:T], top[:, ch, :, 1:T + 1]
                    dve.scalar_tensor_tensor(out=wave(keep1[:, ch, :]), in0=before, scalar=decayed, in1=after,
                                             op0=ALU.add, op1=ALU.subtract)
                    dve.tensor_tensor(wave(keep2[:, ch, :]), kc, after, ALU.subtract).then_inc(s["diff_ready"], 1)
                    dstep.link(dve.scalar_tensor_tensor(out=wave(out2[:, ch, :]), in0=kc, scalar=first, in1=before,
                                                        op0=ALU.add, op1=ALU.max))
                    dstep.link(dve.tensor_tensor(wave(out1[:, ch, :]), before, wave(out2[:, ch, :]), ALU.subtract))
                    dve.scalar_tensor_tensor(out=wave(out2[:, ch, :]), in0=kc, scalar=first, in1=wave(out2[:, ch, :]),
                                             op0=ALU.add, op1=ALU.subtract).then_inc(s["diff_ready"], 1)
                for ch in range(CH):
                    dve.wait_ge(s["exp_ready"], 2 * ch + 1)
                    dve.wait_ge(s["prod_ready"], 2 * ch + 1)
                    for b in range(NB):
                        c = slice(b * T, (b + 1) * T)
                        ins = dve.tensor_tensor_scan(num[:, ch, b, 1:T + 1], keep1[:, ch, c], grow[:, ch, c], 0.0,
                                                     ALU.mult, ALU.add)
                    ins.then_inc(s["num_ready"], 1)
                    for b in range(NB):
                        c = slice(b * T, (b + 1) * T)
                        ins = dve.tensor_tensor_scan(den[:, ch, b, 1:T + 1], keep1[:, ch, c], keep2[:, ch, c], 0.0,
                                                     ALU.mult, ALU.add)
                    dstep.link(ins)
                    dve.wait_ge(s["exp_ready"], 2 * ch + 2)
                    d, e1, e2 = den[:, ch, :, 0:T], wave(out1[:, ch, :]), wave(out2[:, ch, :])
                    dstep.link(dve.tensor_tensor(d, d, e1, ALU.mult))
                    dve.wait_ge(s["prod_ready"], 2 * ch + 2)
                    dstep.link(dve.tensor_tensor(e2, d, e2, ALU.add))
                    dstep.link(dve.reciprocal(e2, e2))
                    dve.wait_ge(s["top_ready"], ch + 1)
                    dve.tensor_tensor(r[:, ch, :], r[:, ch, :], out2[:, ch, :], ALU.mult).then_inc(s["rwkv_ready"], 1)
                for g in range(4):
                    dve.wait_ge(s["done"], 12 + g + 1)
                    x = xT[:, g // 2, half(g % 2)]
                    dstep.mark(dve.tensor_tensor(x, x, ps[:, (12 + g) % 8, :], ALU.add))

            @block.tensor
            def _(pe):
                pe.wait_ge(s["ld_w"], 16)
                for g in range(16):
                    j, m, h = g // 4, g // 2 % 2, g % 2
                    if j < 3:
                        pe.wait_ge(s["mixed"], j + 1)
                    elif g == 12:
                        pe.wait_ge(s["rwkv_ready"], 2)
                    if g >= 8:
                        pe.wait_ge(s["evac"], g - 7)
                    for c in range(CH):
                        src = mixed[:, j, c, half(h)] if j < 3 else r[:, c, half(h)]
                        ins = pe.matmul(ps[:, g % 8, :], w[:, j, c, m * P:(m + 1) * P], src, start=(c == 0), stop=(c == CH - 1))
                    ins.then_inc(s["done"], 1)

    def stage_last():
        with ExitStack() as st:
            stored = sem("stored")
            block = st.enter_context(nc.Block())

            @block.sync
            def _(sp):
                sp.dma_start(io["yT"], xT[:, :, :]).then_inc(stored, 16)
                sp.wait_ge(stored, 16)

    stage_l0_attn(0)
    stage_moe(1, "L0")
    stage_l1_attn(2)
    stage_l1_ffn(3)
    stage_l2_attn(4)
    scan_inputs.close()
    stage_l2_ffn(5)
    stage_l3_attn(6)
    stage_moe(7, "L3")
    stage_last()
    outer.close()


def chunks(a, axis, n):
    pad = [(0, 0)] * a.ndim
    pad[axis] = (0, n * P - a.shape[axis])
    a = np.pad(a, pad)
    return a.reshape(a.shape[:axis] + (n, P) + a.shape[axis + 1:])


def features(a):
    n = -(-a.shape[0] // P)
    return chunks(a, 0, n).transpose(1, 0, 2)


def columns(v, n):
    return chunks(v.reshape(-1), 0, n).T


def lay_out(i):
    f = np.float32
    out = {}
    tokens = lambda a: a.reshape(NT, C).T.reshape(CH, P, NT).transpose(1, 0, 2)
    out["xT"], out["fT"] = tokens(i["x"]), tokens(i["fside_BxSxS_0"])
    out["cond"] = np.broadcast_to(i["cond_512"], (P, NB, 64))
    out["ident"] = np.eye(P, dtype=f)
    conds = ["L0_cond", "L0_cond2", "L1_cond", "L1_cond2", "L2_cond", "L2_cond2", "L3_cond", "L3_cond2"]
    pieces = {
        "w": np.concatenate([columns(i[c + "_w"], CH) for c in conds], 1),
        "u": np.repeat(np.concatenate([columns(i[c + "_u"], CH) for c in conds], 1), NB, axis=1),
        "bq": i["L0_attn_bq"].reshape(4, 2, 4, HD).transpose(1, 3, 0, 2).reshape(P, 16),
        "kw": np.repeat(i["L0_attn_key_weights"].reshape(4, 2, 4).transpose(1, 0, 2), HD, axis=0).reshape(P, 16),
        "bk": columns(i["L0_attn_bk"], 4), "bv": columns(i["L0_attn_bv"], 4), "bo0": columns(i["L0_attn_bo"], 2),
        "b1": columns(np.concatenate([i["L1_attn_b1"], i["L1_attn_b1"][2 * P:]]), 3), "convb": columns(i["L1_attn_conv_b"], 3),
        "ba": columns(i["L1_attn_ba"], 3), "bx": columns(i["L1_attn_bx"], 3), "lam": columns(i["L1_attn_lam"], 3),
        "b2": columns(i["L1_attn_b2"], 2), "fc1b": columns(i["L1_ffn_fc1_b"], NE * FF // P),
        "bo2": columns(i["L2_attn_bo"], 2), "fscale": columns(i["L2_ffn_scale_weight"], 2),
        "fbias": columns(i["L2_ffn_bias"], 2), "decay": columns(i["L3_attn_time_decay"], 2),
        "first": columns(i["L3_attn_time_first"], 2), "mk": columns(i["L3_attn_time_mix_k"], 2),
        "mv": columns(i["L3_attn_time_mix_v"], 2), "mr": columns(i["L3_attn_time_mix_r"], 2),
    }
    out["vecs"] = np.concatenate([pieces[n] for n in VEC], 1)
    inv = (f(1.0) / f(10000.0) ** (np.arange(0, HD, 2, dtype=f) / f(HD))).astype(f)
    ang = np.arange(T, dtype=f)[None, :] * inv[:, None]
    cos, sin = np.cos(ang), np.sin(ang)
    out["rope"] = np.stack([np.concatenate([cos] * 4), np.concatenate([-sin, sin] * 2)], 1).astype(f)
    out["mask"] = np.where(np.arange(T)[None, :] - P > np.arange(P)[:, None], f(NEG), f(0))
    wq = i["L0_attn_Wq"].reshape(4, 2, 4, HD, CH, P).transpose(0, 5, 2, 4, 1, 3).reshape(4, P, 1024)
    wk = i["L0_attn_Wk"].reshape(4, P, CH, P).transpose(0, 3, 2, 1).reshape(4, P, 256)
    wv = i["L0_attn_Wv"].reshape(4, P, CH, P).transpose(0, 3, 2, 1).reshape(4, P, 256)
    wo = i["L0_attn_Wo"].reshape(C, 4, 2, 4, HD).transpose(1, 2, 4, 3, 0).reshape(4, P, 1024)
    out["w_l0a"] = np.concatenate([wk, wv, wq, wo], 2)
    for name, sh in (("L0", ("shw_gate", "shw_up", "shw_down")), ("L3", ("sw_gate", "sw_up", "sw_down"))):
        g = lambda n: i[f"{name}_ffn_{n}"]
        shared = g("shgate_w" if name == "L0" else "shared_gate_w").reshape(C, 1)
        out[name + "_gate"] = features(np.concatenate([g("gate_w").T, shared], 1))
        n = -(-g(sh[0]).shape[1] // P)
        up = []
        for a, b in (("w_gate", sh[0]), ("w_up", sh[1])):
            experts = g(a).reshape(NE, C, EH * NE // P, P // NE).transpose(1, 2, 0, 3).reshape(C, -1, P)
            m = np.concatenate([experts, chunks(g(b), 1, n)], 1)
            up.append(m.reshape(CH, P, -1, P).transpose(2, 1, 0, 3).reshape(-1, P, 2 * P))
        experts = g("w_down").reshape(NE, EH * NE // P, P // NE, C).transpose(1, 0, 2, 3).reshape(-1, P, C)
        down = np.concatenate([experts, chunks(g(sh[2]), 0, n)], 0)
        out[name + "_w"] = np.concatenate(up + [down], 2)
    out["rank"] = np.broadcast_to(np.arange(NE, 0, -1, dtype=f), (P, 8, NE))
    w1 = i["L1_attn_w1"].T
    out["l1_w1"] = features(np.concatenate([w1, w1[:, 2 * P:]], 1))
    cw = i["L1_attn_conv_w"].transpose(2, 1, 0)
    full = cw[:, :2 * P].reshape(TAPS * CH, P, R1)
    half = cw[:, 2 * P:].reshape(2, P, R1)
    out["l1_conv"] = np.concatenate([full, half], 0).transpose(1, 0, 2)
    out["l1_gate"] = np.stack([features(i["L1_attn_wa"].T), features(i["L1_attn_wx"].T)], 1)
    out["l1_w2"] = features(i["L1_attn_w2"].T)
    out["l1_wg"] = features(i["L1_ffn_wg"])
    n16, later = 2 * NT // P, np.arange(P)[:, None] > np.arange(P)[None, :]
    carry = np.broadcast_to(np.arange(n16) > 0, (NE, n16)).reshape(-1)
    slots = np.broadcast_to(np.arange(NE) * CAP, (n16, NE)).reshape(-1)
    out["seq"] = np.stack([np.where(later, f(-1), f(0)), np.ones((P, P), f), np.broadcast_to(carry, (P, P)),
                           np.broadcast_to(slots, (P, P))], 1).astype(f)
    tokens_of = np.arange(P)[:, None] + P * (np.arange(n16) % (NT // P))[None, :]
    out["ids"] = np.concatenate([np.broadcast_to(np.arange(CAP), (P, CAP)), tokens_of], 1).astype(f)
    out["l1_fc1"] = i["L1_ffn_fc1_w"].reshape(NE, CH, P, FF).transpose(0, 2, 1, 3).reshape(NE, P, CH * FF)
    out["l1_fc2"] = i["L1_ffn_fc2_w"].reshape(NE, FF // P, P, C).transpose(0, 2, 1, 3).reshape(NE, P, FF // P * C)
    out["l1_fc2b"] = i["L1_ffn_fc2_b"].reshape(1, NE * C)
    w = np.stack([i["L2_attn_" + n].reshape(CH, P, L2_PAIRS, P) for n in ("Wq", "Wk", "Wv")], 3)
    out["l2_wqkv"] = w.transpose(2, 1, 0, 3, 4).reshape(L2_PAIRS, P, CH * 3 * P)
    out["l2_wo"] = i["L2_attn_Wo"].reshape(L2_PAIRS, P, C)
    out["l2_w"] = features(i["L2_ffn_weight"].T)
    out["l3_w"] = np.stack([features(i["L3_attn_" + n].T) for n in ("Wk", "Wv", "Wr", "Wo")], 1)
    return {k: np.ascontiguousarray(v) for k, v in out.items()}


def kernel(**inputs):
    import concourse.bacc as bacc
    from concourse.bass_utils import run_bass_kernel_spmd

    arrays = lay_out({k: np.asarray(v) for k, v in inputs.items()})
    nc = bacc.Bacc("TRN2", target_bir_lowering=False, num_devices=1)
    io = {n: nc.dram_tensor(n + "_dram", a.shape, mybir.dt.from_np(a.dtype), kind="ExternalInput").ap()
          for n, a in arrays.items()}
    io["yT"] = nc.dram_tensor("yT_dram", (P, CH, NT), F32, kind="ExternalOutput").ap()
    build_program(nc, io)
    r = run_bass_kernel_spmd(nc, [{n + "_dram": a for n, a in arrays.items()}], core_ids=[0])
    y = r.results[0]["yT_dram"]
    return y.transpose(1, 0, 2).reshape(C, NT).T.reshape(NB, T, C)
```
